# Optimizing a Trainium2 kernel written in Bass

```python
import numpy as np
import jax
import jax.numpy as jnp

def _softmax(x, axis=-1):
    return jax.nn.softmax(x, axis=axis)

def _gelu(x):
    return jax.nn.gelu(x, approximate=True)

def _silu(x):
    return jax.nn.silu(x)

def _sigmoid(x):
    return jax.nn.sigmoid(x)

def _layernorm(x, axis=-1, eps=1e-05):
    m = jnp.mean(x, axis=axis, keepdims=True)
    v = jnp.var(x, axis=axis, keepdims=True)
    return (x - m) / jnp.sqrt(v + eps)

def _scatter_add(tgt, idx, src, axis=0):
    return tgt.at[idx].add(src)

def _segment_sum(src, seg, n):
    return jax.ops.segment_sum(src, seg, n)
kernel_name = 'mk_xattn_seq_d2_seqx_r2_835238'

def setup_inputs(seed: int=0):
    np.random.seed(seed)
    _w = jnp.asarray

    def _rec_inputs():
        import jax
        import jax.numpy as jnp
        _rk = jax.random.key(seed)
        x = -1.394e-06 + 0.9999 * jax.random.normal(jax.random.fold_in(_rk, 1), (2, 2048, 512), jnp.float32)
        _lenS = 2048 - jax.random.randint(jax.random.fold_in(_rk, 7), (2,), 0, max(1, 2048 // 4) + 1, jnp.int32)
        _lenS2 = 77 - jax.random.randint(jax.random.fold_in(_rk, 8), (2,), 0, max(1, 77 // 4) + 1, jnp.int32)
        _ctx_1024P = jax.random.normal(jax.random.fold_in(_rk, 11), (2, 16, 512), jnp.float32)
        _ctx_1024c = jax.random.dirichlet(jax.random.fold_in(_rk, 511), 0.3 * jnp.ones((16,), jnp.float32), (2, 77))
        _ctx_1024t = jnp.einsum('bsk,bkd->bsd', _ctx_1024c, _ctx_1024P)
        _ctx_1024t = _ctx_1024t * jax.lax.rsqrt(jnp.mean(jnp.square(_ctx_1024t)) + 1e-12) * 0.953939
        ctx_1024 = 0.000241658 + 0.999772 * (_ctx_1024t + 0.3 * jax.random.normal(jax.random.fold_in(_rk, 611), (2, 77, 512), jnp.float32))
        return (x, ctx_1024)
    x, ctx_1024 = _rec_inputs()

    def _L0_xattn_setup():
        import jax, jax.numpy as jnp
        import numpy as np
        D = 512
        H = 16
        DF = 4 * D
        LQ, LKV, B = (1024, 2048, 2)
        EPS = 1e-05

        def _ln(x, g, b):
            mu = jnp.mean(x, axis=-1, keepdims=True)
            var = jnp.mean(jnp.square(x - mu), axis=-1, keepdims=True)
            return (x - mu) * jax.lax.rsqrt(var + EPS) * g + b

        def _mha(q, k, v, wq, wk, wv, wo):
            q = q @ wq.T
            k = k @ wk.T
            v = v @ wv.T
            b, lq, _ = q.shape
            lv = v.shape[1]
            qh = q.reshape(b, lq, H, -1).transpose(0, 2, 1, 3)
            kh = k.reshape(b, lv, H, -1).transpose(0, 2, 1, 3)
            vh = v.reshape(b, lv, H, -1).transpose(0, 2, 1, 3)
            dh = qh.shape[-1]
            scores = jnp.einsum('bhqd,bhkd->bhqk', qh, kh) / jnp.sqrt(jnp.float32(dh))
            attn = jax.nn.softmax(scores, axis=-1)
            o = jnp.einsum('bhqk,bhkd->bhqd', attn, vh)
            o = o.transpose(0, 2, 1, 3).reshape(b, lq, -1)
            return o @ wo.T
        key = jax.random.key(seed)
        kid = [0]

        def nrm(shape, s=1.0):
            kid[0] += 1
            return jax.random.normal(jax.random.fold_in(key, kid[0]), shape, dtype=jnp.float32) * s
        inp = {'q': nrm((B, LQ, D)), 'k': nrm((B, LKV, D)), 'v': nrm((B, LKV, D)), 'sa_wq': nrm((D, D), 0.02), 'sa_wk': nrm((D, D), 0.02), 'sa_wv': nrm((D, D), 0.02), 'sa_wo': nrm((D, D), 0.02), 'ca_wq': nrm((D, D), 0.02), 'ca_wk': nrm((D, D), 0.02), 'ca_wv': nrm((D, D), 0.02), 'ca_wo': nrm((D, D), 0.02), 'g_sa': jnp.ones((D,), jnp.float32), 'b_sa': jnp.zeros((D,), jnp.float32), 'g_qca': jnp.ones((D,), jnp.float32), 'b_qca': jnp.zeros((D,), jnp.float32), 'g_kca': jnp.ones((D,), jnp.float32), 'b_kca': jnp.zeros((D,), jnp.float32), 'g_vca': jnp.ones((D,), jnp.float32), 'b_vca': jnp.zeros((D,), jnp.float32), 'g_out': jnp.ones((D,), jnp.float32), 'b_out': jnp.zeros((D,), jnp.float32), 'ffn_w1': nrm((DF, D), 0.02), 'ffn_b1': jnp.zeros((DF,), jnp.float32), 'ffn_w2': nrm((D, DF), 0.02), 'ffn_b2': jnp.zeros((D,), jnp.float32)}
        return inp
    _L0_xattn_all = _L0_xattn_setup()
    _L0_xattn_in = {k: v for k, v in _L0_xattn_all.items() if k in ('sa_wq', 'sa_wk', 'sa_wv', 'sa_wo', 'ca_wq', 'ca_wk', 'ca_wv', 'ca_wo', 'g_sa', 'b_sa', 'g_qca', 'b_qca', 'g_kca', 'b_kca', 'g_vca', 'b_vca', 'g_out', 'b_out', 'ffn_w1', 'ffn_b1', 'ffn_w2', 'ffn_b2')}
    del _L0_xattn_all

    def _L1_xattn_setup():
        import jax, jax.numpy as jnp
        import numpy as np
        D_MODEL = 512
        N_HEADS = 16
        D_K = D_MODEL // N_HEADS
        LN_EPS = 1e-05

        def _attention(query, key_value, W_qkv, b_qkv, W_o, b_o, ln_gamma, ln_beta):
            B, Sq, _ = query.shape
            Skv = key_value.shape[1]
            Wq, Wk, Wv = (W_qkv[:D_MODEL], W_qkv[D_MODEL:2 * D_MODEL], W_qkv[2 * D_MODEL:])
            bq, bk, bv = (b_qkv[:D_MODEL], b_qkv[D_MODEL:2 * D_MODEL], b_qkv[2 * D_MODEL:])
            Q = (query @ Wq.T + bq).reshape(B, Sq, N_HEADS, D_K).transpose(0, 2, 1, 3)
            K = (key_value @ Wk.T + bk).reshape(B, Skv, N_HEADS, D_K).transpose(0, 2, 1, 3)
            V = (key_value @ Wv.T + bv).reshape(B, Skv, N_HEADS, D_K).transpose(0, 2, 1, 3)
            scores = jnp.einsum('bhqd,bhkd->bhqk', Q.astype(jnp.float32), K.astype(jnp.float32))
            scores = scores / np.sqrt(D_K)
            attn = jax.nn.softmax(scores, axis=-1)
            context = jnp.einsum('bhqk,bhkd->bhqd', attn, V.astype(jnp.float32)).astype(query.dtype)
            context = context.transpose(0, 2, 1, 3).reshape(B, Sq, D_MODEL)
            output = context @ W_o.T + b_o
            x = output + query
            mu = jnp.mean(x, axis=-1, keepdims=True)
            var = jnp.mean(jnp.square(x - mu), axis=-1, keepdims=True)
            return (x - mu) / jnp.sqrt(var + LN_EPS) * ln_gamma + ln_beta
        key = jax.random.key(seed)
        ks = jax.random.split(key, 8)
        B, Sq, Skv = (2, 1024, 1024)
        scale = 1.0 / np.sqrt(D_MODEL)
        return {'query': jax.random.normal(ks[0], (B, Sq, D_MODEL), dtype=jnp.float32), 'key_value': jax.random.normal(ks[1], (B, Skv, D_MODEL), dtype=jnp.float32), 'W_qkv': jax.random.normal(ks[2], (3 * D_MODEL, D_MODEL), dtype=jnp.float32) * scale, 'b_qkv': jax.random.normal(ks[3], (3 * D_MODEL,), dtype=jnp.float32) * 0.01, 'W_o': jax.random.normal(ks[4], (D_MODEL, D_MODEL), dtype=jnp.float32) * scale, 'b_o': jax.random.normal(ks[5], (D_MODEL,), dtype=jnp.float32) * 0.01, 'ln_gamma': jnp.ones((D_MODEL,), dtype=jnp.float32), 'ln_beta': jnp.zeros((D_MODEL,), dtype=jnp.float32)}
    _L1_xattn_all = _L1_xattn_setup()
    _L1_xattn_in = {k: v for k, v in _L1_xattn_all.items() if k in ('W_qkv', 'b_qkv', 'W_o', 'b_o', 'ln_gamma', 'ln_beta')}
    del _L1_xattn_all
    return {'x': x, 'ctx_1024': ctx_1024, 'L0_xattn_sa_wq': _L0_xattn_in['sa_wq'], 'L0_xattn_sa_wk': _L0_xattn_in['sa_wk'], 'L0_xattn_sa_wv': _L0_xattn_in['sa_wv'], 'L0_xattn_sa_wo': _L0_xattn_in['sa_wo'], 'L0_xattn_ca_wq': _L0_xattn_in['ca_wq'], 'L0_xattn_ca_wk': _L0_xattn_in['ca_wk'], 'L0_xattn_ca_wv': _L0_xattn_in['ca_wv'], 'L0_xattn_ca_wo': _L0_xattn_in['ca_wo'], 'L0_xattn_g_sa': _L0_xattn_in['g_sa'], 'L0_xattn_b_sa': _L0_xattn_in['b_sa'], 'L0_xattn_g_qca': _L0_xattn_in['g_qca'], 'L0_xattn_b_qca': _L0_xattn_in['b_qca'], 'L0_xattn_g_kca': _L0_xattn_in['g_kca'], 'L0_xattn_b_kca': _L0_xattn_in['b_kca'], 'L0_xattn_g_vca': _L0_xattn_in['g_vca'], 'L0_xattn_b_vca': _L0_xattn_in['b_vca'], 'L0_xattn_g_out': _L0_xattn_in['g_out'], 'L0_xattn_b_out': _L0_xattn_in['b_out'], 'L0_xattn_ffn_w1': _L0_xattn_in['ffn_w1'], 'L0_xattn_ffn_b1': _L0_xattn_in['ffn_b1'], 'L0_xattn_ffn_w2': _L0_xattn_in['ffn_w2'], 'L0_xattn_ffn_b2': _L0_xattn_in['ffn_b2'], 'L1_xattn_W_qkv': _L1_xattn_in['W_qkv'], 'L1_xattn_b_qkv': _L1_xattn_in['b_qkv'], 'L1_xattn_W_o': _L1_xattn_in['W_o'], 'L1_xattn_b_o': _L1_xattn_in['b_o'], 'L1_xattn_ln_gamma': _L1_xattn_in['ln_gamma'], 'L1_xattn_ln_beta': _L1_xattn_in['ln_beta']}

def reference(x, ctx_1024, L0_xattn_sa_wq, L0_xattn_sa_wk, L0_xattn_sa_wv, L0_xattn_sa_wo, L0_xattn_ca_wq, L0_xattn_ca_wk, L0_xattn_ca_wv, L0_xattn_ca_wo, L0_xattn_g_sa, L0_xattn_b_sa, L0_xattn_g_qca, L0_xattn_b_qca, L0_xattn_g_kca, L0_xattn_b_kca, L0_xattn_g_vca, L0_xattn_b_vca, L0_xattn_g_out, L0_xattn_b_out, L0_xattn_ffn_w1, L0_xattn_ffn_b1, L0_xattn_ffn_w2, L0_xattn_ffn_b2, L1_xattn_W_qkv, L1_xattn_b_qkv, L1_xattn_W_o, L1_xattn_b_o, L1_xattn_ln_gamma, L1_xattn_ln_beta):
    import jax
    import jax.numpy as jnp

    def _L0_xattn_ref(q, k, v, sa_wq, sa_wk, sa_wv, sa_wo, ca_wq, ca_wk, ca_wv, ca_wo, g_sa, b_sa, g_qca, b_qca, g_kca, b_kca, g_vca, b_vca, g_out, b_out, ffn_w1, ffn_b1, ffn_w2, ffn_b2):
        import jax, jax.numpy as jnp
        import numpy as np
        D = 512
        H = 16
        DF = 4 * D
        LQ, LKV, B = (1024, 2048, 2)
        EPS = 1e-05

        def _ln(x, g, b):
            mu = jnp.mean(x, axis=-1, keepdims=True)
            var = jnp.mean(jnp.square(x - mu), axis=-1, keepdims=True)
            return (x - mu) * jax.lax.rsqrt(var + EPS) * g + b

        def _mha(q, k, v, wq, wk, wv, wo):
            q = q @ wq.T
            k = k @ wk.T
            v = v @ wv.T
            b, lq, _ = q.shape
            lv = v.shape[1]
            qh = q.reshape(b, lq, H, -1).transpose(0, 2, 1, 3)
            kh = k.reshape(b, lv, H, -1).transpose(0, 2, 1, 3)
            vh = v.reshape(b, lv, H, -1).transpose(0, 2, 1, 3)
            dh = qh.shape[-1]
            scores = jnp.einsum('bhqd,bhkd->bhqk', qh, kh) / jnp.sqrt(jnp.float32(dh))
            attn = jax.nn.softmax(scores, axis=-1)
            o = jnp.einsum('bhqk,bhkd->bhqd', attn, vh)
            o = o.transpose(0, 2, 1, 3).reshape(b, lq, -1)
            return o @ wo.T
        q = _ln(q, g_sa, b_sa)
        q = q + _mha(q, q, q, sa_wq, sa_wk, sa_wv, sa_wo)
        q = _ln(q, g_qca, b_qca)
        k = _ln(k, g_kca, b_kca)
        v = _ln(v, g_vca, b_vca)
        q = q[..., :D] + _mha(q, k, v, ca_wq, ca_wk, ca_wv, ca_wo)
        h = _ln(q, g_out, b_out)
        h = jax.nn.relu(h @ ffn_w1.T + ffn_b1) @ ffn_w2.T + ffn_b2
        return q + h

    def _L1_xattn_ref(query, key_value, W_qkv, b_qkv, W_o, b_o, ln_gamma, ln_beta):
        import jax, jax.numpy as jnp
        import numpy as np
        D_MODEL = 512
        N_HEADS = 16
        D_K = D_MODEL // N_HEADS
        LN_EPS = 1e-05

        def _attention(query, key_value, W_qkv, b_qkv, W_o, b_o, ln_gamma, ln_beta):
            B, Sq, _ = query.shape
            Skv = key_value.shape[1]
            Wq, Wk, Wv = (W_qkv[:D_MODEL], W_qkv[D_MODEL:2 * D_MODEL], W_qkv[2 * D_MODEL:])
            bq, bk, bv = (b_qkv[:D_MODEL], b_qkv[D_MODEL:2 * D_MODEL], b_qkv[2 * D_MODEL:])
            Q = (query @ Wq.T + bq).reshape(B, Sq, N_HEADS, D_K).transpose(0, 2, 1, 3)
            K = (key_value @ Wk.T + bk).reshape(B, Skv, N_HEADS, D_K).transpose(0, 2, 1, 3)
            V = (key_value @ Wv.T + bv).reshape(B, Skv, N_HEADS, D_K).transpose(0, 2, 1, 3)
            scores = jnp.einsum('bhqd,bhkd->bhqk', Q.astype(jnp.float32), K.astype(jnp.float32))
            scores = scores / np.sqrt(D_K)
            attn = jax.nn.softmax(scores, axis=-1)
            context = jnp.einsum('bhqk,bhkd->bhqd', attn, V.astype(jnp.float32)).astype(query.dtype)
            context = context.transpose(0, 2, 1, 3).reshape(B, Sq, D_MODEL)
            output = context @ W_o.T + b_o
            x = output + query
            mu = jnp.mean(x, axis=-1, keepdims=True)
            var = jnp.mean(jnp.square(x - mu), axis=-1, keepdims=True)
            return (x - mu) / jnp.sqrt(var + LN_EPS) * ln_gamma + ln_beta
        return _attention(query, key_value, W_qkv, b_qkv, W_o, b_o, ln_gamma, ln_beta)
    x = _L0_xattn_ref(x, ctx_1024, ctx_1024, L0_xattn_sa_wq, L0_xattn_sa_wk, L0_xattn_sa_wv, L0_xattn_sa_wo, L0_xattn_ca_wq, L0_xattn_ca_wk, L0_xattn_ca_wv, L0_xattn_ca_wo, L0_xattn_g_sa, L0_xattn_b_sa, L0_xattn_g_qca, L0_xattn_b_qca, L0_xattn_g_kca, L0_xattn_b_kca, L0_xattn_g_vca, L0_xattn_b_vca, L0_xattn_g_out, L0_xattn_b_out, L0_xattn_ffn_w1, L0_xattn_ffn_b1, L0_xattn_ffn_w2, L0_xattn_ffn_b2)
    x = _L1_xattn_ref(x, ctx_1024, L1_xattn_W_qkv, L1_xattn_b_qkv, L1_xattn_W_o, L1_xattn_b_o, L1_xattn_ln_gamma, L1_xattn_ln_beta)
    return x

_drawn_inputs = setup_inputs


def setup_inputs(seed=0):
    import zlib

    import numpy as np

    out = dict(_drawn_inputs(seed))
    spreads = {'L0_xattn_g_sa': (1.0, 0.2),
     'L0_xattn_b_sa': (0.0, 0.1),
     'L0_xattn_g_qca': (1.0, 0.2),
     'L0_xattn_b_qca': (0.0, 0.1),
     'L0_xattn_g_kca': (1.0, 0.6),
     'L0_xattn_b_kca': (0.0, 0.8),
     'L0_xattn_g_vca': (1.0, 0.6),
     'L0_xattn_b_vca': (0.0, 0.487),
     'L0_xattn_g_out': (1.0, 0.2),
     'L0_xattn_b_out': (0.0, 0.34),
     'L0_xattn_ffn_b1': (0.0, 0.1),
     'L0_xattn_ffn_b2': (0.0, 0.1),
     'L1_xattn_ln_gamma': (1.0, 0.2),
     'L1_xattn_ln_beta': (0.0, 0.1)}
    factors = {'L0_xattn_sa_wq': 8.0,
     'L0_xattn_sa_wk': 8.0,
     'L0_xattn_sa_wv': 3.554,
     'L0_xattn_sa_wo': 3.233,
     'L0_xattn_ca_wq': 7.374,
     'L0_xattn_ca_wk': 7.362,
     'L1_xattn_b_qkv': 7.078,
     'L1_xattn_b_o': 6.817}
    for name, (base, spread) in spreads.items():
        noise = np.random.default_rng([zlib.crc32(name.encode()), seed]).standard_normal(out[name].shape)
        drawn = base * np.exp(spread * noise) if base else spread * noise
        out[name] = jnp.asarray(drawn.astype(out[name].dtype))
    for name, factor in factors.items():
        out[name] = (out[name] * factor).astype(out[name].dtype)
    return out
```

```python
from contextlib import ExitStack

import concourse.bass as bass
from concourse import mybir

F32 = mybir.dt.float32
F32R = mybir.dt.float32r
ALU = mybir.AluOpType
ACT = mybir.ActivationFunctionType
AX = mybir.AxisListType

P = 128
BATCH, SEQ, D = 2, 2048, 512
CTX = 77
HEADS, DH = 16, 32
DFF = 4 * D
KC = D // P
GROUP = P // DH
CHUNK = 512
TILES = CHUNK // P
CHUNKS = SEQ // CHUNK
KT = SEQ // P
BANKS = 8
EPS = 1e-5
SCALE = float(DH) ** -0.5
STREAMS = range(BATCH)


class Tally:

    def __init__(self, sem, per, credit=False, ahead=0):
        self.sem, self.per, self.start = sem, per, per if credit else ahead
        self.given = per - ahead if credit else 0

    def at(self, it, k):
        return it * self.per + (k + self.start)


class Chain:

    def __init__(self, eng, tally, it):
        self.eng, self.tally, self.it, self.n = eng, tally, it, 0

    def link(self, ins):
        self.n += 1
        return ins.then_inc(self.tally.sem, 1)

    def settle(self, alone=None):
        value = self.tally.at(self.it, self.n)
        if alone:
            alone.wait(self.eng, self.tally.sem, value)
        else:
            self.eng.wait_ge(self.tally.sem, value)

    def end(self):
        assert self.n == self.tally.per, (self.n, self.tally.per)


class Alone:

    def __init__(self, sem):
        self.sem = sem

    def wait(self, eng, sem, value):
        eng.wait_ge(sem, value)
        eng.sem_inc(self.sem, 1)


class Ring:

    def __init__(self, banks, readers, tallies):
        self.banks, self.readers, self.tallies = banks, readers, tallies
        assert len(readers) % banks == 0
        for r, t in tallies.items():
            assert t.per == readers.count(r), (r, t.per, readers.count(r))

    def bank(self, e):
        return e % self.banks

    def free(self, it, e):
        back = e - self.banks
        r = self.readers[back]
        n = self.readers[:back % len(self.readers)].count(r) + 1 - (self.tallies[r].per if back < 0 else 0)
        return self.tallies[r].sem, self.tallies[r].at(it, n)


def split_product(pe, out, pairs):
    n = len(pairs)
    for i, ((ah, al), (bh, bl)) in enumerate(pairs):
        pe.matmul(out, ah, bh, start=(i == 0), stop=False)
        pe.matmul(out, ah, bl, start=False, stop=False)
        last = pe.matmul(out, al, bh, start=False, stop=(i == n - 1))
    return last


def transposes(pe, bank, src, kc, ident):
    for t in range(TILES):
        last = pe.transpose(bank[:, t * P:(t + 1) * P], src[:, t, kc * P:(kc + 1) * P], ident)
    return last


LN_STEPS = 3 * TILES


def make_constants(nc, ctx):
    ident = ctx.enter_context(nc.sbuf_tensor("ident", [P, P], F32))
    ones = ctx.enter_context(nc.sbuf_tensor("ones", [P, DH], F32))
    minus_half = ctx.enter_context(nc.sbuf_tensor("minus_half", [P, TILES], F32))
    made = ctx.enter_context(nc.semaphore("constants_made"))
    with nc.Block() as block:
        @block.gpsimd
        def _(pool):
            pool.memset(ones[:], 1.0).then_inc(made, 1)
            pool.memset(minus_half[:], -0.5).then_inc(made, 1)
            pool.memset(ident[:], 0.0).then_inc(made, 1)
            pool.wait_ge(made, 3)
            pool.affine_select(out=ident[:], in_=ident[:], compare_op=ALU.not_equal, fill=1.0, base=0,
                               pattern=[[-1, P]], channel_multiplier=1).then_inc(made, 1)
            pool.wait_ge(made, 4)
    return ident, ones, minus_half


def split_weights(nc, name, jobs, raw):
    with ExitStack() as ctx:
        loaded = [ctx.enter_context(nc.semaphore(f"{name}_w_loaded{i}")) for i in range(2)]
        hi_made = ctx.enter_context(nc.semaphore(f"{name}_w_hi"))
        lo_made = ctx.enter_context(nc.semaphore(f"{name}_w_lo"))
        block = ctx.enter_context(nc.Block())

        @block.sync
        def _(sp):
            for n, (src, hi, lo) in enumerate(jobs):
                if n >= 2:
                    sp.wait_ge(lo_made, n - 1)
                sp.dma_start(raw[n % 2][:], src).then_inc(loaded[n % 2], 16)

        @block.scalar
        def _(act):
            for n, (src, hi, lo) in enumerate(jobs):
                act.wait_ge(loaded[n % 2], 16 * (n // 2 + 1))
                act.activation(hi, raw[n % 2][:], ACT.Copy).then_inc(hi_made, 1)

        @block.vector
        def _(dve):
            for n, (src, hi, lo) in enumerate(jobs):
                dve.wait_ge(hi_made, n + 1)
                dve.tensor_tensor(lo, raw[n % 2][:], hi.bitcast(F32), ALU.subtract).then_inc(lo_made, 1)
            dve.wait_ge(lo_made, len(jobs))


def rows_of(a, t=TILES):
    return a.rearrange("(t p) n -> p t n", p=P)


def load_broadcast(eng, dst, src, sem):
    return eng.dma_start(dst, src.rearrange("(a n) -> a n", a=1).to_broadcast(list(dst.shape))).then_inc(sem, 16)


def project_qkv(nc, const, x, wq, wk, wv, gain_d, bias_d, scratch):
    ident, ones, minus_half = const
    xn_d, q_hi_d, q_lo_d, k_hi_d, k_lo_d, v_d = scratch
    with ExitStack() as ctx:
        def sb(name, shape, dt=F32):
            return ctx.enter_context(nc.sbuf_tensor("a_" + name, shape, dt))

        def tally(name, per, credit=False):
            return Tally(ctx.enter_context(nc.semaphore("a_" + name)), per, credit)

        w = {n: (sb(f"w{n}_hi", [P, KC, D], F32R), sb(f"w{n}_lo", [P, KC, D], F32R)) for n in "qkv"}
        gain, bias = sb("gain", [P, D]), sb("bias", [P, D])
        xin = [sb(f"xin{s}", [P, TILES, D]) for s in STREAMS]
        xn = [sb(f"xn{s}", [P, TILES, D]) for s in STREAMS]
        xT = [[sb(f"xT{p}{s}", [P, KC, CHUNK], F32R) for p in ("hi", "lo")] for s in STREAMS]
        stage = [{n: [sb(f"{n}T{p}{s}", [P, KC, CHUNK], F32R) for p in ("hi", "lo")] for n in "qk"} for s in STREAMS]
        vst = [sb(f"v{s}", [P, TILES, D]) for s in STREAMS]
        stats, mv = sb("stats", [P, TILES, 6]), sb("mv", [P, TILES, 2])
        veps, rstd = sb("veps", [P, TILES]), sb("rstd", [P, TILES])
        psum = ctx.enter_context(nc.psum_tensor("a_psum", [P, BANKS, 512], F32))

        raw = [xin[0][:].rearrange("p t n -> p (t n)"), xin[1][:].rearrange("p t n -> p (t n)")]
        jobs = []
        for n, src in (("q", wq), ("k", wk), ("v", wv)):
            jobs.append((src.rearrange("(c p) n -> p c n", p=P),
                         w[n][0][:], w[n][1][:]))
        split_weights(nc, "a", jobs, xin)

        PER_STREAM = 4 * 4
        params = ctx.enter_context(nc.semaphore("a_params"))
        loaded = [tally(f"x_loaded{s}", 16) for s in STREAMS]
        normed = [tally(f"normed{s}", 1, True) for s in STREAMS]
        filled = tally("bank_filled", 2 * PER_STREAM)
        hi_made = tally("hi_made", 2 * 12)
        emptied = tally("bank_emptied", 2 * PER_STREAM, True)
        steps = tally("vector_steps", 2 * LN_STEPS)
        veps_made = tally("veps_made", 2)
        rstd_made = tally("rstd_made", 2)
        stored = [{n: tally(f"{n}_stored{s}", 16 * (2 if n in "qk" else 1), True) for n in ("xn", "q", "k", "v")}
                  for s in STREAMS]
        ring = Ring(BANKS, "D" * (2 * PER_STREAM), {"D": emptied})
        sp_alone = Alone(ctx.enter_context(nc.semaphore("a_sync_waits")))
        dve_alone = Alone(ctx.enter_context(nc.semaphore("a_vector_waits")))
        block = ctx.enter_context(nc.Block())

        def event(s, j):
            return s * PER_STREAM + j

        @block.scalar
        def _(act):
            load_broadcast(act, gain[:], gain_d, params)
            load_broadcast(act, bias[:], bias_d, params)
            for s in STREAMS:
                act.sem_inc(normed[s].sem, normed[s].per)
            with act.Fori(0, CHUNKS) as it:
                for s in STREAMS:
                    act.wait_ge(normed[s].sem, normed[s].at(it, 0))
                    act.dma_start(xin[s][:], rows_of(x[bass.ds(it * CHUNK + s * SEQ, CHUNK), :])).then_inc(loaded[s].sem, 16)
                for s in STREAMS:
                    for j in range(12):
                        e = event(s, j)
                        part, c = divmod(j, 4)
                        hi = (xT[s][0], stage[s]["q"][0], stage[s]["k"][0])[part]
                        if part and c == 0:
                            st = stored[s]["qk"[part - 1]]
                            act.wait_ge(st.sem, st.at(it, 0))
                        act.wait_ge(filled.sem, filled.at(it, e + 1))
                        act.activation(hi[:, c, :], psum[:, ring.bank(e), :], ACT.Copy).then_inc(hi_made.sem, 1)

        @block.gpsimd
        def _(pool):
            with pool.Fori(0, CHUNKS) as it:
                for s in STREAMS:
                    pool.wait_ge(veps_made.sem, veps_made.at(it, s + 1))
                    pool.tensor_tensor(rstd[:], veps[:], minus_half[:], ALU.pow).then_inc(rstd_made.sem, 1)

        @block.vector
        def _(dve):
            dve.sem_inc(emptied.sem, emptied.per)
            dve.wait_ge(params, 32)
            with dve.Fori(0, CHUNKS) as it:
                chain = Chain(dve, steps, it)
                for s in STREAMS:
                    dve.wait_ge(loaded[s].sem, loaded[s].at(it, 16))
                    dve.wait_ge(stored[s]["xn"].sem, stored[s]["xn"].at(it, 0))
                    x_, y_ = xin[s], xn[s]
                    for t in range(TILES):
                        chain.link(dve.bn_stats(stats[:, t, :], x_[:, t, :]))
                    chain.settle(dve_alone)
                    for t in range(TILES):
                        chain.link(dve.bn_aggr(mv[:, t, :], stats[:, t, :]))
                    chain.settle()
                    dve.tensor_scalar(veps[:], mv[:, :, 1], EPS, None, ALU.add).then_inc(veps_made.sem, 1)
                    for t in range(TILES):
                        chain.link(dve.scalar_tensor_tensor(y_[:, t, :], x_[:, t, :], mv[:, t, 0:1], gain[:],
                                                            ALU.subtract, ALU.mult))
                    chain.settle()
                    dve.wait_ge(rstd_made.sem, rstd_made.at(it, s + 1))
                    for t in range(TILES):
                        last = dve.scalar_tensor_tensor(y_[:, t, :], y_[:, t, :], rstd[:, t:t + 1], bias[:],
                                                        ALU.mult, ALU.add)
                    last.then_inc(normed[s].sem, 1)
                    for j in range(PER_STREAM):
                        e = event(s, j)
                        part, c = divmod(j, 4)
                        if part < 3:
                            hi, lo = (xT[s], stage[s]["q"], stage[s]["k"])[part]
                            if part and c == 0:
                                st = stored[s]["qk"[part - 1]]
                                dve.wait_ge(st.sem, st.at(it, 0))
                            dve.wait_ge(hi_made.sem, hi_made.at(it, s * 12 + j + 1))
                            dve.tensor_tensor(lo[:, c, :], psum[:, ring.bank(e), :], hi[:, c, :].bitcast(F32),
                                              ALU.subtract).then_inc(emptied.sem, 1)
                        else:
                            if c == 0:
                                dve.wait_ge(stored[s]["v"].sem, stored[s]["v"].at(it, 0))
                            dve.wait_ge(filled.sem, filled.at(it, e + 1))
                            dve.tensor_copy(vst[s][:, c, :], psum[:, ring.bank(e), :]).then_inc(emptied.sem, 1)

        @block.tensor
        def _(pe):
            with pe.Fori(0, CHUNKS) as it:
                for s in STREAMS:
                    pe.wait_ge(normed[s].sem, normed[s].at(it, 1))
                    for j in range(PER_STREAM):
                        e = event(s, j)
                        part, c = divmod(j, 4)
                        bank = psum[:, ring.bank(e), :]
                        pe.wait_ge(*ring.free(it, e))
                        if part == 0:
                            last = transposes(pe, bank, xn[s], c, ident[:])
                        elif part < 3:
                            if part == 1 and c == 0:
                                pe.wait_ge(emptied.sem, emptied.at(it, event(s, 4)))
                            wh, wl = w["qk"[part - 1]]
                            last = split_product(pe, bank, [
                                ((wh[:, k, c * P:(c + 1) * P], wl[:, k, c * P:(c + 1) * P]),
                                 (xT[s][0][:, k, :], xT[s][1][:, k, :])) for k in range(KC)])
                        else:
                            wh, wl = w["v"]
                            last = split_product(pe, bank, [
                                ((xT[s][0][:, k, c * P:(c + 1) * P], xT[s][1][:, k, c * P:(c + 1) * P]),
                                 (wh[:, k, :], wl[:, k, :])) for k in range(KC)])
                        last.then_inc(filled.sem, 1)

        @block.sync
        def _(sp):
            for s in STREAMS:
                for n in ("xn", "q", "k", "v"):
                    sp.sem_inc(stored[s][n].sem, stored[s][n].per)
            with sp.Fori(0, CHUNKS) as it:
                for s in STREAMS:
                    tokens = bass.ds(it * CHUNK + s * SEQ, CHUNK)
                    sp_alone.wait(sp, normed[s].sem, normed[s].at(it, 1))
                    sp.dma_start(rows_of(xn_d[tokens, :]), xn[s][:]).then_inc(stored[s]["xn"].sem, 16)
                    for part, (n, hi_d, lo_d) in enumerate((("q", q_hi_d, q_lo_d), ("k", k_hi_d, k_lo_d))):
                        sp_alone.wait(sp, emptied.sem, emptied.at(it, event(s, 4 * part + 8)))
                        for d, buf in zip((hi_d, lo_d), stage[s][n]):
                            sp.dma_start(d[:, tokens].rearrange("(c p) n -> p c n", p=P),
                                         buf[:].bitcast(F32)).then_inc(stored[s][n].sem, 16)
                    sp_alone.wait(sp, emptied.sem, emptied.at(it, event(s, 16)))
                    sp.dma_start(rows_of(v_d[tokens, :]), vst[s][:]).then_inc(stored[s]["v"].sem, 16)
            for s in STREAMS:
                for n in ("xn", "q", "k", "v"):
                    sp_alone.wait(sp, stored[s][n].sem, stored[s][n].at(CHUNKS, 0))


def self_attention(nc, const, scratch, oT_d):
    ident, ones, minus_half = const
    xn_d, q_hi_d, q_lo_d, k_hi_d, k_lo_d, v_d = scratch
    STACK = 3 * DH
    ROWS = STACK + 2
    STEPS = BATCH * CHUNKS
    GROUPS = HEADS // GROUP
    QBUF, PBUF = 4, 4
    UNITS = TILES * GROUP * CHUNKS
    ALL_UNITS = UNITS + 1
    UNIT_BANKS, SCORE_BANKS, O_BANK, L_BANK = 0, 2, 6, 7
    with ExitStack() as ctx:
        def sb(name, shape, dt=F32):
            return ctx.enter_context(nc.sbuf_tensor("b_" + name, shape, dt))

        def tally(name, per, credit=False):
            return Tally(ctx.enter_context(nc.semaphore("b_" + name)), per, credit)

        kst = [sb(f"k_stack{b}", [ROWS, GROUP, SEQ], F32R) for b in STREAMS]
        qst = [sb(f"q_stack{i}", [ROWS, GROUP, CHUNK], F32R) for i in range(QBUF)]
        vt = [sb(f"v{b}", [P, KT, P]) for b in STREAMS]
        probs = [sb(f"probs{i}", [P, GROUP, CHUNK]) for i in range(PBUF)]
        part_max = [sb(f"part_max{i}", [P, TILES * GROUP, CHUNKS]) for i in range(2)]
        neg_max = [sb(f"neg_max{i}", [P, TILES * GROUP]) for i in range(2)]
        row_hi = [sb(f"row_hi{i}", [GROUP, CHUNK], F32R) for i in range(2)]
        row_lo = [sb(f"row_lo{i}", [GROUP, CHUNK], F32R) for i in range(2)]
        o_sb = [sb(f"o{i}", [P, CHUNK]) for i in range(2)]
        inv = [sb(f"inv{i}", [P, CHUNK]) for i in range(2)]
        psum = ctx.enter_context(nc.psum_tensor("b_psum", [P, BANKS, 512], F32))

        k_loaded = [tally(f"k_loaded{b}", 64) for b in STREAMS]
        q_loaded = [tally(f"q_loaded{i}", 48 * STEPS // QBUF) for i in range(QBUF)]
        rows_loaded = [tally(f"rows_loaded{i}", 32 * STEPS // QBUF) for i in range(QBUF)]
        unit_filled = tally("unit_filled", STEPS * ALL_UNITS)
        unit_emptied = tally("unit_emptied", STEPS * ALL_UNITS, True)
        max_made = tally("max_made", STEPS)
        rows_made = tally("rows_made", STEPS)
        row_steps = tally("row_steps", STEPS)
        scored = tally("scored", STEPS * KT * 2)
        exped = tally("exped", STEPS * KT * 2, True)
        pv_done = tally("pv_done", STEPS * KT, True)
        o_copied = tally("o_copied", STEPS, True)
        inv_made = tally("inv_made", STEPS, True)
        o_made = tally("o_made", STEPS)
        o_stored = [tally(f"o_stored{i}", 16 * STEPS // 2, True) for i in range(2)]
        ones_made = ctx.enter_context(nc.semaphore("b_ones_made"))
        sp_alone = Alone(ctx.enter_context(nc.semaphore("b_sync_waits")))
        dve_alone = Alone(ctx.enter_context(nc.semaphore("b_vector_waits")))
        block = ctx.enter_context(nc.Block())

        def tokens(q):
            return (q // CHUNKS) * SEQ + (q % CHUNKS) * CHUNK

        @block.gpsimd
        def _(pool):
            for b in STREAMS:
                pool.memset(kst[b][STACK:ROWS].bitcast(F32), 1.0).then_inc(ones_made, 1)

        @block.sync
        def _(sp):
            sp.sem_inc(pv_done.sem, pv_done.per)
            for i in range(2):
                sp.sem_inc(o_stored[i].sem, o_stored[i].per)

            def load_k(it, b):
                rows, cols = bass.ds(it * P, P), slice(b * SEQ, (b + 1) * SEQ)
                for n, d in enumerate((k_hi_d, k_lo_d, k_hi_d)):
                    sp.dma_start(kst[b][n * DH:(n + 1) * DH].bitcast(F32),
                                 d[rows, cols].rearrange("(h p) n -> p h n", p=DH)).then_inc(k_loaded[b].sem, 16)
                sp.dma_start(vt[b][:], v_d[cols, rows].rearrange("(t p) n -> p t n", p=P)).then_inc(k_loaded[b].sem, 16)

            def load_q(it, q):
                rows, cols = bass.ds(it * P, P), slice(tokens(q), tokens(q) + CHUNK)
                for n, d in enumerate((q_hi_d, q_hi_d, q_lo_d)):
                    sp.dma_start(qst[q % QBUF][n * DH:(n + 1) * DH].bitcast(F32),
                                 d[rows, cols].rearrange("(h p) n -> p h n", p=DH)).then_inc(q_loaded[q % QBUF].sem, 16)

            def send_rows(it, q):
                sp_alone.wait(sp, rows_made.sem, rows_made.at(it, q + 1))
                for n, row in enumerate((row_hi[q % 2], row_lo[q % 2])):
                    sp.dma_start(qst[q % QBUF][STACK + n:STACK + n + 1].bitcast(F32),
                                 row[:].bitcast(F32)).then_inc(rows_loaded[q % QBUF].sem, 16)

            def store_o(it, q):
                sp_alone.wait(sp, o_made.sem, o_made.at(it, q + 1))
                sp.dma_start(oT_d[bass.ds(it * P, P), tokens(q):tokens(q) + CHUNK], o_sb[q % 2][:]).then_inc(
                    o_stored[q % 2].sem, 16)

            def body(it, last):
                for q in range(STEPS):
                    if q == 0:
                        sp_alone.wait(sp, pv_done.sem, pv_done.at(it, 0))
                        load_k(it, 1)
                    if q == CHUNKS and not last:
                        sp_alone.wait(sp, pv_done.sem, pv_done.at(it, CHUNKS * KT))
                        load_k(it + 1, 0)
                    if q + 2 < STEPS or not last:
                        sp_alone.wait(sp, pv_done.sem, pv_done.at(it, (q - 1) * KT))
                        load_q(*((it, q + 2) if q + 2 < STEPS else (it + 1, q + 2 - STEPS)))
                    if q >= 1:
                        store_o(it, q - 1)
                    if q + 1 < STEPS:
                        send_rows(it, q + 1)
                    elif not last:
                        send_rows(it + 1, 0)
                store_o(it, STEPS - 1)

            load_k(0, 0)
            load_q(0, 0)
            load_q(0, 1)
            send_rows(0, 0)
            with sp.Fori(0, GROUPS - 1) as it:
                body(it, False)
            body(GROUPS - 1, True)
            for i in range(2):
                sp_alone.wait(sp, o_stored[i].sem, o_stored[i].at(GROUPS, 0))

        @block.tensor
        def _(pe):
            pe.wait_ge(ones_made, len(STREAMS))

            def unit(it, q, u):
                b, n = q // CHUNKS, q * ALL_UNITS + u
                bank = UNIT_BANKS + n % 2
                if u == 0:
                    pe.wait_ge(q_loaded[q % QBUF].sem, q_loaded[q % QBUF].at(it, 48 * (q // QBUF + 1)))
                    pe.wait_ge(k_loaded[b].sem, k_loaded[b].at(it, 64))
                pe.wait_ge(unit_emptied.sem, unit_emptied.at(it, n - 1))
                if u < UNITS:
                    (t, h), c = divmod(u // CHUNKS, GROUP), u % CHUNKS
                    last = pe.matmul(psum[:, bank, :], qst[q % QBUF][0:STACK, h, t * P:(t + 1) * P],
                                     kst[b][0:STACK, h, c * 512:(c + 1) * 512], start=True, stop=True)
                else:
                    pe.wait_ge(max_made.sem, max_made.at(it, q + 1))
                    for t in range(TILES):
                        last = pe.transpose(psum[0:GROUP, bank, t * P:(t + 1) * P],
                                            neg_max[q % 2][:, t * GROUP:(t + 1) * GROUP], ident[:])
                last.then_inc(unit_filled.sem, 1)

            def body(it, last_group):
                pending = None
                for q in range(STEPS):
                    b = q // CHUNKS
                    ahead = (it, q + 1) if q + 1 < STEPS else (it + 1, 0)
                    some = q + 1 < STEPS or not last_group
                    todo = iter(range(UNITS) if some else ())

                    def units(n):
                        for _ in range(n):
                            u = next(todo, None)
                            if u is not None:
                                unit(*ahead, u)

                    pe.wait_ge(rows_loaded[q % QBUF].sem, rows_loaded[q % QBUF].at(it, 32 * (q // QBUF + 1)))
                    for kt in range(KT):
                        per_kt = 5 if kt <= 12 else 0
                        for pair in range(2):
                            n = (q * KT + kt) * 2 + pair
                            pe.wait_ge(exped.sem, exped.at(it, n - 1))
                            for h in (2 * pair, 2 * pair + 1):
                                last = pe.matmul(psum[:, SCORE_BANKS + h, :], kst[b][:, h, kt * P:(kt + 1) * P],
                                                 qst[q % QBUF][:, h, :], start=True, stop=True)
                            last.then_inc(scored.sem, 1)
                            if per_kt:
                                units(1)
                        if kt == 14 and some:
                            unit(*ahead, UNITS)
                        if pending is not None:
                            pv(it, *pending, units if per_kt else None)
                        if per_kt:
                            units(per_kt - 3)
                        pending = (q, kt)
                pv(it, *pending, None)

            def pv(it, q, kt, units):
                b, n = q // CHUNKS, q * KT + kt
                if kt == 0:
                    pe.wait_ge(o_copied.sem, o_copied.at(it, q))
                    pe.wait_ge(inv_made.sem, inv_made.at(it, q))
                pe.wait_ge(exped.sem, exped.at(it, 2 * n + 2))
                for h in range(GROUP):
                    pe.matmul(psum[h * DH:(h + 1) * DH, O_BANK, :], vt[b][:, kt, h * DH:(h + 1) * DH],
                              probs[n % PBUF][:, h, :], start=(kt == 0), stop=(kt == KT - 1))
                if units:
                    units(1)
                for h in range(GROUP):
                    last = pe.matmul(psum[h * DH:(h + 1) * DH, L_BANK, :], ones[:],
                                     probs[n % PBUF][:, h, :], start=(kt == 0), stop=(kt == KT - 1))
                last.then_inc(pv_done.sem, 1)

            for u in range(ALL_UNITS):
                unit(0, 0, u)
            with pe.Fori(0, GROUPS - 1) as it:
                body(it, False)
            body(GROUPS - 1, True)

        @block.scalar
        def _(act):
            for t in (exped, o_copied):
                act.sem_inc(t.sem, t.per)

            def copy_o(it, q):
                act.wait_ge(pv_done.sem, pv_done.at(it, (q + 1) * KT))
                act.wait_ge(o_stored[q % 2].sem, o_stored[q % 2].at(it, 16 * (q // 2)))
                act.activation(o_sb[q % 2][:], psum[:, O_BANK, :], ACT.Copy).then_inc(o_copied.sem, 1)

            def body(it):
                for q in range(STEPS):
                    for kt in range(KT):
                        n = q * KT + kt
                        for pair in range(2):
                            act.wait_ge(scored.sem, scored.at(it, 2 * n + pair + 1))
                            if pair == 0:
                                act.wait_ge(pv_done.sem, pv_done.at(it, n - PBUF + 1))
                            act.activation(probs[n % PBUF][:, 2 * pair:2 * pair + 2, :],
                                           psum[:, SCORE_BANKS + 2 * pair:SCORE_BANKS + 2 * pair + 2, :],
                                           ACT.Exp, scale=SCALE).then_inc(exped.sem, 1)
                        if kt == 0 and q >= 1:
                            copy_o(it, q - 1)
                copy_o(it, STEPS - 1)

            with act.Fori(0, GROUPS - 1) as it:
                body(it)
            body(GROUPS - 1)

        @block.vector
        def _(dve):
            for t in (unit_emptied, inv_made):
                dve.sem_inc(t.sem, t.per)

            def unit(it, q, u):
                n, i = q * ALL_UNITS + u, q % 2
                bank = UNIT_BANKS + n % 2
                if u == UNITS:
                    dve.wait_ge(unit_emptied.sem, unit_emptied.at(it, n))
                    dve.tensor_reduce(neg_max[i][:], part_max[i][:], AX.X, ALU.max,
                                      negate=True).then_inc(max_made.sem, 1)
                    dve.wait_ge(unit_filled.sem, unit_filled.at(it, n + 1))
                    dve.tensor_copy(row_hi[i][:], psum[0:GROUP, bank, :]).then_inc(row_steps.sem, 1)
                    dve.wait_ge(row_steps.sem, row_steps.at(it, q + 1))
                    dve.tensor_tensor(row_lo[i][:], psum[0:GROUP, bank, :], row_hi[i][:].bitcast(F32),
                                      ALU.subtract).then_inc(rows_made.sem, 1)
                    dve.wait_ge(rows_made.sem, rows_made.at(it, q + 1))
                    dve.sem_inc(unit_emptied.sem, 1)
                else:
                    dve.wait_ge(unit_filled.sem, unit_filled.at(it, n + 1))
                    dve.tensor_reduce(part_max[i][:, u // CHUNKS, u % CHUNKS:u % CHUNKS + 1], psum[:, bank, :],
                                      AX.X, ALU.max).then_inc(unit_emptied.sem, 1)

            def finish_o(it, q):
                i = q % 2
                dve.wait_ge(pv_done.sem, pv_done.at(it, (q + 1) * KT))
                dve.reciprocal(inv[i][:], psum[:, L_BANK, :]).then_inc(inv_made.sem, 1)
                dve.wait_ge(inv_made.sem, inv_made.at(it, q + 1))
                dve.wait_ge(o_copied.sem, o_copied.at(it, q + 1))
                dve.tensor_tensor(o_sb[i][:], o_sb[i][:], inv[i][:], ALU.mult).then_inc(o_made.sem, 1)

            def body(it, last):
                for q in range(STEPS):
                    ahead = (it, q + 1) if q + 1 < STEPS else (it + 1, 0)
                    some = q + 1 < STEPS or not last
                    for u in range(ALL_UNITS):
                        if some:
                            unit(*ahead, u)
                        if u == 4 and q >= 1:
                            finish_o(it, q - 1)
                finish_o(it, STEPS - 1)

            for u in range(ALL_UNITS):
                unit(0, 0, u)
            with dve.Fori(0, GROUPS - 1) as it:
                body(it, False)
            body(GROUPS - 1, True)


def context_keys(nc, const, name, ctx_d, wk_d, wv_d, norms, biases, kblk, values):
    ident, ones, minus_half = const
    with ExitStack() as ctx:
        def sb(n, shape, dt=F32):
            return ctx.enter_context(nc.sbuf_tensor(f"{name}_{n}", shape, dt))

        def sem(n):
            return ctx.enter_context(nc.semaphore(f"{name}_{n}"))

        rows = sb("ctx", [CTX, BATCH, D])
        w = [sb("wk", [P, KC, D]), sb("wv", [P, KC, D])]
        xT = [sb("kin_T", [P, KC, BATCH * CTX]), sb("vin_T", [P, KC, BATCH * CTX])]
        y = [sb("kin", [CTX, BATCH, D]), sb("vin", [CTX, BATCH, D])] if norms else [rows, rows]
        gb = [[sb(f"gb{i}{j}", [CTX, D]) for j in range(2)] for i in range(2)] if norms else None
        kbias = sb("kbias", [P, KC]) if biases else None
        vbias = sb("vbias", [CTX, D]) if biases else None
        stats, mv = sb("stats", [CTX, BATCH, 6]), sb("mv", [CTX, BATCH, 2])
        veps, rstd = sb("veps", [CTX, BATCH]), sb("rstd", [CTX, BATCH])
        psum = ctx.enter_context(nc.psum_tensor(f"{name}_psum", [P, BANKS, 512], F32))
        loaded, zeroed, veps_made, rstd_made = sem("loaded"), sem("zeroed"), sem("veps_made"), sem("rstd_made")
        steps, normed, filled, emptied = sem("vector_steps"), sem("normed"), sem("filled"), sem("emptied")
        LOADS = 3 + (4 if norms else 0) + (2 if biases else 0)
        sp_alone = Alone(ctx.enter_context(nc.semaphore(f"{name}_sync_waits")))
        dve_alone = Alone(ctx.enter_context(nc.semaphore(f"{name}_vector_waits")))
        block = ctx.enter_context(nc.Block())

        @block.sync
        def _(sp):
            sp.dma_start(rows[:], ctx_d.rearrange("(b n) d -> n b d", b=BATCH)).then_inc(loaded, 16)
            for i, d in enumerate((wk_d, wv_d)):
                sp.dma_start(w[i][:], d.rearrange("(c p) n -> p c n", p=P)).then_inc(loaded, 16)
            if norms:
                for i in range(2):
                    for j in range(2):
                        load_broadcast(sp, gb[i][j][:], norms[i][j], loaded)
            if biases:
                sp.dma_start(kbias[:], biases[0]).then_inc(loaded, 16)
                load_broadcast(sp, vbias[:], biases[1], loaded)

        @block.gpsimd
        def _(pool):
            pool.memset(kblk[:], 0.0).then_inc(zeroed, 1)
            if norms:
                pool.wait_ge(veps_made, 1)
                pool.tensor_tensor(rstd[:], veps[:], minus_half[0:CTX, 0:BATCH], ALU.pow).then_inc(rstd_made, 1)

        @block.vector
        def _(dve):
            chain = Chain(dve, Tally(steps, 0), 0)
            dve.wait_ge(loaded, 16 * LOADS)
            if norms:
                for b in range(BATCH):
                    chain.link(dve.bn_stats(stats[:, b, :], rows[:, b, :]))
                chain.settle(dve_alone)
                for b in range(BATCH):
                    chain.link(dve.bn_aggr(mv[:, b, :], stats[:, b, :]))
                chain.settle()
                dve.tensor_scalar(veps[:], mv[:, :, 1], EPS, None, ALU.add).then_inc(veps_made, 1)
                for i in range(2):
                    for b in range(BATCH):
                        chain.link(dve.scalar_tensor_tensor(y[i][:, b, :], rows[:, b, :], mv[:, b, 0:1], gb[i][0][:],
                                                            ALU.subtract, ALU.mult))
                chain.settle()
                dve.wait_ge(rstd_made, 1)
                for i in range(2):
                    for b in range(BATCH):
                        dve.scalar_tensor_tensor(y[i][:, b, :], y[i][:, b, :], rstd[:, b:b + 1], gb[i][1][:],
                                                 ALU.mult, ALU.add).then_inc(normed, 1)
            for i in range(2):
                for c in range(KC):
                    dve.wait_ge(filled, i * KC + c + 1)
                    dve.tensor_copy(xT[i][:, c, :], psum[:, i * KC + c, 0:BATCH * CTX]).then_inc(emptied, 1)
            dve.wait_ge(zeroed, 1)
            for c in range(KC):
                dve.wait_ge(filled, 2 * KC + c + 1)
                for h in range(GROUP):
                    r = slice(h * DH, (h + 1) * DH)
                    out = kblk[r, :, c, h * CTX:(h + 1) * CTX]
                    src = psum[r, c, 0:BATCH * CTX].rearrange("p (b n) -> p b n", b=BATCH)
                    if biases:
                        dve.tensor_scalar(out, src, kbias[r, c:c + 1], None, ALU.add).then_inc(emptied, 1)
                    else:
                        dve.tensor_copy(out, src).then_inc(emptied, 1)
            for b in range(BATCH):
                dve.wait_ge(filled, 3 * KC + b + 1)
                src = psum[0:CTX, KC + b, :]
                if biases:
                    dve.tensor_tensor(values[:, b, :], src, vbias[:], ALU.add).then_inc(emptied, 1)
                else:
                    dve.tensor_copy(values[:, b, :], src).then_inc(emptied, 1)
            dve.wait_ge(emptied, 2 * KC + KC * GROUP + BATCH)

        @block.tensor
        def _(pe):
            pe.wait_ge(loaded, 16 * LOADS)
            if norms:
                pe.wait_ge(normed, 2 * BATCH)
            for i in range(2):
                for c in range(KC):
                    for b in range(BATCH):
                        last = pe.transpose(psum[:, i * KC + c, b * CTX:(b + 1) * CTX],
                                            y[i][:, b, c * P:(c + 1) * P], ident[0:CTX, 0:CTX])
                    last.then_inc(filled, 1)
            pe.wait_ge(emptied, 2 * KC)
            for c in range(KC):
                for k in range(KC):
                    last = pe.matmul(psum[:, c, 0:BATCH * CTX], w[0][:, k, c * P:(c + 1) * P], xT[0][:, k, :],
                                     start=(k == 0), stop=(k == KC - 1))
                last.then_inc(filled, 1)
            for b in range(BATCH):
                for k in range(KC):
                    last = pe.matmul(psum[0:CTX, KC + b, :], xT[1][:, k, b * CTX:(b + 1) * CTX], w[1][:, k, :],
                                     start=(k == 0), stop=(k == KC - 1))
                last.then_inc(filled, 1)


def cross_attention(nc, const, name, first, x_d, out_d, oT_d, wo0_d, wq_d, wo_d, vectors, q_bias_d, kblk, values):
    ident, ones, minus_half = const
    GW = GROUP * CTX
    with ExitStack() as ctx:
        def sb(n, shape, dt=F32):
            return ctx.enter_context(nc.sbuf_tensor(f"{name}_{n}", shape, dt))

        def tally(n, per, credit=False):
            return Tally(ctx.enter_context(nc.semaphore(f"{name}_{n}")), per, credit)

        weights = ([("wo0", wo0_d)] if first else []) + [("wq", wq_d), ("wo", wo_d)]
        w = {n: (sb(n + "_hi", [P, KC, D], F32R), sb(n + "_lo", [P, KC, D], F32R)) for n, _ in weights}
        vec = [sb(f"vec{i}", [P, D]) for i in range(len(vectors))]
        q_bias = None if first else sb("q_bias", [P, KC])
        oT = [sb(f"oT{s}", [P, KC, CHUNK]) for s in STREAMS] if first else None
        x = [sb(f"x{s}", [P, TILES, D]) for s in STREAMS]
        xT = [[sb(f"xT{p}{s}", [P, KC, CHUNK], F32R) for p in ("hi", "lo")] for s in STREAMS]
        qT = [sb(f"qT{s}", [P, KC, CHUNK]) for s in STREAMS]
        probs = [sb(f"probs{i}", [P, HEADS, CTX]) for i in range(2)]
        pT = sb("pT", [CTX, HEADS, P])
        o2T = [[sb(f"o2T{p}{i}", [P, KC, P], F32R) for p in ("hi", "lo")] for i in range(2)]
        row_max, row_sum, row_inv = (sb(n, [P, HEADS]) for n in ("row_max", "row_sum", "row_inv"))
        stats, mv = sb("stats", [P, TILES, 6]), sb("mv", [P, TILES, 2])
        veps, rstd = sb("veps", [P, TILES]), sb("rstd", [P, TILES])
        psum = ctx.enter_context(nc.psum_tensor(f"{name}_psum", [P, BANKS, 512], F32))
        RING, S_BANK = 4, 4

        split_weights(nc, name, [(d.rearrange("(c p) n -> p c n", p=P), w[n][0][:], w[n][1][:]) for n, d in weights], qT)

        tiles = [(s, t) for s in STREAMS for t in range(TILES)]
        order = []
        if first:
            order += [("out0", s, t, 0) for s in STREAMS for t in range(TILES)]
        for s in STREAMS:
            order += [("turn", s, 0, c) for c in range(KC)] + [("q", s, 0, c) for c in range(KC)]
        for i in range(len(tiles) + 2):
            if i < len(tiles):
                order.append(("scores", 0, i, 0))
            if 1 <= i <= len(tiles):
                order += [("pT", 0, i - 1, c) for c in range(KC)] + [("pv", 0, i - 1, 0)]
            if i >= 2:
                order.append(("out", 0, i - 2, 0))
            if i < len(tiles):
                order.append(("norm", 0, i, 0))
        reader = {"out0": "D", "turn": "D", "q": "A", "pT": "A", "pv": "D", "out": "D"}
        with_bank = [e for e in order if e[0] not in ("scores", "norm")]
        number = {e: n for n, e in enumerate(with_bank)}
        readers = "".join(reader[e[0]] for e in with_bank)
        d_emptied = tally("vector_emptied", readers.count("D"), True)
        a_emptied = tally("scalar_emptied", readers.count("A"), True)
        ring = Ring(RING, readers, {"D": d_emptied, "A": a_emptied})
        hi_events = [e for e in with_bank if e[0] in ("turn", "pv")]
        filled = tally("filled", len(with_bank))
        hi_made = tally("hi_made", len(hi_events))

        def emptied_count(e):
            return readers[:number[e] + 1].count(reader[e[0]])

        loaded = [tally(f"loaded{s}", 32 if first else 16) for s in STREAMS]
        oT_hi = tally("oT_hi", 2)
        oT_lo = tally("oT_lo", 2, True)
        veps_made, rstd_made, normed = tally("veps_made", 2), tally("rstd_made", 2), tally("normed", 2)
        scores_filled = tally("scores_filled", len(tiles))
        scores_emptied = tally("scores_emptied", len(tiles), True)
        exped = tally("exped", len(tiles))
        probs_made = tally("probs_made", len(tiles))
        LINKS = 2 * LN_STEPS + len(tiles) * 3 + (0 if first else len(tiles))
        steps = tally("vector_steps", LINKS)
        stored = [tally(f"stored{s}", 16, True) for s in STREAMS]
        params = ctx.enter_context(nc.semaphore(f"{name}_params"))
        N_PARAMS = len(vectors) + (0 if first else 1)
        sp_alone = Alone(ctx.enter_context(nc.semaphore(f"{name}_sync_waits")))
        dve_alone = Alone(ctx.enter_context(nc.semaphore(f"{name}_vector_waits")))
        block = ctx.enter_context(nc.Block())

        @block.sync
        def _(sp):
            for s in STREAMS:
                sp.sem_inc(stored[s].sem, stored[s].per)
            for v, d in zip(vec, vectors):
                load_broadcast(sp, v[:], d, params)
            if not first:
                sp.dma_start(q_bias[:], q_bias_d).then_inc(params, 16)

            def load(it, s):
                tokens = bass.ds(it * CHUNK + s * SEQ, CHUNK)
                if first:
                    sp_alone.wait(sp, oT_lo.sem, oT_lo.at(it, s + 1 - 2))
                    sp.dma_start(oT[s][:], oT_d[:, tokens].rearrange("(c p) n -> p c n", p=P)).then_inc(loaded[s].sem, 16)
                sp_alone.wait(sp, stored[s].sem, stored[s].at(it, 0))
                sp.dma_start(x[s][:], rows_of(x_d[tokens, :])).then_inc(loaded[s].sem, 16)

            def store(it, s):
                if first:
                    e = ("out", 0, s * TILES + TILES - 1, 0)
                    sp_alone.wait(sp, d_emptied.sem, d_emptied.at(it, emptied_count(e)))
                else:
                    sp_alone.wait(sp, normed.sem, normed.at(it, s + 1))
                sp.dma_start(rows_of(out_d[bass.ds(it * CHUNK + s * SEQ, CHUNK), :]), x[s][:]).then_inc(stored[s].sem, 16)

            def body(it, last):
                load(it, 1)
                store(it, 0)
                if not last:
                    load(it + 1, 0)
                store(it, 1)

            load(0, 0)
            with sp.Fori(0, CHUNKS - 1) as it:
                body(it, False)
            body(CHUNKS - 1, True)
            for s in STREAMS:
                sp_alone.wait(sp, stored[s].sem, stored[s].at(CHUNKS, 0))

        @block.gpsimd
        def _(pool):
            with pool.Fori(0, CHUNKS) as it:
                for s in STREAMS:
                    pool.wait_ge(veps_made.sem, veps_made.at(it, s + 1))
                    pool.tensor_tensor(rstd[:], veps[:], minus_half[:], ALU.pow).then_inc(rstd_made.sem, 1)

        @block.tensor
        def _(pe):
            with pe.Fori(0, CHUNKS) as it:
                for e in order:
                    kind, s, i, c = e
                    if kind == "norm":
                        continue
                    if kind == "scores":
                        s, t = tiles[i]
                        if t == 0:
                            ready = ("q", s, 0, KC - 1)
                            pe.wait_ge(a_emptied.sem, a_emptied.at(it, emptied_count(ready)))
                        pe.wait_ge(scores_emptied.sem, scores_emptied.at(it, i))
                        for g in range(KC):
                            last = pe.matmul(psum[:, S_BANK + g, 0:GW], qT[s][:, g, t * P:(t + 1) * P],
                                             kblk[:, s, g, :], start=True, stop=True)
                        last.then_inc(scores_filled.sem, 1)
                        continue
                    bank = psum[:, ring.bank(number[e]), :]
                    pe.wait_ge(*ring.free(it, number[e]))
                    if kind == "out0":
                        if i == 0:
                            pe.wait_ge(oT_lo.sem, oT_lo.at(it, s + 1))
                        last = split_product(pe, bank, [
                            ((xT[s][0][:, k, i * P:(i + 1) * P], xT[s][1][:, k, i * P:(i + 1) * P]),
                             (w["wo0"][0][:, k, :], w["wo0"][1][:, k, :])) for k in range(KC)])
                    elif kind == "turn":
                        if c == 0:
                            if first:
                                pe.wait_ge(normed.sem, normed.at(it, s + 1))
                            else:
                                pe.wait_ge(loaded[s].sem, loaded[s].at(it, 16))
                        last = transposes(pe, bank, x[s], c, ident[:])
                    elif kind == "q":
                        if c == 0:
                            ready = ("turn", s, 0, KC - 1)
                            pe.wait_ge(d_emptied.sem, d_emptied.at(it, emptied_count(ready)))
                        last = split_product(pe, bank, [
                            ((w["wq"][0][:, k, c * P:(c + 1) * P], w["wq"][1][:, k, c * P:(c + 1) * P]),
                             (xT[s][0][:, k, :], xT[s][1][:, k, :])) for k in range(KC)])
                    elif kind == "pT":
                        if c == 0:
                            pe.wait_ge(probs_made.sem, probs_made.at(it, i + 1))
                        for h in range(GROUP):
                            last = pe.transpose(bank[0:CTX, h * P:(h + 1) * P], probs[i % 2][:, c * GROUP + h, :],
                                                ident[:])
                    elif kind == "pv":
                        s, t = tiles[i]
                        pe.wait_ge(a_emptied.sem, a_emptied.at(it, emptied_count(("pT", 0, i, KC - 1))))
                        for g in range(KC):
                            for h in range(GROUP):
                                last = pe.matmul(bank[h * DH:(h + 1) * DH, g * P:(g + 1) * P],
                                                 values[:, s, (g * GROUP + h) * DH:(g * GROUP + h + 1) * DH],
                                                 pT[:, g * GROUP + h, :], start=True, stop=True)
                    elif kind == "out":
                        pe.wait_ge(d_emptied.sem, d_emptied.at(it, emptied_count(("pv", 0, i, 0))))
                        hi, lo = o2T[i % 2]
                        last = split_product(pe, bank, [
                            ((hi[:, k, :], lo[:, k, :]), (w["wo"][0][:, k, :], w["wo"][1][:, k, :]))
                            for k in range(KC)])
                    last.then_inc(filled.sem, 1)

        @block.scalar
        def _(act):
            act.sem_inc(a_emptied.sem, a_emptied.per)
            act.wait_ge(params, 16 * N_PARAMS)
            with act.Fori(0, CHUNKS) as it:
                if first:
                    for s in STREAMS:
                        act.wait_ge(loaded[s].sem, loaded[s].at(it, 32))
                        act.activation(xT[s][0][:], oT[s][:], ACT.Copy).then_inc(oT_hi.sem, 1)
                for e in order:
                    kind, s, i, c = e
                    if kind == "scores":
                        act.wait_ge(scores_emptied.sem, scores_emptied.at(it, i + 1))
                        act.activation(probs[i % 2][:], probs[i % 2][:], ACT.Exp, scale=SCALE).then_inc(exped.sem, 1)
                        continue
                    if kind in ("out0", "out", "norm"):
                        continue
                    bank = psum[:, ring.bank(number[e]), :]
                    act.wait_ge(filled.sem, filled.at(it, number[e] + 1))
                    if kind == "turn":
                        act.activation(xT[s][0][:, c, :], bank, ACT.Copy).then_inc(hi_made.sem, 1)
                    elif kind == "q":
                        if first:
                            act.activation(qT[s][:, c, :], bank, ACT.Copy).then_inc(a_emptied.sem, 1)
                        else:
                            act.activation(qT[s][:, c, :], bank, ACT.Identity, bias=q_bias[:, c:c + 1]).then_inc(
                                a_emptied.sem, 1)
                    elif kind == "pT":
                        act.activation(pT[:, c * GROUP:(c + 1) * GROUP, :].rearrange("p h n -> p (h n)"),
                                       bank[0:CTX, :], ACT.Copy).then_inc(a_emptied.sem, 1)
                    elif kind == "pv":
                        act.activation(o2T[i % 2][0][:].rearrange("p c n -> p (c n)"), bank,
                                       ACT.Copy).then_inc(hi_made.sem, 1)

        @block.vector
        def _(dve):
            for t in (d_emptied, scores_emptied):
                dve.sem_inc(t.sem, t.per)
            if first:
                dve.sem_inc(oT_lo.sem, oT_lo.per)
            dve.wait_ge(params, 16 * N_PARAMS)
            with dve.Fori(0, CHUNKS) as it:
                chain = Chain(dve, steps, it)

                def norm(s):
                    x_ = x[s]
                    for t in range(TILES):
                        chain.link(dve.bn_stats(stats[:, t, :], x_[:, t, :]))
                    chain.settle(dve_alone)
                    for t in range(TILES):
                        chain.link(dve.bn_aggr(mv[:, t, :], stats[:, t, :]))
                    chain.settle()
                    dve.tensor_scalar(veps[:], mv[:, :, 1], EPS, None, ALU.add).then_inc(veps_made.sem, 1)
                    for t in range(TILES):
                        chain.link(dve.scalar_tensor_tensor(x_[:, t, :], x_[:, t, :], mv[:, t, 0:1], vec[0][:],
                                                            ALU.subtract, ALU.mult))
                    chain.settle()
                    dve.wait_ge(rstd_made.sem, rstd_made.at(it, s + 1))
                    for t in range(TILES):
                        last = dve.scalar_tensor_tensor(x_[:, t, :], x_[:, t, :], rstd[:, t:t + 1], vec[1][:],
                                                        ALU.mult, ALU.add)
                    last.then_inc(normed.sem, 1)

                if first:
                    for s in STREAMS:
                        dve.wait_ge(oT_hi.sem, oT_hi.at(it, s + 1))
                        dve.tensor_tensor(xT[s][1][:], oT[s][:], xT[s][0][:].bitcast(F32),
                                          ALU.subtract).then_inc(oT_lo.sem, 1)
                for e in order:
                    kind, s, i, c = e
                    if kind == "scores":
                        dve.wait_ge(scores_filled.sem, scores_filled.at(it, i + 1))
                        scores = psum[:, S_BANK:S_BANK + KC, 0:GW].rearrange("p g (h n) -> p g h n", h=GROUP)
                        by_head = row_max[:].rearrange("p (g h) -> p g h", g=KC)
                        chain.link(dve.tensor_reduce(by_head, scores, AX.X, ALU.max))
                        chain.settle()
                        dve.tensor_tensor(probs[i % 2][:].rearrange("p (g h) n -> p g h n", g=KC), scores,
                                          by_head.unsqueeze(3).to_broadcast([P, KC, GROUP, CTX]),
                                          ALU.subtract).then_inc(scores_emptied.sem, 1)
                        continue
                    if kind == "norm":
                        dve.wait_ge(exped.sem, exped.at(it, i + 1))
                        chain.link(dve.tensor_reduce(row_sum[:], probs[i % 2][:], AX.X, ALU.add))
                        chain.settle()
                        chain.link(dve.reciprocal(row_inv[:], row_sum[:]))
                        chain.settle()
                        dve.tensor_tensor(probs[i % 2][:], probs[i % 2][:],
                                          row_inv[:].unsqueeze(2).to_broadcast([P, HEADS, CTX]),
                                          ALU.mult).then_inc(probs_made.sem, 1)
                        continue
                    if kind in ("q", "pT"):
                        continue
                    if kind == "turn" and c == 0 and first:
                        norm(s)
                    bank = psum[:, ring.bank(number[e]), :]
                    if kind == "out0":
                        if i == 0:
                            dve.wait_ge(loaded[s].sem, loaded[s].at(it, 32))
                        dve.wait_ge(filled.sem, filled.at(it, number[e] + 1))
                        dve.tensor_tensor(x[s][:, i, :], bank, x[s][:, i, :], ALU.add).then_inc(d_emptied.sem, 1)
                        if i == TILES - 1:
                            dve.wait_ge(d_emptied.sem, d_emptied.at(it, emptied_count(e)))
                    elif kind in ("turn", "pv"):
                        dve.wait_ge(hi_made.sem, hi_made.at(it, hi_events.index(e) + 1))
                        if kind == "turn":
                            hi, lo = xT[s][0][:, c, :], xT[s][1][:, c, :]
                        else:
                            hi, lo = (a[:].rearrange("p c n -> p (c n)") for a in o2T[i % 2])
                        dve.tensor_tensor(lo, bank, hi.bitcast(F32), ALU.subtract).then_inc(d_emptied.sem, 1)
                    elif kind == "out":
                        s, t = tiles[i]
                        dve.wait_ge(filled.sem, filled.at(it, number[e] + 1))
                        dve.tensor_tensor(x[s][:, t, :], bank, x[s][:, t, :], ALU.add).then_inc(d_emptied.sem, 1)
                        if not first:
                            dve.wait_ge(d_emptied.sem, d_emptied.at(it, emptied_count(e)))
                            chain.link(dve.tensor_tensor(x[s][:, t, :], x[s][:, t, :], vec[2][:], ALU.add))
                            if t == TILES - 1:
                                chain.settle()
                                norm(s)
                chain.end()


def mlp(nc, const, x_d, out_d, w1_d, w2_d, b1_d, b2_d, gain_d, bias_d):
    ident, ones, minus_half = const
    PART = 2
    PARTS = DFF // P // PART
    RING, ACC = 4, 4
    SLOTS = range(2)
    N = BATCH * CHUNKS // 2
    with ExitStack() as ctx:
        def sb(n, shape, dt=F32):
            return ctx.enter_context(nc.sbuf_tensor(f"m_{n}", shape, dt))

        def tally(n, per, credit=False, ahead=0):
            return Tally(ctx.enter_context(nc.semaphore(f"m_{n}")), per, credit, ahead)

        w1 = [sb(f"w1_{p}", [P, KC, DFF], F32R) for p in ("hi", "lo")]
        w2 = [sb(f"w2_{p}", [P, DFF // P, D], F32R) for p in ("hi", "lo")]
        gain, bias, b2 = sb("gain", [P, D]), sb("bias", [P, D]), sb("b2", [P, D])
        b1 = sb("b1", [P, DFF // P])
        x = [sb(f"x{s}", [P, TILES, D]) for s in SLOTS]
        h = sb("h", [P, TILES, D])
        hT = [sb(f"hT_{p}", [P, KC, CHUNK], F32R) for p in ("hi", "lo")]
        relu = [sb(f"relu{i}", [P, CHUNK]) for i in range(2)]
        hidden = [[sb(f"hidden_{p}{i}", [P, PART, CHUNK], F32R) for p in ("hi", "lo")] for i in range(2)]
        stats, mv = sb("stats", [P, TILES, 6]), sb("mv", [P, TILES, 2])
        veps, rstd = sb("veps", [P, TILES]), sb("rstd", [P, TILES])
        psum = ctx.enter_context(nc.psum_tensor("m_psum", [P, BANKS, 512], F32))

        jobs = [(w1_d[k * P:(k + 1) * P, :], w1[0][:, k, :], w1[1][:, k, :]) for k in range(KC)]
        raw = [x[0][:].rearrange("p t n -> p (t n)"), x[1][:].rearrange("p t n -> p (t n)")]
        split_weights(nc, "m1", jobs, raw)
        jobs = [(w2_d[k * 4 * P:(k + 1) * 4 * P, :].rearrange("(c p) n -> p c n", p=P),
                 w2[0][:, 4 * k:4 * k + 4, :], w2[1][:, 4 * k:4 * k + 4, :]) for k in range(KC)]
        split_weights(nc, "m2", jobs, x)

        MADE = PARTS * PART
        EVENTS = MADE + KC
        d_emptied = tally("vector_emptied", 2 * KC, True, KC)
        a_emptied = tally("scalar_emptied", 2 * MADE, True)
        ring = Ring(RING, ("A" * MADE + "D" * KC) * 2, {"D": d_emptied, "A": a_emptied})
        filled = tally("filled", 2 * EVENTS, ahead=KC)
        hi_made = tally("hT_hi_made", 2 * KC, ahead=KC)
        hidden_made = tally("hidden_made", 2 * MADE, True)
        split = tally("hidden_hi_made", 2 * MADE)
        part_used = tally("part_used", 2 * PARTS, True)
        out_emptied = tally("out_emptied", 2 * TILES, True)
        loaded = [tally(f"loaded{s}", 16) for s in SLOTS]
        stored = [tally(f"stored{s}", 16, True) for s in SLOTS]
        steps = tally("vector_steps", 2 * LN_STEPS, ahead=LN_STEPS)
        veps_made, rstd_made = tally("veps_made", 2, ahead=1), tally("rstd_made", 2, ahead=1)
        h_made = tally("h_made", 2, ahead=1)
        x_read = tally("x_read", 2, ahead=1)
        b2_added = tally("b2_added", 2, ahead=1)
        params = ctx.enter_context(nc.semaphore("m_params"))
        sp_alone = Alone(ctx.enter_context(nc.semaphore("m_sync_waits")))
        dve_alone = Alone(ctx.enter_context(nc.semaphore("m_vector_waits")))
        block = ctx.enter_context(nc.Block())

        def event(s, j):
            return s * EVENTS + j

        @block.sync
        def _(sp):
            for s in SLOTS:
                sp.sem_inc(stored[s].sem, stored[s].given)
            for v, d in ((gain, gain_d), (bias, bias_d), (b2, b2_d)):
                load_broadcast(sp, v[:], d, params)
            sp.dma_start(b1[:], b1_d).then_inc(params, 16)

            def load(it, s):
                sp_alone.wait(sp, stored[s].sem, stored[s].at(it, 0))
                sp.dma_start(x[s][:], rows_of(x_d[bass.ds(it * (2 * CHUNK) + s * CHUNK, CHUNK), :])).then_inc(
                    loaded[s].sem, 16)

            def body(it, last):
                for s in SLOTS:
                    if s == 0:
                        load(it, 1)
                    elif not last:
                        load(it + 1, 0)
                    sp_alone.wait(sp, out_emptied.sem, out_emptied.at(it, (s + 1) * TILES))
                    sp.dma_start(rows_of(out_d[bass.ds(it * (2 * CHUNK) + s * CHUNK, CHUNK), :]), x[s][:]).then_inc(
                        stored[s].sem, 16)

            load(0, 0)
            with sp.Fori(0, N - 1) as it:
                body(it, False)
            body(N - 1, True)
            for s in SLOTS:
                sp_alone.wait(sp, stored[s].sem, stored[s].at(N, 0))

        @block.gpsimd
        def _(pool):
            pool.wait_ge(params, 64)

            def norm(it, s, k):
                pool.wait_ge(veps_made.sem, veps_made.at(it, k))
                pool.tensor_tensor(rstd[:], veps[:], minus_half[:], ALU.pow).then_inc(rstd_made.sem, 1)
                pool.wait_ge(x_read.sem, x_read.at(it, k))
                pool.tensor_tensor(x[s][:], x[s][:], b2[:].unsqueeze(1).to_broadcast([P, TILES, D]),
                                   ALU.add).then_inc(b2_added.sem, 1)

            norm(0, 0, 0)
            with pool.Fori(0, N - 1) as it:
                for s in SLOTS:
                    norm(it, 1 - s, s + 1)
            norm(N - 1, 1, 1)

        @block.tensor
        def _(pe):
            def turn(it, s, j0):
                pe.wait_ge(h_made.sem, h_made.at(it, s + 1))
                for c in range(KC):
                    if j0 is not None:
                        pe.wait_ge(*ring.free(it, j0 + c))
                    transposes(pe, psum[:, ring.bank((j0 or 0) + c), :], h, c, ident[:]).then_inc(filled.sem, 1)

            def up(it, s, part):
                for m in range(PART):
                    j = part * PART + m
                    e = event(s, j)
                    pe.wait_ge(*ring.free(it, e))
                    split_product(pe, psum[:, ring.bank(e), :], [
                        ((w1[0][:, k, j * P:(j + 1) * P], w1[1][:, k, j * P:(j + 1) * P]),
                         (hT[0][:, k, :], hT[1][:, k, :])) for k in range(KC)]).then_inc(filled.sem, 1)

            def down(it, s, part):
                hi, lo = hidden[part % 2]
                if part == 0:
                    pe.wait_ge(out_emptied.sem, out_emptied.at(it, s * TILES))
                pe.wait_ge(hidden_made.sem, hidden_made.at(it, s * MADE + (part + 1) * PART))
                for t in range(TILES):
                    out = psum[:, ACC + t, :]
                    for m in range(PART):
                        k = part * PART + m
                        ah, al = hi[:, m, t * P:(t + 1) * P], lo[:, m, t * P:(t + 1) * P]
                        pe.matmul(out, ah, w2[0][:, k, :], start=(k == 0), stop=False)
                        pe.matmul(out, ah, w2[1][:, k, :], start=False, stop=False)
                        last = pe.matmul(out, al, w2[0][:, k, :], start=False, stop=(k == DFF // P - 1))
                last.then_inc(part_used.sem, 1)

            def body(it, last):
                for s in SLOTS:
                    pe.wait_ge(d_emptied.sem, d_emptied.at(it, s * KC))
                    up(it, s, 0)
                    for part in range(1, PARTS):
                        up(it, s, part)
                        down(it, s, part - 1)
                    if s == 0 or not last:
                        turn(it, s, event(s, MADE))
                    down(it, s, PARTS - 1)

            turn(0, -1, None)
            with pe.Fori(0, N - 1) as it:
                body(it, False)
            body(N - 1, True)

        @block.scalar
        def _(act):
            act.sem_inc(a_emptied.sem, a_emptied.given)
            act.wait_ge(params, 64)

            def turn(it, s, j0):
                for c in range(KC):
                    act.wait_ge(filled.sem, filled.at(it, j0 + c + 1))
                    act.activation(hT[0][:, c, :], psum[:, ring.bank(j0 + c), :], ACT.Copy).then_inc(hi_made.sem, 1)

            def body(it, last):
                for s in SLOTS:
                    for j in range(MADE):
                        e, n = event(s, j), s * MADE + j
                        act.wait_ge(filled.sem, filled.at(it, e + 1))
                        act.wait_ge(hidden_made.sem, hidden_made.at(it, n - 1))
                        act.activation(relu[j % 2][:], psum[:, ring.bank(e), :], ACT.Relu,
                                       bias=b1[:, j:j + 1]).then_inc(a_emptied.sem, 1)
                    if s == 0 or not last:
                        turn(it, s, event(s, MADE))

            turn(0, -1, -KC)
            with act.Fori(0, N - 1) as it:
                body(it, False)
            body(N - 1, True)

        @block.vector
        def _(dve):
            for t in (d_emptied, hidden_made, part_used, out_emptied):
                dve.sem_inc(t.sem, t.given)
            dve.wait_ge(params, 64)

            def norm(it, s, k, chain):
                x_ = x[s]
                dve.wait_ge(loaded[s].sem, loaded[s].at(it + 1 if k == 2 else it, 16))
                for t in range(TILES):
                    chain.link(dve.bn_stats(stats[:, t, :], x_[:, t, :]))
                chain.settle(dve_alone)
                for t in range(TILES):
                    chain.link(dve.bn_aggr(mv[:, t, :], stats[:, t, :]))
                chain.settle()
                dve.tensor_scalar(veps[:], mv[:, :, 1], EPS, None, ALU.add).then_inc(veps_made.sem, 1)
                for t in range(TILES):
                    last = chain.link(dve.scalar_tensor_tensor(h[:, t, :], x_[:, t, :], mv[:, t, 0:1], gain[:],
                                                               ALU.subtract, ALU.mult))
                chain.settle()
                dve.sem_inc(x_read.sem, 1)
                dve.wait_ge(rstd_made.sem, rstd_made.at(it, k))
                for t in range(TILES):
                    last = dve.scalar_tensor_tensor(h[:, t, :], h[:, t, :], rstd[:, t:t + 1], bias[:],
                                                    ALU.mult, ALU.add)
                last.then_inc(h_made.sem, 1)

            def turn(it, s, j0):
                for c in range(KC):
                    dve.wait_ge(hi_made.sem, hi_made.at(it, s * KC + c + 1))
                    dve.tensor_tensor(hT[1][:, c, :], psum[:, ring.bank(j0 + c), :], hT[0][:, c, :].bitcast(F32),
                                      ALU.subtract).then_inc(d_emptied.sem, 1)

            def body(it, last):
                chain = Chain(dve, steps, it)
                for s in SLOTS:
                    for j in range(MADE):
                        n, (part, m) = s * MADE + j, divmod(j, PART)
                        if j == MADE // 2 and (s == 0 or not last):
                            norm(it, 1 - s, s + 1, chain)
                        dve.wait_ge(a_emptied.sem, a_emptied.at(it, n + 1))
                        dve.wait_ge(part_used.sem, part_used.at(it, s * PARTS + part - 1))
                        hi, lo = (a[:, m, :] for a in hidden[part % 2])
                        dve.tensor_copy(hi, relu[j % 2][:]).then_inc(split.sem, 1)
                        dve.wait_ge(split.sem, split.at(it, n + 1))
                        dve.tensor_tensor(lo, relu[j % 2][:], hi.bitcast(F32), ALU.subtract).then_inc(hidden_made.sem, 1)
                    if s == 0 or not last:
                        turn(it, s, event(s, MADE))
                    dve.wait_ge(part_used.sem, part_used.at(it, (s + 1) * PARTS))
                    dve.wait_ge(b2_added.sem, b2_added.at(it, s))
                    for t in range(TILES):
                        dve.tensor_tensor(x[s][:, t, :], psum[:, ACC + t, :], x[s][:, t, :], ALU.add).then_inc(
                            out_emptied.sem, 1)

            norm(0, 0, 0, Chain(dve, Tally(steps.sem, 0), 0))
            turn(0, -1, -KC)
            with dve.Fori(0, N - 1) as it:
                body(it, False)
            body(N - 1, True)


def two_layers(nc, t, out):
    x, context = t["x"], t["ctx_1024"]
    with ExitStack() as ctx:
        def dram(name, shape):
            return nc.dram_tensor(name, shape, F32, kind="Internal").ap()

        tokens = BATCH * SEQ
        xn, v = dram("xn_scratch", [tokens, D]), dram("v_scratch", [tokens, D])
        q_hi, q_lo, k_hi, k_lo, oT = (dram(n + "_scratch", [D, tokens]) for n in ("q_hi", "q_lo", "k_hi", "k_lo", "oT"))
        after_cross, after_mlp = dram("cross_scratch", [tokens, D]), dram("mlp_scratch", [tokens, D])
        const = make_constants(nc, ctx)
        scratch = (xn, q_hi, q_lo, k_hi, k_lo, v)
        project_qkv(nc, const, x, t["sa_wqT"], t["sa_wkT"], t["sa_wvT"], t["g_sa"], t["b_sa"], scratch)
        self_attention(nc, const, scratch, oT)
        with ExitStack() as held:
            kblk = held.enter_context(nc.sbuf_tensor("kblk0", [P, BATCH, KC, GROUP * CTX], F32))
            values = held.enter_context(nc.sbuf_tensor("values0", [CTX, BATCH, D], F32))
            context_keys(nc, const, "c", context, t["ca_wkT"], t["ca_wvT"],
                         ((t["g_kca"], t["b_kca"]), (t["g_vca"], t["b_vca"])), None, kblk, values)
            cross_attention(nc, const, "d", True, xn, after_cross, oT, t["sa_woT"], t["ca_wqT"], t["ca_woT"],
                            (t["g_qca"], t["b_qca"]), None, kblk, values)
        mlp(nc, const, after_cross, after_mlp, t["w1T"], t["w2T"], t["b1"], t["b2"], t["g_out"], t["b_out"])
        with ExitStack() as held:
            kblk = held.enter_context(nc.sbuf_tensor("kblk1", [P, BATCH, KC, GROUP * CTX], F32))
            values = held.enter_context(nc.sbuf_tensor("values1", [CTX, BATCH, D], F32))
            context_keys(nc, const, "f", context, t["l1_wkT"], t["l1_wvT"], None, (t["l1_bk"], t["l1_bv"]), kblk, values)
            cross_attention(nc, const, "g", False, after_mlp, out, None, None, t["l1_wqT"], t["l1_woT"],
                            (t["l1_gain"], t["l1_bias"], t["l1_bo"]), t["l1_bq"], kblk, values)


def kernel(**inputs):
    import numpy as np
    import concourse.bacc as bacc
    from concourse.bass_utils import run_bass_kernel_spmd

    def turned(a):
        return np.ascontiguousarray(np.asarray(a).T)

    def by_partition(a):
        return np.ascontiguousarray(np.asarray(a).reshape(-1, P).T)

    a0 = {k[len("L0_xattn_"):]: np.asarray(v) for k, v in inputs.items() if k.startswith("L0_xattn_")}
    a1 = {k[len("L1_xattn_"):]: np.asarray(v) for k, v in inputs.items() if k.startswith("L1_xattn_")}
    arrays = {
        "x": np.ascontiguousarray(np.asarray(inputs["x"]).reshape(BATCH * SEQ, D)),
        "ctx_1024": np.ascontiguousarray(np.asarray(inputs["ctx_1024"]).reshape(BATCH * CTX, D)),
    }
    for n in ("sa_wq", "sa_wk", "sa_wv", "sa_wo", "ca_wq", "ca_wk", "ca_wv", "ca_wo"):
        arrays[n + "T"] = turned(a0[n])
    for n in ("g_sa", "b_sa", "g_qca", "b_qca", "g_kca", "b_kca", "g_vca", "b_vca", "g_out", "b_out"):
        arrays[n] = np.ascontiguousarray(a0[n])
    arrays["w1T"], arrays["w2T"] = turned(a0["ffn_w1"]), turned(a0["ffn_w2"])
    arrays["b1"], arrays["b2"] = by_partition(a0["ffn_b1"]), np.ascontiguousarray(a0["ffn_b2"])
    for i, n in enumerate(("wq", "wk", "wv")):
        arrays[f"l1_{n}T"] = turned(a1["W_qkv"][i * D:(i + 1) * D])
    arrays["l1_woT"] = turned(a1["W_o"])
    arrays["l1_bq"] = by_partition(a1["b_qkv"][0:D])
    arrays["l1_bk"] = by_partition(a1["b_qkv"][D:2 * D])
    arrays["l1_bv"] = np.ascontiguousarray(a1["b_qkv"][2 * D:3 * D])
    arrays["l1_bo"] = np.ascontiguousarray(a1["b_o"])
    arrays["l1_gain"], arrays["l1_bias"] = np.ascontiguousarray(a1["ln_gamma"]), np.ascontiguousarray(a1["ln_beta"])

    nc = bacc.Bacc("TRN2", target_bir_lowering=False, num_devices=1)
    handles = {n: nc.dram_tensor(n, a.shape, mybir.dt.from_np(a.dtype), kind="ExternalInput").ap()
               for n, a in arrays.items()}
    out = nc.dram_tensor("out", [BATCH * SEQ, D], F32, kind="ExternalOutput").ap()
    two_layers(nc, handles, out)
    result = run_bass_kernel_spmd(nc, [arrays], core_ids=[0]).results[0]["out"]
    return np.asarray(result).reshape(BATCH, SEQ, D)
```

```python
from contextlib import ExitStack

import concourse.bass as bass
from concourse import mybir

F32 = mybir.dt.float32
F32R = mybir.dt.float32r
ALU = mybir.AluOpType
ACT = mybir.ActivationFunctionType
AX = mybir.AxisListType

P = 128
BATCH, SEQ, D = 2, 2048, 512
CTX = 77
HEADS, DH = 16, 32
DFF = 4 * D
KC = D // P
GROUP = P // DH
CHUNK = 512
TILES = CHUNK // P
CHUNKS = SEQ // CHUNK
KT = SEQ // P
BANKS = 8
EPS = 1e-5
SCALE = float(DH) ** -0.5
STREAMS = range(BATCH)


class Tally:

    def __init__(self, sem, per, credit=False, ahead=0):
        self.sem, self.per, self.start = sem, per, per if credit else ahead
        self.given = per - ahead if credit else 0

    def at(self, it, k):
        return it * self.per + (k + self.start)


class Chain:

    def __init__(self, eng, tally, it):
        self.eng, self.tally, self.it, self.n = eng, tally, it, 0

    def link(self, ins):
        self.n += 1
        return ins.then_inc(self.tally.sem, 1)

    def settle(self, alone=None):
        value = self.tally.at(self.it, self.n)
        if alone:
            alone.wait(self.eng, self.tally.sem, value)
        else:
            self.eng.wait_ge(self.tally.sem, value)

    def end(self):
        assert self.n == self.tally.per, (self.n, self.tally.per)


class Alone:

    def __init__(self, sem):
        self.sem = sem

    def wait(self, eng, sem, value):
        eng.wait_ge(sem, value)
        eng.sem_inc(self.sem, 1)


class Ring:

    def __init__(self, banks, readers, tallies):
        self.banks, self.readers, self.tallies = banks, readers, tallies
        assert len(readers) % banks == 0
        for r, t in tallies.items():
            assert t.per == readers.count(r), (r, t.per, readers.count(r))

    def bank(self, e):
        return e % self.banks

    def free(self, it, e):
        back = e - self.banks
        r = self.readers[back]
        n = self.readers[:back % len(self.readers)].count(r) + 1 - (self.tallies[r].per if back < 0 else 0)
        return self.tallies[r].sem, self.tallies[r].at(it, n)


def split_product(pe, out, pairs):
    n = len(pairs)
    for i, ((ah, al), (bh, bl)) in enumerate(pairs):
        pe.matmul(out, ah, bh, start=(i == 0), stop=False)
        pe.matmul(out, ah, bl, start=False, stop=False)
        last = pe.matmul(out, al, bh, start=False, stop=(i == n - 1))
    return last


def transposes(pe, bank, src, kc, ident):
    for t in range(TILES):
        last = pe.transpose(bank[:, t * P:(t + 1) * P], src[:, t, kc * P:(kc + 1) * P], ident)
    return last


LN_STEPS = 3 * TILES


def make_constants(nc, ctx):
    ident = ctx.enter_context(nc.sbuf_tensor("ident", [P, P], F32))
    ones = ctx.enter_context(nc.sbuf_tensor("ones", [P, DH], F32))
    minus_half = ctx.enter_context(nc.sbuf_tensor("minus_half", [P, TILES], F32))
    made = ctx.enter_context(nc.semaphore("constants_made"))
    with nc.Block() as block:
        @block.gpsimd
        def _(pool):
            pool.memset(ones[:], 1.0).then_inc(made, 1)
            pool.memset(minus_half[:], -0.5).then_inc(made, 1)
            pool.memset(ident[:], 0.0).then_inc(made, 1)
            pool.wait_ge(made, 3)
            pool.affine_select(out=ident[:], in_=ident[:], compare_op=ALU.not_equal, fill=1.0, base=0,
                               pattern=[[-1, P]], channel_multiplier=1).then_inc(made, 1)
            pool.wait_ge(made, 4)
    sp_alone = Alone(ctx.enter_context(nc.semaphore("sync_waits")))
    dve_alone = Alone(ctx.enter_context(nc.semaphore("vector_waits")))
    return ident, ones, minus_half, sp_alone, dve_alone


def split_weights(nc, name, jobs, raw):
    with ExitStack() as ctx:
        loaded = [ctx.enter_context(nc.semaphore(f"{name}_w_loaded{i}")) for i in range(2)]
        hi_made = ctx.enter_context(nc.semaphore(f"{name}_w_hi"))
        lo_made = ctx.enter_context(nc.semaphore(f"{name}_w_lo"))
        block = ctx.enter_context(nc.Block())

        @block.sync
        def _(sp):
            for n, (src, hi, lo) in enumerate(jobs):
                if n >= 2:
                    sp.wait_ge(lo_made, n - 1)
                sp.dma_start(raw[n % 2][:], src).then_inc(loaded[n % 2], 16)

        @block.scalar
        def _(act):
            for n, (src, hi, lo) in enumerate(jobs):
                act.wait_ge(loaded[n % 2], 16 * (n // 2 + 1))
                act.activation(hi, raw[n % 2][:], ACT.Copy).then_inc(hi_made, 1)

        @block.vector
        def _(dve):
            for n, (src, hi, lo) in enumerate(jobs):
                dve.wait_ge(hi_made, n + 1)
                dve.tensor_tensor(lo, raw[n % 2][:], hi.bitcast(F32), ALU.subtract).then_inc(lo_made, 1)
            dve.wait_ge(lo_made, len(jobs))


def rows_of(a, t=TILES):
    return a.rearrange("(t p) n -> p t n", p=P)


def load_broadcast(eng, dst, src, sem):
    return eng.dma_start(dst, src.rearrange("(a n) -> a n", a=1).to_broadcast(list(dst.shape))).then_inc(sem, 16)


def project_qkv(nc, const, x, wq, wk, wv, gain_d, bias_d, scratch):
    ident, ones, minus_half, sp_alone, dve_alone = const
    xn_d, q_hi_d, q_lo_d, k_hi_d, k_lo_d, v_d = scratch
    with ExitStack() as ctx:
        def sb(name, shape, dt=F32):
            return ctx.enter_context(nc.sbuf_tensor("a_" + name, shape, dt))

        def tally(name, per, credit=False):
            return Tally(ctx.enter_context(nc.semaphore("a_" + name)), per, credit)

        w = {n: (sb(f"w{n}_hi", [P, KC, D], F32R), sb(f"w{n}_lo", [P, KC, D], F32R)) for n in "qkv"}
        gain, bias = sb("gain", [P, D]), sb("bias", [P, D])
        xin = [sb(f"xin{s}", [P, TILES, D]) for s in STREAMS]
        xn = [sb(f"xn{s}", [P, TILES, D]) for s in STREAMS]
        xT = [[sb(f"xT{p}{s}", [P, KC, CHUNK], F32R) for p in ("hi", "lo")] for s in STREAMS]
        stage = [{n: [sb(f"{n}T{p}{s}", [P, KC, CHUNK], F32R) for p in ("hi", "lo")] for n in "qk"} for s in STREAMS]
        vst = [sb(f"v{s}", [P, TILES, D]) for s in STREAMS]
        stats, mv = sb("stats", [P, TILES, 6]), sb("mv", [P, TILES, 2])
        veps, rstd = sb("veps", [P, TILES]), sb("rstd", [P, TILES])
        psum = ctx.enter_context(nc.psum_tensor("a_psum", [P, BANKS, 512], F32))

        raw = [xin[0][:].rearrange("p t n -> p (t n)"), xin[1][:].rearrange("p t n -> p (t n)")]
        jobs = []
        for n, src in (("q", wq), ("k", wk), ("v", wv)):
            jobs.append((src.rearrange("(c p) n -> p c n", p=P),
                         w[n][0][:], w[n][1][:]))
        split_weights(nc, "a", jobs, xin)

        PER_STREAM = 4 * 4
        params = ctx.enter_context(nc.semaphore("a_params"))
        loaded = [tally(f"x_loaded{s}", 16) for s in STREAMS]
        normed = [tally(f"normed{s}", 1, True) for s in STREAMS]
        filled = tally("bank_filled", 2 * PER_STREAM)
        hi_made = tally("hi_made", 2 * 12)
        emptied = tally("bank_emptied", 2 * PER_STREAM, True)
        steps = tally("vector_steps", 2 * LN_STEPS)
        veps_made = tally("veps_made", 2)
        rstd_made = tally("rstd_made", 2)
        stored = [{n: tally(f"{n}_stored{s}", 16 * (2 if n in "qk" else 1), True) for n in ("xn", "q", "k", "v")}
                  for s in STREAMS]
        ring = Ring(BANKS, "D" * (2 * PER_STREAM), {"D": emptied})
        block = ctx.enter_context(nc.Block())

        def event(s, j):
            return s * PER_STREAM + j

        @block.scalar
        def _(act):
            load_broadcast(act, gain[:], gain_d, params)
            load_broadcast(act, bias[:], bias_d, params)
            for s in STREAMS:
                act.sem_inc(normed[s].sem, normed[s].per)
            with act.Fori(0, CHUNKS) as it:
                for s in STREAMS:
                    act.wait_ge(normed[s].sem, normed[s].at(it, 0))
                    act.dma_start(xin[s][:], rows_of(x[bass.ds(it * CHUNK + s * SEQ, CHUNK), :])).then_inc(loaded[s].sem, 16)
                for s in STREAMS:
                    for j in range(12):
                        e = event(s, j)
                        part, c = divmod(j, 4)
                        hi = (xT[s][0], stage[s]["q"][0], stage[s]["k"][0])[part]
                        if part and c == 0:
                            st = stored[s]["qk"[part - 1]]
                            act.wait_ge(st.sem, st.at(it, 0))
                        act.wait_ge(filled.sem, filled.at(it, e + 1))
                        act.activation(hi[:, c, :], psum[:, ring.bank(e), :], ACT.Copy).then_inc(hi_made.sem, 1)

        @block.gpsimd
        def _(pool):
            with pool.Fori(0, CHUNKS) as it:
                for s in STREAMS:
                    pool.wait_ge(veps_made.sem, veps_made.at(it, s + 1))
                    pool.tensor_tensor(rstd[:], veps[:], minus_half[:], ALU.pow).then_inc(rstd_made.sem, 1)

        @block.vector
        def _(dve):
            dve.sem_inc(emptied.sem, emptied.per)
            dve.wait_ge(params, 32)
            with dve.Fori(0, CHUNKS) as it:
                chain = Chain(dve, steps, it)
                for s in STREAMS:
                    dve.wait_ge(loaded[s].sem, loaded[s].at(it, 16))
                    dve.wait_ge(stored[s]["xn"].sem, stored[s]["xn"].at(it, 0))
                    x_, y_ = xin[s], xn[s]
                    for t in range(TILES):
                        chain.link(dve.bn_stats(stats[:, t, :], x_[:, t, :]))
                    chain.settle(dve_alone)
                    for t in range(TILES):
                        chain.link(dve.bn_aggr(mv[:, t, :], stats[:, t, :]))
                    chain.settle()
                    dve.tensor_scalar(veps[:], mv[:, :, 1], EPS, None, ALU.add).then_inc(veps_made.sem, 1)
                    for t in range(TILES):
                        chain.link(dve.scalar_tensor_tensor(y_[:, t, :], x_[:, t, :], mv[:, t, 0:1], gain[:],
                                                            ALU.subtract, ALU.mult))
                    chain.settle()
                    dve.wait_ge(rstd_made.sem, rstd_made.at(it, s + 1))
                    for t in range(TILES):
                        last = dve.scalar_tensor_tensor(y_[:, t, :], y_[:, t, :], rstd[:, t:t + 1], bias[:],
                                                        ALU.mult, ALU.add)
                    last.then_inc(normed[s].sem, 1)
                    for j in range(PER_STREAM):
                        e = event(s, j)
                        part, c = divmod(j, 4)
                        if part < 3:
                            hi, lo = (xT[s], stage[s]["q"], stage[s]["k"])[part]
                            if part and c == 0:
                                st = stored[s]["qk"[part - 1]]
                                dve.wait_ge(st.sem, st.at(it, 0))
                            dve.wait_ge(hi_made.sem, hi_made.at(it, s * 12 + j + 1))
                            dve.tensor_tensor(lo[:, c, :], psum[:, ring.bank(e), :], hi[:, c, :].bitcast(F32),
                                              ALU.subtract).then_inc(emptied.sem, 1)
                        else:
                            if c == 0:
                                dve.wait_ge(stored[s]["v"].sem, stored[s]["v"].at(it, 0))
                            dve.wait_ge(filled.sem, filled.at(it, e + 1))
                            dve.tensor_copy(vst[s][:, c, :], psum[:, ring.bank(e), :]).then_inc(emptied.sem, 1)

        @block.tensor
        def _(pe):
            with pe.Fori(0, CHUNKS) as it:
                for s in STREAMS:
                    pe.wait_ge(normed[s].sem, normed[s].at(it, 1))
                    for j in range(PER_STREAM):
                        e = event(s, j)
                        part, c = divmod(j, 4)
                        bank = psum[:, ring.bank(e), :]
                        pe.wait_ge(*ring.free(it, e))
                        if part == 0:
                            last = transposes(pe, bank, xn[s], c, ident[:])
                        elif part < 3:
                            if part == 1 and c == 0:
                                pe.wait_ge(emptied.sem, emptied.at(it, event(s, 4)))
                            wh, wl = w["qk"[part - 1]]
                            last = split_product(pe, bank, [
                                ((wh[:, k, c * P:(c + 1) * P], wl[:, k, c * P:(c + 1) * P]),
                                 (xT[s][0][:, k, :], xT[s][1][:, k, :])) for k in range(KC)])
                        else:
                            wh, wl = w["v"]
                            last = split_product(pe, bank, [
                                ((xT[s][0][:, k, c * P:(c + 1) * P], xT[s][1][:, k, c * P:(c + 1) * P]),
                                 (wh[:, k, :], wl[:, k, :])) for k in range(KC)])
                        last.then_inc(filled.sem, 1)

        @block.sync
        def _(sp):
            for s in STREAMS:
                for n in ("xn", "q", "k", "v"):
                    sp.sem_inc(stored[s][n].sem, stored[s][n].per)
            with sp.Fori(0, CHUNKS) as it:
                for s in STREAMS:
                    tokens = bass.ds(it * CHUNK + s * SEQ, CHUNK)
                    sp_alone.wait(sp, normed[s].sem, normed[s].at(it, 1))
                    sp.dma_start(rows_of(xn_d[tokens, :]), xn[s][:]).then_inc(stored[s]["xn"].sem, 16)
                    for part, (n, hi_d, lo_d) in enumerate((("q", q_hi_d, q_lo_d), ("k", k_hi_d, k_lo_d))):
                        sp_alone.wait(sp, emptied.sem, emptied.at(it, event(s, 4 * part + 8)))
                        for d, buf in zip((hi_d, lo_d), stage[s][n]):
                            sp.dma_start(d[:, tokens].rearrange("(c p) n -> p c n", p=P),
                                         buf[:].bitcast(F32)).then_inc(stored[s][n].sem, 16)
                    sp_alone.wait(sp, emptied.sem, emptied.at(it, event(s, 16)))
                    sp.dma_start(rows_of(v_d[tokens, :]), vst[s][:]).then_inc(stored[s]["v"].sem, 16)
            for s in STREAMS:
                for n in ("xn", "q", "k", "v"):
                    sp_alone.wait(sp, stored[s][n].sem, stored[s][n].at(CHUNKS, 0))


def self_attention(nc, const, scratch, oT_d):
    ident, ones, minus_half, sp_alone, dve_alone = const
    xn_d, q_hi_d, q_lo_d, k_hi_d, k_lo_d, v_d = scratch
    STACK = 3 * DH
    ROWS = STACK + 2
    STEPS = BATCH * CHUNKS
    GROUPS = HEADS // GROUP
    QBUF, PBUF = 4, 4
    UNITS = TILES * GROUP * CHUNKS
    ALL_UNITS = UNITS + 1
    UB, SB = 3, 3
    UNIT_BANKS, SCORE_BANKS, O_BANK, L_BANK = 0, UB, UB + SB, UB + SB + 1
    DIRECT = (2, 5, 8, 11, 14)
    ADDED = [kt for kt in range(KT) if kt not in DIRECT]
    ADDS = len(ADDED) - 1
    NO_UNITS, TURN_AT = 2, 12
    SLOTS = [4 * (kt != NO_UNITS) + (kt - 1 in DIRECT) for kt in range(KT)]
    EARLY = ALL_UNITS - sum(SLOTS[:TURN_AT + 1])
    assert sum(SLOTS) == ALL_UNITS
    SUMS_AT = sum(SLOTS[:NO_UNITS]) - 1
    with ExitStack() as ctx:
        def sb(name, shape, dt=F32):
            return ctx.enter_context(nc.sbuf_tensor("b_" + name, shape, dt))

        def tally(name, per, credit=False):
            return Tally(ctx.enter_context(nc.semaphore("b_" + name)), per, credit)

        kst = [sb(f"k_stack{b}", [ROWS, GROUP, SEQ], F32R) for b in STREAMS]
        qst = [sb(f"q_stack{i}", [ROWS, GROUP, CHUNK], F32R) for i in range(QBUF)]
        vt = [sb(f"v{b}", [P, KT, P]) for b in STREAMS]
        probs = [sb(f"probs{i}", [P, GROUP, CHUNK]) for i in range(PBUF)]
        part_max = [sb(f"part_max{i}", [P, TILES * GROUP, CHUNKS]) for i in range(2)]
        neg_max = [sb(f"neg_max{i}", [P, TILES * GROUP]) for i in range(2)]
        row_hi = [sb(f"row_hi{i}", [GROUP, CHUNK], F32R) for i in range(2)]
        row_lo = [sb(f"row_lo{i}", [GROUP, CHUNK], F32R) for i in range(2)]
        added = [sb(f"added{i}", [P, GROUP, CHUNK]) for i in range(2)]
        o_sb = [sb(f"o{i}", [P, CHUNK]) for i in range(2)]
        inv = [sb(f"inv{i}", [P, CHUNK]) for i in range(2)]
        psum = ctx.enter_context(nc.psum_tensor("b_psum", [P, BANKS, 512], F32))

        k_loaded = [tally(f"k_loaded{b}", 64) for b in STREAMS]
        q_loaded = [tally(f"q_loaded{i}", 48 * STEPS // QBUF) for i in range(QBUF)]
        rows_loaded = [tally(f"rows_loaded{i}", 32 * STEPS // QBUF) for i in range(QBUF)]
        unit_filled = tally("unit_filled", STEPS * ALL_UNITS)
        unit_emptied = tally("unit_emptied", STEPS * ALL_UNITS, True)
        max_made = tally("max_made", STEPS)
        rows_made = tally("rows_made", STEPS)
        row_steps = tally("row_steps", STEPS)
        scored = tally("scored", STEPS * KT * GROUP)
        exped = tally("exped", STEPS * KT * GROUP, True)
        adds = tally("adds", STEPS * ADDS, True)
        l_done = tally("l_done", STEPS, True)
        pv_done = tally("pv_done", STEPS * KT, True)
        o_copied = tally("o_copied", STEPS, True)
        inv_made = tally("inv_made", STEPS, True)
        o_made = tally("o_made", STEPS)
        o_stored = [tally(f"o_stored{i}", 16 * STEPS // 2, True) for i in range(2)]
        ones_made = ctx.enter_context(nc.semaphore("b_ones_made"))
        block = ctx.enter_context(nc.Block())

        def tokens(q):
            return (q // CHUNKS) * SEQ + (q % CHUNKS) * CHUNK

        def units_of(q, last_group):
            todo = [(q + 1, u) for u in range(EARLY, ALL_UNITS)] + [(q + 2, u) for u in range(EARLY)]
            return [(a, u) for a, u in todo if a < STEPS or not last_group]

        def same_bank_before(n):
            per = STEPS * ALL_UNITS
            return n - UB if n >= UB else max(m for m in range(per - UB, per) if m % UB == n % UB) - per

        first_units = [(0, u) for u in range(ALL_UNITS)] + [(1, u) for u in range(EARLY)]

        @block.gpsimd
        def _(pool):
            for b in STREAMS:
                pool.memset(kst[b][STACK:ROWS].bitcast(F32), 1.0).then_inc(ones_made, 1)
            pool.sem_inc(adds.sem, adds.given)

            def body(it):
                for q in range(STEPS):
                    for i, kt in enumerate(ADDED):
                        if i == 0:
                            continue
                        n, total = q * KT + kt, added[q % 2][:]
                        pool.wait_ge(exped.sem, exped.at(it, GROUP * (n + 1)))
                        if i == 1:
                            pool.wait_ge(l_done.sem, l_done.at(it, q - 1))
                            before = probs[(q * KT + ADDED[0]) % PBUF][:]
                        else:
                            pool.wait_ge(adds.sem, adds.at(it, q * ADDS + i - 1))
                            before = total
                        pool.tensor_tensor(total, before, probs[n % PBUF][:], ALU.add).then_inc(adds.sem, 1)

            with pool.Fori(0, GROUPS - 1) as it:
                body(it)
            body(GROUPS - 1)

        @block.sync
        def _(sp):
            sp.sem_inc(pv_done.sem, pv_done.per)
            sp.sem_inc(l_done.sem, l_done.per)
            for i in range(2):
                sp.sem_inc(o_stored[i].sem, o_stored[i].per)

            def load_k(it, b):
                rows, cols = bass.ds(it * P, P), slice(b * SEQ, (b + 1) * SEQ)
                for n, d in enumerate((k_hi_d, k_lo_d, k_hi_d)):
                    sp.dma_start(kst[b][n * DH:(n + 1) * DH].bitcast(F32),
                                 d[rows, cols].rearrange("(h p) n -> p h n", p=DH)).then_inc(k_loaded[b].sem, 16)
                sp.dma_start(vt[b][:], v_d[cols, rows].rearrange("(t p) n -> p t n", p=P)).then_inc(k_loaded[b].sem, 16)

            def load_q(it, q):
                rows, cols = bass.ds(it * P, P), slice(tokens(q), tokens(q) + CHUNK)
                for n, d in enumerate((q_hi_d, q_hi_d, q_lo_d)):
                    sp.dma_start(qst[q % QBUF][n * DH:(n + 1) * DH].bitcast(F32),
                                 d[rows, cols].rearrange("(h p) n -> p h n", p=DH)).then_inc(q_loaded[q % QBUF].sem, 16)

            def send_rows(it, q):
                sp_alone.wait(sp, rows_made.sem, rows_made.at(it, q + 1))
                for n, row in enumerate((row_hi[q % 2], row_lo[q % 2])):
                    sp.dma_start(qst[q % QBUF][STACK + n:STACK + n + 1].bitcast(F32),
                                 row[:].bitcast(F32)).then_inc(rows_loaded[q % QBUF].sem, 16)

            def store_o(it, q):
                sp_alone.wait(sp, o_made.sem, o_made.at(it, q + 1))
                sp.dma_start(oT_d[bass.ds(it * P, P), tokens(q):tokens(q) + CHUNK], o_sb[q % 2][:]).then_inc(
                    o_stored[q % 2].sem, 16)

            def body(it, last):
                for q in range(STEPS):
                    if q == 0:
                        sp_alone.wait(sp, pv_done.sem, pv_done.at(it, 0))
                        load_k(it, 1)
                    if q == CHUNKS and not last:
                        sp_alone.wait(sp, pv_done.sem, pv_done.at(it, CHUNKS * KT))
                        load_k(it + 1, 0)
                    if q + 2 < STEPS or not last:
                        sp_alone.wait(sp, pv_done.sem, pv_done.at(it, (q - 1) * KT))
                        load_q(*((it, q + 2) if q + 2 < STEPS else (it + 1, q + 2 - STEPS)))
                    if q >= 1:
                        store_o(it, q - 1)
                    if q + 1 < STEPS:
                        send_rows(it, q + 1)
                    elif not last:
                        send_rows(it + 1, 0)
                store_o(it, STEPS - 1)

            load_k(0, 0)
            load_q(0, 0)
            load_q(0, 1)
            send_rows(0, 0)
            with sp.Fori(0, GROUPS - 1) as it:
                body(it, False)
            body(GROUPS - 1, True)
            for i in range(2):
                sp_alone.wait(sp, o_stored[i].sem, o_stored[i].at(GROUPS, 0))

        @block.tensor
        def _(pe):
            pe.wait_ge(ones_made, len(STREAMS))

            def unit(it, q, u):
                it, q = (it, q) if q < STEPS else (it + 1, q - STEPS)
                b, n = q // CHUNKS, q * ALL_UNITS + u
                bank = UNIT_BANKS + n % UB
                if u == 0:
                    pe.wait_ge(q_loaded[q % QBUF].sem, q_loaded[q % QBUF].at(it, 48 * (q // QBUF + 1)))
                    pe.wait_ge(k_loaded[b].sem, k_loaded[b].at(it, 64))
                pe.wait_ge(unit_emptied.sem, unit_emptied.at(it, same_bank_before(n) + 1))
                if u < UNITS:
                    (t, h), c = divmod(u // CHUNKS, GROUP), u % CHUNKS
                    last = pe.matmul(psum[:, bank, :], qst[q % QBUF][0:STACK, h, t * P:(t + 1) * P],
                                     kst[b][0:STACK, h, c * 512:(c + 1) * 512], start=True, stop=True)
                else:
                    pe.wait_ge(max_made.sem, max_made.at(it, q + 1))
                    for t in range(TILES):
                        last = pe.transpose(psum[0:GROUP, bank, t * P:(t + 1) * P],
                                            neg_max[q % 2][:, t * GROUP:(t + 1) * GROUP], ident[:])
                last.then_inc(unit_filled.sem, 1)

            def body(it, last_group):
                pending = None
                for q in range(STEPS):
                    todo = iter(units_of(q, last_group))

                    def units(n):
                        for _ in range(n):
                            step, u = next(todo, (0, None))
                            if u is not None:
                                unit(it, step, u)

                    pe.wait_ge(rows_loaded[q % QBUF].sem, rows_loaded[q % QBUF].at(it, 32 * (q // QBUF + 1)))
                    for kt in range(KT):
                        one = 0 if kt == NO_UNITS else 1
                        units(one)
                        scores(it, q, kt, 0)
                        scores(it, q, kt, 1)
                        units(one)
                        scores(it, q, kt, 2)
                        units(one)
                        if pending is not None:
                            pv(it, *pending, units)
                        scores(it, q, kt, 3)
                        if kt == NO_UNITS - 1 and q >= 1:
                            sum_added(it, q - 1)
                        units(one)
                        pending = (q, kt)
                pv(it, *pending, units)
                sum_added(it, STEPS - 1)

            def scores(it, q, kt, h):
                n = (q * KT + kt) * GROUP + h
                pe.wait_ge(exped.sem, exped.at(it, n - SB + 1))
                pe.matmul(psum[:, SCORE_BANKS + n % SB, :], kst[q // CHUNKS][:, h, kt * P:(kt + 1) * P],
                          qst[q % QBUF][:, h, :], start=True, stop=True).then_inc(scored.sem, 1)

            def pv(it, q, kt, units):
                b, n = q // CHUNKS, q * KT + kt
                if kt == 0:
                    pe.wait_ge(o_copied.sem, o_copied.at(it, q))
                pe.wait_ge(exped.sem, exped.at(it, GROUP * (n + 1)))
                for h in range(GROUP):
                    last = pe.matmul(psum[h * DH:(h + 1) * DH, O_BANK, :], vt[b][:, kt, h * DH:(h + 1) * DH],
                                     probs[n % PBUF][:, h, :], start=(kt == 0), stop=(kt == KT - 1))
                if kt in DIRECT:
                    units(1)
                    if kt == DIRECT[0]:
                        pe.wait_ge(inv_made.sem, inv_made.at(it, q))
                    for h in range(GROUP):
                        last = pe.matmul(psum[h * DH:(h + 1) * DH, L_BANK, :], ones[:],
                                         probs[n % PBUF][:, h, :], start=(kt == DIRECT[0]), stop=False)
                last.then_inc(pv_done.sem, 1)

            def sum_added(it, q):
                pe.wait_ge(adds.sem, adds.at(it, (q + 1) * ADDS))
                for h in range(GROUP):
                    last = pe.matmul(psum[h * DH:(h + 1) * DH, L_BANK, :], ones[:], added[q % 2][:, h, :],
                                     start=False, stop=True)
                last.then_inc(l_done.sem, 1)

            for q, u in first_units:
                unit(0, q, u)
            with pe.Fori(0, GROUPS - 1) as it:
                body(it, False)
            body(GROUPS - 1, True)

        @block.scalar
        def _(act):
            for t in (exped, o_copied):
                act.sem_inc(t.sem, t.per)

            def copy_o(it, q):
                act.wait_ge(pv_done.sem, pv_done.at(it, (q + 1) * KT))
                act.wait_ge(o_stored[q % 2].sem, o_stored[q % 2].at(it, 16 * (q // 2)))
                act.activation(o_sb[q % 2][:], psum[:, O_BANK, :], ACT.Copy).then_inc(o_copied.sem, 1)

            def body(it):
                for q in range(STEPS):
                    for kt in range(KT):
                        n = q * KT + kt
                        act.wait_ge(pv_done.sem, pv_done.at(it, n - PBUF + 1))
                        if (kt - PBUF) % KT in ADDED:
                            step, which = (q if kt >= PBUF else q - 1), ADDED.index((kt - PBUF) % KT)
                            act.wait_ge(adds.sem, adds.at(it, step * ADDS + max(which, 1)))
                        for h in range(GROUP):
                            act.wait_ge(scored.sem, scored.at(it, GROUP * n + h + 1))
                            act.activation(probs[n % PBUF][:, h, :], psum[:, SCORE_BANKS + (GROUP * n + h) % SB, :],
                                           ACT.Exp, scale=SCALE).then_inc(exped.sem, 1)
                        if kt == 0 and q >= 1:
                            copy_o(it, q - 1)
                copy_o(it, STEPS - 1)

            with act.Fori(0, GROUPS - 1) as it:
                body(it)
            body(GROUPS - 1)

        @block.vector
        def _(dve):
            for t in (unit_emptied, inv_made):
                dve.sem_inc(t.sem, t.per)

            def unit(it, q, u):
                it, q = (it, q) if q < STEPS else (it + 1, q - STEPS)
                n, i = q * ALL_UNITS + u, q % 2
                bank = UNIT_BANKS + n % UB
                if u == UNITS:
                    dve.wait_ge(unit_emptied.sem, unit_emptied.at(it, n))
                    dve.tensor_reduce(neg_max[i][:], part_max[i][:], AX.X, ALU.max,
                                      negate=True).then_inc(max_made.sem, 1)
                    dve.wait_ge(unit_filled.sem, unit_filled.at(it, n + 1))
                    dve.tensor_copy(row_hi[i][:], psum[0:GROUP, bank, :]).then_inc(row_steps.sem, 1)
                    dve.wait_ge(row_steps.sem, row_steps.at(it, q + 1))
                    dve.tensor_tensor(row_lo[i][:], psum[0:GROUP, bank, :], row_hi[i][:].bitcast(F32),
                                      ALU.subtract).then_inc(rows_made.sem, 1)
                    dve.wait_ge(rows_made.sem, rows_made.at(it, q + 1))
                    dve.sem_inc(unit_emptied.sem, 1)
                else:
                    dve.wait_ge(unit_filled.sem, unit_filled.at(it, n + 1))
                    dve.tensor_reduce(part_max[i][:, u // CHUNKS, u % CHUNKS:u % CHUNKS + 1], psum[:, bank, :],
                                      AX.X, ALU.max).then_inc(unit_emptied.sem, 1)

            def finish_o(it, q):
                i = q % 2
                dve.wait_ge(l_done.sem, l_done.at(it, q + 1))
                dve.reciprocal(inv[i][:], psum[:, L_BANK, :]).then_inc(inv_made.sem, 1)
                dve.wait_ge(inv_made.sem, inv_made.at(it, q + 1))
                dve.wait_ge(o_copied.sem, o_copied.at(it, q + 1))
                dve.tensor_tensor(o_sb[i][:], o_sb[i][:], inv[i][:], ALU.mult).then_inc(o_made.sem, 1)

            def body(it, last):
                for q in range(STEPS):
                    todo = units_of(q, last)
                    for step, u in todo[:SUMS_AT]:
                        unit(it, step, u)
                    if q >= 1:
                        finish_o(it, q - 1)
                    for step, u in todo[SUMS_AT:]:
                        unit(it, step, u)
                finish_o(it, STEPS - 1)

            for q, u in first_units:
                unit(0, q, u)
            with dve.Fori(0, GROUPS - 1) as it:
                body(it, False)
            body(GROUPS - 1, True)


def context_keys(nc, const, name, ctx_d, wk_d, wv_d, norms, biases, kblk, values):
    ident, ones, minus_half, sp_alone, dve_alone = const
    with ExitStack() as ctx:
        def sb(n, shape, dt=F32):
            return ctx.enter_context(nc.sbuf_tensor(f"{name}_{n}", shape, dt))

        def sem(n):
            return ctx.enter_context(nc.semaphore(f"{name}_{n}"))

        rows = sb("ctx", [CTX, BATCH, D])
        w = [sb("wk", [P, KC, D]), sb("wv", [P, KC, D])]
        xT = [sb("kin_T", [P, KC, BATCH * CTX]), sb("vin_T", [P, KC, BATCH * CTX])]
        y = [sb("kin", [CTX, BATCH, D]), sb("vin", [CTX, BATCH, D])] if norms else [rows, rows]
        gb = [[sb(f"gb{i}{j}", [CTX, D]) for j in range(2)] for i in range(2)] if norms else None
        kbias = sb("kbias", [P, KC]) if biases else None
        vbias = sb("vbias", [CTX, D]) if biases else None
        stats, mv = sb("stats", [CTX, BATCH, 6]), sb("mv", [CTX, BATCH, 2])
        veps, rstd = sb("veps", [CTX, BATCH]), sb("rstd", [CTX, BATCH])
        psum = ctx.enter_context(nc.psum_tensor(f"{name}_psum", [P, BANKS, 512], F32))
        loaded, zeroed, veps_made, rstd_made = sem("loaded"), sem("zeroed"), sem("veps_made"), sem("rstd_made")
        steps, normed, filled, emptied = sem("vector_steps"), sem("normed"), sem("filled"), sem("emptied")
        LOADS = 3 + (4 if norms else 0) + (2 if biases else 0)
        block = ctx.enter_context(nc.Block())

        @block.sync
        def _(sp):
            sp.dma_start(rows[:], ctx_d.rearrange("(b n) d -> n b d", b=BATCH)).then_inc(loaded, 16)
            for i, d in enumerate((wk_d, wv_d)):
                sp.dma_start(w[i][:], d.rearrange("(c p) n -> p c n", p=P)).then_inc(loaded, 16)
            if norms:
                for i in range(2):
                    for j in range(2):
                        load_broadcast(sp, gb[i][j][:], norms[i][j], loaded)
            if biases:
                sp.dma_start(kbias[:], biases[0]).then_inc(loaded, 16)
                load_broadcast(sp, vbias[:], biases[1], loaded)

        @block.gpsimd
        def _(pool):
            pool.memset(kblk[:], 0.0).then_inc(zeroed, 1)
            if norms:
                pool.wait_ge(veps_made, 1)
                pool.tensor_tensor(rstd[:], veps[:], minus_half[0:CTX, 0:BATCH], ALU.pow).then_inc(rstd_made, 1)

        @block.vector
        def _(dve):
            chain = Chain(dve, Tally(steps, 0), 0)
            dve.wait_ge(loaded, 16 * LOADS)
            if norms:
                for b in range(BATCH):
                    chain.link(dve.bn_stats(stats[:, b, :], rows[:, b, :]))
                chain.settle(dve_alone)
                for b in range(BATCH):
                    chain.link(dve.bn_aggr(mv[:, b, :], stats[:, b, :]))
                chain.settle()
                dve.tensor_scalar(veps[:], mv[:, :, 1], EPS, None, ALU.add).then_inc(veps_made, 1)
                for i in range(2):
                    for b in range(BATCH):
                        chain.link(dve.scalar_tensor_tensor(y[i][:, b, :], rows[:, b, :], mv[:, b, 0:1], gb[i][0][:],
                                                            ALU.subtract, ALU.mult))
                chain.settle()
                dve.wait_ge(rstd_made, 1)
                for i in range(2):
                    for b in range(BATCH):
                        dve.scalar_tensor_tensor(y[i][:, b, :], y[i][:, b, :], rstd[:, b:b + 1], gb[i][1][:],
                                                 ALU.mult, ALU.add).then_inc(normed, 1)
            for i in range(2):
                for c in range(KC):
                    dve.wait_ge(filled, i * KC + c + 1)
                    dve.tensor_copy(xT[i][:, c, :], psum[:, i * KC + c, 0:BATCH * CTX]).then_inc(emptied, 1)
            dve.wait_ge(zeroed, 1)
            for c in range(KC):
                dve.wait_ge(filled, 2 * KC + c + 1)
                for h in range(GROUP):
                    r = slice(h * DH, (h + 1) * DH)
                    out = kblk[r, :, c, h * CTX:(h + 1) * CTX]
                    src = psum[r, c, 0:BATCH * CTX].rearrange("p (b n) -> p b n", b=BATCH)
                    if biases:
                        dve.tensor_scalar(out, src, kbias[r, c:c + 1], None, ALU.add).then_inc(emptied, 1)
                    else:
                        dve.tensor_copy(out, src).then_inc(emptied, 1)
            for b in range(BATCH):
                dve.wait_ge(filled, 3 * KC + b + 1)
                src = psum[0:CTX, KC + b, :]
                if biases:
                    dve.tensor_tensor(values[:, b, :], src, vbias[:], ALU.add).then_inc(emptied, 1)
                else:
                    dve.tensor_copy(values[:, b, :], src).then_inc(emptied, 1)
            dve.wait_ge(emptied, 2 * KC + KC * GROUP + BATCH)

        @block.tensor
        def _(pe):
            pe.wait_ge(loaded, 16 * LOADS)
            if norms:
                pe.wait_ge(normed, 2 * BATCH)
            for i in range(2):
                for c in range(KC):
                    for b in range(BATCH):
                        last = pe.transpose(psum[:, i * KC + c, b * CTX:(b + 1) * CTX],
                                            y[i][:, b, c * P:(c + 1) * P], ident[0:CTX, 0:CTX])
                    last.then_inc(filled, 1)
            pe.wait_ge(emptied, 2 * KC)
            for c in range(KC):
                for k in range(KC):
                    last = pe.matmul(psum[:, c, 0:BATCH * CTX], w[0][:, k, c * P:(c + 1) * P], xT[0][:, k, :],
                                     start=(k == 0), stop=(k == KC - 1))
                last.then_inc(filled, 1)
            for b in range(BATCH):
                for k in range(KC):
                    last = pe.matmul(psum[0:CTX, KC + b, :], xT[1][:, k, b * CTX:(b + 1) * CTX], w[1][:, k, :],
                                     start=(k == 0), stop=(k == KC - 1))
                last.then_inc(filled, 1)


def attention_order(first):
    tiles = BATCH * TILES
    places = {}

    def put(slot, place, steps):
        places.setdefault((slot, place), []).extend(steps)

    def steps(kind, ahead, s, which):
        return [(kind, ahead, s, j) for j in which]

    def projected(ahead, s, t):
        return [("out0", ahead, s, t), ("n1", ahead, s, t), ("n2", ahead, s, t)]

    if first:
        for ahead, s, out0, turn, q in ((0, 1, 0, 2, (3, 3)), (1, 0, 5, 7, (8, 9))):
            for t in range(TILES):
                put(out0 + t // 2, t % 2, projected(ahead, s, t))
            for half in range(2):
                put(turn, half, steps("turn", ahead, s, (2 * half, 2 * half + 1)))
                place = half if q[0] == q[1] else 0
                put(q[half], place, steps("q", ahead, s, (2 * half, 2 * half + 1)))
        put(4, 1, [("split", 1, 0, 0)])
        put(9, 1, [("split", 1, 1, 0)])
    else:
        for ahead, s, turn, q in ((0, 1, 1, (2, 3)), (1, 0, 8, (9, 10))):
            for half in range(2):
                put(turn, half, steps("turn", ahead, s, (2 * half, 2 * half + 1)))
                put(q[half], 1, steps("q", ahead, s, (2 * half, 2 * half + 1)))
    order = []
    for i in range(tiles + 3):
        def at(kind, tile, groups=(0,)):
            return [(kind, tile, g) for g in groups] if 0 <= tile < tiles else []

        if not first and i in (2, 2 + TILES):
            order.append(("residual", (i - 2) // TILES, 0))
        order += at("scores", i) + at("soft", i - 1) + at("pT", i - 2, (0, 1)) + places.get((i, 0), [])
        order += at("pT", i - 2, (2, 3)) + at("exp", i) + at("out", i - 3) + places.get((i, 1), [])
        order += at("pv", i - 2)
    return order


def cross_attention(nc, const, name, first, x_d, out_d, oT_d, wo0_d, wq_d, wo_d, vectors, q_bias_d, kblk, values):
    ident, ones, minus_half, sp_alone, dve_alone = const
    GW = GROUP * CTX
    N = BATCH * TILES
    with ExitStack() as ctx:
        def sb(n, shape, dt=F32):
            return ctx.enter_context(nc.sbuf_tensor(f"{name}_{n}", shape, dt))

        def tally(n, per, credit=False):
            return Tally(ctx.enter_context(nc.semaphore(f"{name}_{n}")), per, credit)

        weights = ([("wo0", wo0_d)] if first else []) + [("wq", wq_d), ("wo", wo_d)]
        w = {n: (sb(n + "_hi", [P, KC, D], F32R), sb(n + "_lo", [P, KC, D], F32R)) for n, _ in weights}
        vec = [sb(f"vec{i}", [P, D]) for i in range(len(vectors))]
        q_bias = None if first else sb("q_bias", [P, KC])
        oT = sb("oT", [P, KC, CHUNK]) if first else None
        xin = sb("xin", [P, TILES, D]) if first else None
        x = [sb(f"x{s}", [P, TILES, D]) for s in STREAMS]
        xT = [[sb(f"xT{p}{s}", [P, KC, CHUNK], F32R) for p in ("hi", "lo")] for s in STREAMS]
        qT = [sb(f"qT{s}", [P, KC, CHUNK]) for s in STREAMS]
        probs = [sb(f"probs{i}", [P, HEADS, CTX]) for i in range(3)]
        pT = sb("pT", [CTX, HEADS, P])
        o2T = [[sb(f"o2T{p}{i}", [P, KC, P], F32R) for p in ("hi", "lo")] for i in range(2)]
        y = [sb(f"y{s}", [P, TILES, D]) for s in STREAMS]
        row_max = sb("row_max", [P, HEADS])
        row_sum, row_inv = ([sb(f"{n}{i}", [P, HEADS]) for i in range(2)] for n in ("row_sum", "row_inv"))
        stats, mv = sb("stats", [P, TILES, 6]), sb("mv", [P, TILES, 2])
        veps, rstd = sb("veps", [P, TILES]), sb("rstd", [P, TILES])
        psum = ctx.enter_context(nc.psum_tensor(f"{name}_psum", [P, BANKS, 512], F32))
        RING = 2
        PREP_BANKS, ATT_BANKS, S_BANK = 0, RING, 2 * RING

        split_weights(nc, name, [(d.rearrange("(c p) n -> p c n", p=P), w[n][0][:], w[n][1][:]) for n, d in weights], qT)

        order = attention_order(first)
        prep = [(kind, s, j) for s in STREAMS for kind in (("out0",) if first else ()) + ("turn", "q")
                for j in range(4)]
        att = [e for e in order if e[0] in ("pT", "out", "pv")]
        prep_readers = "".join({"out0": "D", "turn": "D", "q": "A"}[e[0]] for e in prep)
        att_readers = "".join({"out": "D", "pv": "D", "pT": "A"}[e[0]] for e in att)
        prep_filled, att_filled = tally("prep_filled", len(prep)), tally("att_filled", len(att))
        prep_read = {r: tally(f"prep_read_{r}", prep_readers.count(r), True) for r in "DA"}
        att_read = {r: tally(f"att_read_{r}", att_readers.count(r), True) for r in "DA"}
        prep_ring, att_ring = Ring(RING, prep_readers, prep_read), Ring(RING, att_readers, att_read)
        turn_hi, pv_hi = tally("turn_hi", BATCH * KC), tally("pv_hi", N)

        def was_read(it, e):
            events, readers, read = (prep, prep_readers, prep_read) if e in prep else (att, att_readers, att_read)
            n = events.index(e)
            return read[readers[n]].sem, read[readers[n]].at(it, readers[:n + 1].count(readers[n]))

        if first:
            oT_loaded, xin_loaded = tally("oT_loaded", 16 * BATCH), tally("xin_loaded", 16 * BATCH)
            oT_hi, oT_lo = tally("oT_hi", BATCH), tally("oT_lo", BATCH)
            prep_steps = tally("prep_steps", 3 * N)
        else:
            x_loaded = [tally(f"x_loaded{s}", 16) for s in STREAMS]
            residual = tally("residual", BATCH)
        veps_made, rstd_made, normed = tally("veps_made", N), tally("rstd_made", N), tally("normed", N)
        scores_filled = tally("scores_filled", N)
        scores_emptied = tally("scores_emptied", N, True)
        exped, inverted, probs_made = tally("exped", N), tally("inverted", N), tally("probs_made", N)
        att_steps = tally("att_steps", (2 if first else 5) * N)
        stored = [tally(f"stored{s}", 16, True) for s in STREAMS]
        params = ctx.enter_context(nc.semaphore(f"{name}_params"))
        N_PARAMS = len(vectors) + (0 if first else 1)
        block = ctx.enter_context(nc.Block())

        PREPARING = ("split", "out0", "turn", "q")
        start = [("split", 0, s, 0) for s in STREAMS] if first else []
        for kind in ("out0",) if first else ():
            for t in range(TILES):
                start += [("out0", 0, 0, t), ("n1", 0, 0, t), ("n2", 0, 0, t)]
        start += [(kind, 0, 0, j) for kind in ("turn", "q") for j in range(KC)]

        def is_prep(e):
            return e[0] in PREPARING or (first and e[0] in ("n1", "n2"))

        def run(eng, prepare, attend):
            for kind, _, s, j in start:
                prepare(0, kind, s, j)

            def body(it, last):
                for e in order:
                    if is_prep(e):
                        kind, ahead, s, j = e
                        if not (last and ahead):
                            prepare(it + 1 if ahead else it, kind, s, j)
                    else:
                        attend(it, *e)

            with eng.Fori(0, CHUNKS - 1) as it:
                body(it, False)
            body(CHUNKS - 1, True)

        @block.sync
        def _(sp):
            for s in STREAMS:
                sp.sem_inc(stored[s].sem, stored[s].per)
            for v, d in zip(vec, vectors):
                load_broadcast(sp, v[:], d, params)
            if not first:
                sp.dma_start(q_bias[:], q_bias_d).then_inc(params, 16)

            def tokens(it, s):
                return bass.ds(it * CHUNK + s * SEQ, CHUNK)

            def load_oT(it, s, wait=True):
                if wait:
                    sp_alone.wait(sp, oT_lo.sem, oT_lo.at(it, s))
                sp.dma_start(oT[:], oT_d[:, tokens(it, s)].rearrange("(c p) n -> p c n", p=P)).then_inc(oT_loaded.sem, 16)

            def load_xin(it, s, wait=True):
                if wait:
                    sp_alone.wait(sp, *was_read(it - 1 + s, ("out0", 1 - s, TILES - 1)))
                sp.dma_start(xin[:], rows_of(x_d[tokens(it, s), :])).then_inc(xin_loaded.sem, 16)

            def load_x(it, s, wait=True):
                if wait:
                    sp_alone.wait(sp, *was_read(it - 1, ("turn", s, KC - 1)))
                    sp_alone.wait(sp, residual.sem, residual.at(it - 1, s + 1))
                sp.dma_start(x[s][:], rows_of(x_d[tokens(it, s), :])).then_inc(x_loaded[s].sem, 16)

            def store(it, s):
                if first:
                    sp_alone.wait(sp, *was_read(it, ("out", s * TILES + TILES - 1, 0)))
                else:
                    sp_alone.wait(sp, normed.sem, normed.at(it, (s + 1) * TILES))
                sp.dma_start(rows_of(out_d[tokens(it, s), :]), y[s][:]).then_inc(stored[s].sem, 16)

            def body(it, last):
                if first and not last:
                    load_oT(it + 1, 0)
                    load_xin(it + 1, 0)
                    load_oT(it + 1, 1)
                if not first and not last:
                    load_x(it + 1, 0)
                store(it, 0)
                if not last:
                    load_xin(it + 1, 1) if first else load_x(it + 1, 1)
                store(it, 1)

            for s in STREAMS:
                if first:
                    load_oT(0, s, s > 0)
                    load_xin(0, s, s > 0)
                else:
                    load_x(0, s, False)
            with sp.Fori(0, CHUNKS - 1) as it:
                body(it, False)
            body(CHUNKS - 1, True)
            for s in STREAMS:
                sp_alone.wait(sp, stored[s].sem, stored[s].at(CHUNKS, 0))

        @block.gpsimd
        def _(pool):
            def inverse_root(it, n, t):
                pool.wait_ge(veps_made.sem, veps_made.at(it, n + 1))
                pool.tensor_tensor(rstd[:, t:t + 1], veps[:, t:t + 1], minus_half[:, 0:1], ALU.pow).then_inc(
                    rstd_made.sem, 1)

            def prepare(it, kind, s, j):
                if kind == "n1":
                    inverse_root(it, s * TILES + j, j)

            def attend(it, kind, i, g):
                if kind == "soft":
                    pool.wait_ge(inverted.sem, inverted.at(it, i + 1))
                    pool.tensor_tensor(probs[i % 3][:], probs[i % 3][:],
                                       row_inv[i % 2][:].unsqueeze(2).to_broadcast([P, HEADS, CTX]),
                                       ALU.mult).then_inc(probs_made.sem, 1)
                elif kind == "residual":
                    pool.wait_ge(x_loaded[i].sem, x_loaded[i].at(it, 16))
                    pool.wait_ge(stored[i].sem, stored[i].at(it, 0))
                    pool.tensor_tensor(y[i][:], x[i][:], vec[2][:].unsqueeze(1).to_broadcast([P, TILES, D]),
                                       ALU.add).then_inc(residual.sem, 1)
                elif kind == "out" and not first:
                    inverse_root(it, i, i % TILES)

            if not first:
                pool.wait_ge(params, 16 * N_PARAMS)
            run(pool, prepare, attend)

        @block.tensor
        def _(pe):
            def prepare(it, kind, s, j):
                if kind not in ("out0", "turn", "q"):
                    return
                n = prep.index((kind, s, j))
                bank = psum[:, PREP_BANKS + prep_ring.bank(n), :]
                if j == 0:
                    if kind == "out0":
                        pe.wait_ge(oT_lo.sem, oT_lo.at(it, s + 1))
                    elif kind == "q":
                        pe.wait_ge(*was_read(it, ("turn", s, KC - 1)))
                    elif first:
                        pe.wait_ge(normed.sem, normed.at(it, (s + 1) * TILES))
                    else:
                        pe.wait_ge(x_loaded[s].sem, x_loaded[s].at(it, 16))
                pe.wait_ge(*prep_ring.free(it, n))
                if kind == "out0":
                    last = split_product(pe, bank, [
                        ((xT[s][0][:, k, j * P:(j + 1) * P], xT[s][1][:, k, j * P:(j + 1) * P]),
                         (w["wo0"][0][:, k, :], w["wo0"][1][:, k, :])) for k in range(KC)])
                elif kind == "turn":
                    last = transposes(pe, bank, x[s], j, ident[:])
                else:
                    last = split_product(pe, bank, [
                        ((w["wq"][0][:, k, j * P:(j + 1) * P], w["wq"][1][:, k, j * P:(j + 1) * P]),
                         (xT[s][0][:, k, :], xT[s][1][:, k, :])) for k in range(KC)])
                last.then_inc(prep_filled.sem, 1)

            def attend(it, kind, i, g):
                s, t = divmod(i, TILES)
                if kind == "scores":
                    if t == 0:
                        pe.wait_ge(*was_read(it, ("q", s, KC - 1)))
                    pe.wait_ge(scores_emptied.sem, scores_emptied.at(it, i))
                    for c in range(KC):
                        last = pe.matmul(psum[:, S_BANK + c, 0:GW], qT[s][:, c, t * P:(t + 1) * P],
                                         kblk[:, s, c, :], start=True, stop=True)
                    last.then_inc(scores_filled.sem, 1)
                if kind not in ("pT", "out", "pv"):
                    return
                n = att.index((kind, i, g))
                bank = psum[:, ATT_BANKS + att_ring.bank(n), :]
                pe.wait_ge(*att_ring.free(it, n))
                if kind == "pT":
                    if g == 0:
                        pe.wait_ge(probs_made.sem, probs_made.at(it, i + 1))
                    for h in range(GROUP):
                        last = pe.transpose(bank[0:CTX, h * P:(h + 1) * P], probs[i % 3][:, g * GROUP + h, :], ident[:])
                elif kind == "pv":
                    pe.wait_ge(*was_read(it, ("pT", i, KC - 1)))
                    for c in range(KC):
                        for h in range(GROUP):
                            last = pe.matmul(bank[h * DH:(h + 1) * DH, c * P:(c + 1) * P],
                                             values[:, s, (c * GROUP + h) * DH:(c * GROUP + h + 1) * DH],
                                             pT[:, c * GROUP + h, :], start=True, stop=True)
                else:
                    pe.wait_ge(*was_read(it, ("pv", i, 0)))
                    hi, lo = o2T[i % 2]
                    last = split_product(pe, bank, [
                        ((hi[:, k, :], lo[:, k, :]), (w["wo"][0][:, k, :], w["wo"][1][:, k, :])) for k in range(KC)])
                last.then_inc(att_filled.sem, 1)

            run(pe, prepare, attend)

        @block.scalar
        def _(act):
            def prepare(it, kind, s, j):
                if kind == "split":
                    act.wait_ge(oT_loaded.sem, oT_loaded.at(it, 16 * (s + 1)))
                    act.activation(xT[s][0][:], oT[:], ACT.Copy).then_inc(oT_hi.sem, 1)
                if kind not in ("turn", "q"):
                    return
                n = prep.index((kind, s, j))
                bank = psum[:, PREP_BANKS + prep_ring.bank(n), :]
                act.wait_ge(prep_filled.sem, prep_filled.at(it, n + 1))
                if kind == "turn":
                    act.activation(xT[s][0][:, j, :], bank, ACT.Copy).then_inc(turn_hi.sem, 1)
                elif first:
                    act.activation(qT[s][:, j, :], bank, ACT.Copy).then_inc(prep_read["A"].sem, 1)
                else:
                    act.activation(qT[s][:, j, :], bank, ACT.Identity, bias=q_bias[:, j:j + 1]).then_inc(
                        prep_read["A"].sem, 1)

            def attend(it, kind, i, g):
                if kind == "exp":
                    act.wait_ge(scores_emptied.sem, scores_emptied.at(it, i + 1))
                    act.activation(probs[i % 3][:], probs[i % 3][:], ACT.Exp, scale=SCALE).then_inc(exped.sem, 1)
                if kind not in ("pT", "pv"):
                    return
                n = att.index((kind, i, g))
                bank = psum[:, ATT_BANKS + att_ring.bank(n), :]
                act.wait_ge(att_filled.sem, att_filled.at(it, n + 1))
                if kind == "pT":
                    act.activation(pT[:, g * GROUP:(g + 1) * GROUP, :].rearrange("p h n -> p (h n)"),
                                   bank[0:CTX, :], ACT.Copy).then_inc(att_read["A"].sem, 1)
                else:
                    act.activation(o2T[i % 2][0][:].rearrange("p c n -> p (c n)"), bank,
                                   ACT.Copy).then_inc(pv_hi.sem, 1)

            for t in (prep_read["A"], att_read["A"]):
                act.sem_inc(t.sem, t.per)
            act.wait_ge(params, 16 * N_PARAMS)
            run(act, prepare, attend)

        @block.vector
        def _(dve):
            for t in (prep_read["D"], att_read["D"], scores_emptied):
                dve.sem_inc(t.sem, t.per)
            dve.wait_ge(params, 16 * N_PARAMS)

            def norm_begin(chain, a, t):
                chain.link(dve.bn_stats(stats[:, t, :], a))
                chain.settle(dve_alone)
                chain.link(dve.bn_aggr(mv[:, t, :], stats[:, t, :]))
                chain.settle()
                dve.tensor_scalar(veps[:, t:t + 1], mv[:, t, 1:2], EPS, None, ALU.add).then_inc(veps_made.sem, 1)
                chain.link(dve.scalar_tensor_tensor(a, a, mv[:, t, 0:1], vec[0][:], ALU.subtract, ALU.mult))

            def norm_end(chain, it, n, a, t):
                chain.settle()
                dve.wait_ge(rstd_made.sem, rstd_made.at(it, n + 1))
                dve.scalar_tensor_tensor(a, a, rstd[:, t:t + 1], vec[1][:], ALU.mult, ALU.add).then_inc(normed.sem, 1)

            def prepare(it, kind, s, j):
                tile = x[s][:, j, :]
                if kind == "split":
                    dve.wait_ge(oT_hi.sem, oT_hi.at(it, s + 1))
                    dve.tensor_tensor(xT[s][1][:], oT[:], xT[s][0][:].bitcast(F32), ALU.subtract).then_inc(oT_lo.sem, 1)
                elif kind in ("n1", "n2"):
                    chain = Chain(dve, prep_steps, it)
                    chain.n = 3 * (s * TILES + j) + (3 if kind == "n2" else 0)
                    if kind == "n1":
                        dve.wait_ge(*was_read(it, ("out0", s, j)))
                        norm_begin(chain, tile, j)
                    else:
                        norm_end(chain, it, s * TILES + j, tile, j)
                if kind not in ("out0", "turn"):
                    return
                n = prep.index((kind, s, j))
                bank = psum[:, PREP_BANKS + prep_ring.bank(n), :]
                if kind == "out0":
                    if j == 0:
                        dve.wait_ge(xin_loaded.sem, xin_loaded.at(it, 16 * (s + 1)))
                    dve.wait_ge(*was_read(it - 1, ("out", s * TILES + j, 0)))
                    dve.wait_ge(prep_filled.sem, prep_filled.at(it, n + 1))
                    dve.tensor_tensor(tile, bank, xin[:, j, :], ALU.add).then_inc(prep_read["D"].sem, 1)
                else:
                    dve.wait_ge(turn_hi.sem, turn_hi.at(it, s * KC + j + 1))
                    dve.tensor_tensor(xT[s][1][:, j, :], bank, xT[s][0][:, j, :].bitcast(F32),
                                      ALU.subtract).then_inc(prep_read["D"].sem, 1)

            chains = {}

            def attend(it, kind, i, g):
                s, t = divmod(i, TILES)
                if kind == "scores" and i == 0:
                    chains["att"] = Chain(dve, att_steps, it)
                chain = chains.get("att")
                if kind == "scores":
                    dve.wait_ge(scores_filled.sem, scores_filled.at(it, i + 1))
                    scores = psum[:, S_BANK:S_BANK + KC, 0:GW].rearrange("p g (h n) -> p g h n", h=GROUP)
                    by_head = row_max[:].rearrange("p (g h) -> p g h", g=KC)
                    chain.link(dve.tensor_reduce(by_head, scores, AX.X, ALU.max))
                    chain.settle()
                    dve.tensor_tensor(probs[i % 3][:].rearrange("p (g h) n -> p g h n", g=KC), scores,
                                      by_head.unsqueeze(3).to_broadcast([P, KC, GROUP, CTX]),
                                      ALU.subtract).then_inc(scores_emptied.sem, 1)
                elif kind == "soft":
                    dve.wait_ge(exped.sem, exped.at(it, i + 1))
                    chain.link(dve.tensor_reduce(row_sum[i % 2][:], probs[i % 3][:], AX.X, ALU.add))
                    chain.settle()
                    dve.reciprocal(row_inv[i % 2][:], row_sum[i % 2][:]).then_inc(inverted.sem, 1)
                elif kind == "pv":
                    n = att.index((kind, i, g))
                    dve.wait_ge(pv_hi.sem, pv_hi.at(it, i + 1))
                    hi, lo = (a[:].rearrange("p c n -> p (c n)") for a in o2T[i % 2])
                    dve.tensor_tensor(lo, psum[:, ATT_BANKS + att_ring.bank(n), :], hi.bitcast(F32),
                                      ALU.subtract).then_inc(att_read["D"].sem, 1)
                elif kind == "out":
                    n, tile = att.index((kind, i, g)), y[s][:, t, :]
                    if t == 0:
                        if first:
                            dve.wait_ge(stored[s].sem, stored[s].at(it, 0))
                        else:
                            dve.wait_ge(residual.sem, residual.at(it, s + 1))
                    dve.wait_ge(att_filled.sem, att_filled.at(it, n + 1))
                    dve.tensor_tensor(tile, psum[:, ATT_BANKS + att_ring.bank(n), :], x[s][:, t, :] if first else tile,
                                      ALU.add).then_inc(att_read["D"].sem, 1)
                    if not first:
                        dve.wait_ge(*was_read(it, (kind, i, g)))
                        norm_begin(chain, tile, t)
                        norm_end(chain, it, i, tile, t)
                    if i == N - 1:
                        chain.end()

            run(dve, prepare, attend)


def mlp(nc, const, x_d, out_d, w1_d, w2_d, b1_d, b2_d, gain_d, bias_d):
    ident, ones, minus_half, sp_alone, dve_alone = const
    PART = 2
    PARTS = DFF // P // PART
    RING, ACC = 4, 4
    SLOTS = range(2)
    N = BATCH * CHUNKS // 2
    with ExitStack() as ctx:
        def sb(n, shape, dt=F32):
            return ctx.enter_context(nc.sbuf_tensor(f"m_{n}", shape, dt))

        def tally(n, per, credit=False, ahead=0):
            return Tally(ctx.enter_context(nc.semaphore(f"m_{n}")), per, credit, ahead)

        w1 = [sb(f"w1_{p}", [P, KC, DFF], F32R) for p in ("hi", "lo")]
        w2 = [sb(f"w2_{p}", [P, DFF // P, D], F32R) for p in ("hi", "lo")]
        gain, bias, b2 = sb("gain", [P, D]), sb("bias", [P, D]), sb("b2", [P, D])
        b1 = sb("b1", [P, DFF // P])
        x = [sb(f"x{s}", [P, TILES, D]) for s in SLOTS]
        h = sb("h", [P, TILES, D])
        hT = [sb(f"hT_{p}", [P, KC, CHUNK], F32R) for p in ("hi", "lo")]
        relu = [sb(f"relu{i}", [P, CHUNK]) for i in range(2)]
        hidden = [[sb(f"hidden_{p}{i}", [P, PART, CHUNK], F32R) for p in ("hi", "lo")] for i in range(2)]
        stats, mv = sb("stats", [P, TILES, 6]), sb("mv", [P, TILES, 2])
        veps, rstd = sb("veps", [P, TILES]), sb("rstd", [P, TILES])
        psum = ctx.enter_context(nc.psum_tensor("m_psum", [P, BANKS, 512], F32))

        jobs = [(w1_d[k * P:(k + 1) * P, :], w1[0][:, k, :], w1[1][:, k, :]) for k in range(KC)]
        raw = [x[0][:].rearrange("p t n -> p (t n)"), x[1][:].rearrange("p t n -> p (t n)")]
        split_weights(nc, "m1", jobs, raw)
        jobs = [(w2_d[k * 4 * P:(k + 1) * 4 * P, :].rearrange("(c p) n -> p c n", p=P),
                 w2[0][:, 4 * k:4 * k + 4, :], w2[1][:, 4 * k:4 * k + 4, :]) for k in range(KC)]
        split_weights(nc, "m2", jobs, x)

        MADE = PARTS * PART
        EVENTS = MADE + KC
        d_emptied = tally("vector_emptied", 2 * KC, True, KC)
        a_emptied = tally("scalar_emptied", 2 * MADE, True)
        ring = Ring(RING, ("A" * MADE + "D" * KC) * 2, {"D": d_emptied, "A": a_emptied})
        filled = tally("filled", 2 * EVENTS, ahead=KC)
        hi_made = tally("hT_hi_made", 2 * KC, ahead=KC)
        hidden_made = tally("hidden_made", 2 * MADE, True)
        split = tally("hidden_hi_made", 2 * MADE)
        part_used = tally("part_used", 2 * PARTS, True)
        out_emptied = tally("out_emptied", 2 * TILES, True)
        loaded = [tally(f"loaded{s}", 16) for s in SLOTS]
        stored = [tally(f"stored{s}", 16, True) for s in SLOTS]
        steps = tally("vector_steps", 2 * LN_STEPS, ahead=LN_STEPS)
        veps_made, rstd_made = tally("veps_made", 2, ahead=1), tally("rstd_made", 2, ahead=1)
        h_made = tally("h_made", 2, ahead=1)
        x_read = tally("x_read", 2, ahead=1)
        b2_added = tally("b2_added", 2, ahead=1)
        params = ctx.enter_context(nc.semaphore("m_params"))
        block = ctx.enter_context(nc.Block())

        def event(s, j):
            return s * EVENTS + j

        @block.sync
        def _(sp):
            for s in SLOTS:
                sp.sem_inc(stored[s].sem, stored[s].given)
            for v, d in ((gain, gain_d), (bias, bias_d), (b2, b2_d)):
                load_broadcast(sp, v[:], d, params)
            sp.dma_start(b1[:], b1_d).then_inc(params, 16)

            def load(it, s):
                sp_alone.wait(sp, stored[s].sem, stored[s].at(it, 0))
                sp.dma_start(x[s][:], rows_of(x_d[bass.ds(it * (2 * CHUNK) + s * CHUNK, CHUNK), :])).then_inc(
                    loaded[s].sem, 16)

            def body(it, last):
                for s in SLOTS:
                    if s == 0:
                        load(it, 1)
                    elif not last:
                        load(it + 1, 0)
                    sp_alone.wait(sp, out_emptied.sem, out_emptied.at(it, (s + 1) * TILES))
                    sp.dma_start(rows_of(out_d[bass.ds(it * (2 * CHUNK) + s * CHUNK, CHUNK), :]), x[s][:]).then_inc(
                        stored[s].sem, 16)

            load(0, 0)
            with sp.Fori(0, N - 1) as it:
                body(it, False)
            body(N - 1, True)
            for s in SLOTS:
                sp_alone.wait(sp, stored[s].sem, stored[s].at(N, 0))

        @block.gpsimd
        def _(pool):
            pool.wait_ge(params, 64)

            def norm(it, s, k):
                pool.wait_ge(veps_made.sem, veps_made.at(it, k))
                pool.tensor_tensor(rstd[:], veps[:], minus_half[:], ALU.pow).then_inc(rstd_made.sem, 1)
                pool.wait_ge(x_read.sem, x_read.at(it, k))
                pool.tensor_tensor(x[s][:], x[s][:], b2[:].unsqueeze(1).to_broadcast([P, TILES, D]),
                                   ALU.add).then_inc(b2_added.sem, 1)

            norm(0, 0, 0)
            with pool.Fori(0, N - 1) as it:
                for s in SLOTS:
                    norm(it, 1 - s, s + 1)
            norm(N - 1, 1, 1)

        @block.tensor
        def _(pe):
            def turn(it, s, j0):
                pe.wait_ge(h_made.sem, h_made.at(it, s + 1))
                for c in range(KC):
                    if j0 is not None:
                        pe.wait_ge(*ring.free(it, j0 + c))
                    transposes(pe, psum[:, ring.bank((j0 or 0) + c), :], h, c, ident[:]).then_inc(filled.sem, 1)

            def up(it, s, part):
                for m in range(PART):
                    j = part * PART + m
                    e = event(s, j)
                    pe.wait_ge(*ring.free(it, e))
                    split_product(pe, psum[:, ring.bank(e), :], [
                        ((w1[0][:, k, j * P:(j + 1) * P], w1[1][:, k, j * P:(j + 1) * P]),
                         (hT[0][:, k, :], hT[1][:, k, :])) for k in range(KC)]).then_inc(filled.sem, 1)

            def down(it, s, part):
                hi, lo = hidden[part % 2]
                if part == 0:
                    pe.wait_ge(out_emptied.sem, out_emptied.at(it, s * TILES))
                pe.wait_ge(hidden_made.sem, hidden_made.at(it, s * MADE + (part + 1) * PART))
                for t in range(TILES):
                    out = psum[:, ACC + t, :]
                    for m in range(PART):
                        k = part * PART + m
                        ah, al = hi[:, m, t * P:(t + 1) * P], lo[:, m, t * P:(t + 1) * P]
                        pe.matmul(out, ah, w2[0][:, k, :], start=(k == 0), stop=False)
                        pe.matmul(out, ah, w2[1][:, k, :], start=False, stop=False)
                        last = pe.matmul(out, al, w2[0][:, k, :], start=False, stop=(k == DFF // P - 1))
                last.then_inc(part_used.sem, 1)

            def body(it, last):
                for s in SLOTS:
                    pe.wait_ge(d_emptied.sem, d_emptied.at(it, s * KC))
                    up(it, s, 0)
                    for part in range(1, PARTS):
                        up(it, s, part)
                        down(it, s, part - 1)
                    if s == 0 or not last:
                        turn(it, s, event(s, MADE))
                    down(it, s, PARTS - 1)

            turn(0, -1, None)
            with pe.Fori(0, N - 1) as it:
                body(it, False)
            body(N - 1, True)

        @block.scalar
        def _(act):
            act.sem_inc(a_emptied.sem, a_emptied.given)
            act.wait_ge(params, 64)

            def turn(it, s, j0):
                for c in range(KC):
                    act.wait_ge(filled.sem, filled.at(it, j0 + c + 1))
                    act.activation(hT[0][:, c, :], psum[:, ring.bank(j0 + c), :], ACT.Copy).then_inc(hi_made.sem, 1)

            def body(it, last):
                for s in SLOTS:
                    for j in range(MADE):
                        e, n = event(s, j), s * MADE + j
                        act.wait_ge(filled.sem, filled.at(it, e + 1))
                        act.wait_ge(hidden_made.sem, hidden_made.at(it, n - 1))
                        act.activation(relu[j % 2][:], psum[:, ring.bank(e), :], ACT.Relu,
                                       bias=b1[:, j:j + 1]).then_inc(a_emptied.sem, 1)
                    if s == 0 or not last:
                        turn(it, s, event(s, MADE))

            turn(0, -1, -KC)
            with act.Fori(0, N - 1) as it:
                body(it, False)
            body(N - 1, True)

        @block.vector
        def _(dve):
            for t in (d_emptied, hidden_made, part_used, out_emptied):
                dve.sem_inc(t.sem, t.given)
            dve.wait_ge(params, 64)

            def norm(it, s, k, chain):
                x_ = x[s]
                dve.wait_ge(loaded[s].sem, loaded[s].at(it + 1 if k == 2 else it, 16))
                for t in range(TILES):
                    chain.link(dve.bn_stats(stats[:, t, :], x_[:, t, :]))
                chain.settle(dve_alone)
                for t in range(TILES):
                    chain.link(dve.bn_aggr(mv[:, t, :], stats[:, t, :]))
                chain.settle()
                dve.tensor_scalar(veps[:], mv[:, :, 1], EPS, None, ALU.add).then_inc(veps_made.sem, 1)
                for t in range(TILES):
                    last = chain.link(dve.scalar_tensor_tensor(h[:, t, :], x_[:, t, :], mv[:, t, 0:1], gain[:],
                                                               ALU.subtract, ALU.mult))
                chain.settle()
                dve.sem_inc(x_read.sem, 1)
                dve.wait_ge(rstd_made.sem, rstd_made.at(it, k))
                for t in range(TILES):
                    last = dve.scalar_tensor_tensor(h[:, t, :], h[:, t, :], rstd[:, t:t + 1], bias[:],
                                                    ALU.mult, ALU.add)
                last.then_inc(h_made.sem, 1)

            def turn(it, s, j0):
                for c in range(KC):
                    dve.wait_ge(hi_made.sem, hi_made.at(it, s * KC + c + 1))
                    dve.tensor_tensor(hT[1][:, c, :], psum[:, ring.bank(j0 + c), :], hT[0][:, c, :].bitcast(F32),
                                      ALU.subtract).then_inc(d_emptied.sem, 1)

            def body(it, last):
                chain = Chain(dve, steps, it)
                for s in SLOTS:
                    for j in range(MADE):
                        n, (part, m) = s * MADE + j, divmod(j, PART)
                        if j == MADE // 2 and (s == 0 or not last):
                            norm(it, 1 - s, s + 1, chain)
                        dve.wait_ge(a_emptied.sem, a_emptied.at(it, n + 1))
                        dve.wait_ge(part_used.sem, part_used.at(it, s * PARTS + part - 1))
                        hi, lo = (a[:, m, :] for a in hidden[part % 2])
                        dve.tensor_copy(hi, relu[j % 2][:]).then_inc(split.sem, 1)
                        dve.wait_ge(split.sem, split.at(it, n + 1))
                        dve.tensor_tensor(lo, relu[j % 2][:], hi.bitcast(F32), ALU.subtract).then_inc(hidden_made.sem, 1)
                    if s == 0 or not last:
                        turn(it, s, event(s, MADE))
                    dve.wait_ge(part_used.sem, part_used.at(it, (s + 1) * PARTS))
                    dve.wait_ge(b2_added.sem, b2_added.at(it, s))
                    for t in range(TILES):
                        dve.tensor_tensor(x[s][:, t, :], psum[:, ACC + t, :], x[s][:, t, :], ALU.add).then_inc(
                            out_emptied.sem, 1)

            norm(0, 0, 0, Chain(dve, Tally(steps.sem, 0), 0))
            turn(0, -1, -KC)
            with dve.Fori(0, N - 1) as it:
                body(it, False)
            body(N - 1, True)


def two_layers(nc, t, out):
    x, context = t["x"], t["ctx_1024"]
    with ExitStack() as ctx:
        def dram(name, shape):
            return nc.dram_tensor(name, shape, F32, kind="Internal").ap()

        tokens = BATCH * SEQ
        xn, v = dram("xn_scratch", [tokens, D]), dram("v_scratch", [tokens, D])
        q_hi, q_lo, k_hi, k_lo, oT = (dram(n + "_scratch", [D, tokens]) for n in ("q_hi", "q_lo", "k_hi", "k_lo", "oT"))
        after_cross, after_mlp = dram("cross_scratch", [tokens, D]), dram("mlp_scratch", [tokens, D])
        const = make_constants(nc, ctx)
        scratch = (xn, q_hi, q_lo, k_hi, k_lo, v)
        project_qkv(nc, const, x, t["sa_wqT"], t["sa_wkT"], t["sa_wvT"], t["g_sa"], t["b_sa"], scratch)
        self_attention(nc, const, scratch, oT)
        with ExitStack() as held:
            kblk = held.enter_context(nc.sbuf_tensor("kblk0", [P, BATCH, KC, GROUP * CTX], F32))
            values = held.enter_context(nc.sbuf_tensor("values0", [CTX, BATCH, D], F32))
            context_keys(nc, const, "c", context, t["ca_wkT"], t["ca_wvT"],
                         ((t["g_kca"], t["b_kca"]), (t["g_vca"], t["b_vca"])), None, kblk, values)
            cross_attention(nc, const, "d", True, xn, after_cross, oT, t["sa_woT"], t["ca_wqT"], t["ca_woT"],
                            (t["g_qca"], t["b_qca"]), None, kblk, values)
        mlp(nc, const, after_cross, after_mlp, t["w1T"], t["w2T"], t["b1"], t["b2"], t["g_out"], t["b_out"])
        with ExitStack() as held:
            kblk = held.enter_context(nc.sbuf_tensor("kblk1", [P, BATCH, KC, GROUP * CTX], F32))
            values = held.enter_context(nc.sbuf_tensor("values1", [CTX, BATCH, D], F32))
            context_keys(nc, const, "f", context, t["l1_wkT"], t["l1_wvT"], None, (t["l1_bk"], t["l1_bv"]), kblk, values)
            cross_attention(nc, const, "g", False, after_mlp, out, None, None, t["l1_wqT"], t["l1_woT"],
                            (t["l1_gain"], t["l1_bias"], t["l1_bo"]), t["l1_bq"], kblk, values)


def kernel(**inputs):
    import numpy as np
    import concourse.bacc as bacc
    from concourse.bass_utils import run_bass_kernel_spmd

    def turned(a):
        return np.ascontiguousarray(np.asarray(a).T)

    def by_partition(a):
        return np.ascontiguousarray(np.asarray(a).reshape(-1, P).T)

    a0 = {k[len("L0_xattn_"):]: np.asarray(v) for k, v in inputs.items() if k.startswith("L0_xattn_")}
    a1 = {k[len("L1_xattn_"):]: np.asarray(v) for k, v in inputs.items() if k.startswith("L1_xattn_")}
    arrays = {
        "x": np.ascontiguousarray(np.asarray(inputs["x"]).reshape(BATCH * SEQ, D)),
        "ctx_1024": np.ascontiguousarray(np.asarray(inputs["ctx_1024"]).reshape(BATCH * CTX, D)),
    }
    for n in ("sa_wq", "sa_wk", "sa_wv", "sa_wo", "ca_wq", "ca_wk", "ca_wv", "ca_wo"):
        arrays[n + "T"] = turned(a0[n])
    for n in ("g_sa", "b_sa", "g_qca", "b_qca", "g_kca", "b_kca", "g_vca", "b_vca", "g_out", "b_out"):
        arrays[n] = np.ascontiguousarray(a0[n])
    arrays["w1T"], arrays["w2T"] = turned(a0["ffn_w1"]), turned(a0["ffn_w2"])
    arrays["b1"], arrays["b2"] = by_partition(a0["ffn_b1"]), np.ascontiguousarray(a0["ffn_b2"])
    for i, n in enumerate(("wq", "wk", "wv")):
        arrays[f"l1_{n}T"] = turned(a1["W_qkv"][i * D:(i + 1) * D])
    arrays["l1_woT"] = turned(a1["W_o"])
    arrays["l1_bq"] = by_partition(a1["b_qkv"][0:D])
    arrays["l1_bk"] = by_partition(a1["b_qkv"][D:2 * D])
    arrays["l1_bv"] = np.ascontiguousarray(a1["b_qkv"][2 * D:3 * D])
    arrays["l1_bo"] = np.ascontiguousarray(a1["b_o"])
    arrays["l1_gain"], arrays["l1_bias"] = np.ascontiguousarray(a1["ln_gamma"]), np.ascontiguousarray(a1["ln_beta"])

    nc = bacc.Bacc("TRN2", target_bir_lowering=False, num_devices=1)
    handles = {n: nc.dram_tensor(n, a.shape, mybir.dt.from_np(a.dtype), kind="ExternalInput").ap()
               for n, a in arrays.items()}
    out = nc.dram_tensor("out", [BATCH * SEQ, D], F32, kind="ExternalOutput").ap()
    two_layers(nc, handles, out)
    result = run_bass_kernel_spmd(nc, [arrays], core_ids=[0]).results[0]["out"]
    return np.asarray(result).reshape(BATCH, SEQ, D)
```

```python
from contextlib import ExitStack

import concourse.bass as bass
from concourse import mybir

F32 = mybir.dt.float32
F32R = mybir.dt.float32r
ALU = mybir.AluOpType
ACT = mybir.ActivationFunctionType
AX = mybir.AxisListType

P = 128
BATCH, SEQ, D = 2, 2048, 512
CTX = 77
HEADS, DH = 16, 32
DFF = 4 * D
KC = D // P
GROUP = P // DH
CHUNK = 512
TILES = CHUNK // P
CHUNKS = SEQ // CHUNK
KT = SEQ // P
BANKS = 8
EPS = 1e-5
SCALE = float(DH) ** -0.5
STREAMS = range(BATCH)


class Tally:

    def __init__(self, sem, per, credit=False, ahead=0):
        self.sem, self.per, self.start = sem, per, per if credit else ahead
        self.given = per - ahead if credit else 0

    def at(self, it, k):
        return it * self.per + (k + self.start)


class Chain:

    def __init__(self, eng, tally, it):
        self.eng, self.tally, self.it, self.n = eng, tally, it, 0

    def link(self, ins):
        self.n += 1
        return ins.then_inc(self.tally.sem, 1)

    def settle(self, alone=None):
        value = self.tally.at(self.it, self.n)
        if alone:
            alone.wait(self.eng, self.tally.sem, value)
        else:
            self.eng.wait_ge(self.tally.sem, value)

    def end(self):
        assert self.n == self.tally.per, (self.n, self.tally.per)


class Alone:

    def __init__(self, sem):
        self.sem = sem

    def wait(self, eng, sem, value):
        eng.wait_ge(sem, value)
        eng.sem_inc(self.sem, 1)


class Ring:

    def __init__(self, banks, readers, tallies):
        self.banks, self.readers, self.tallies = banks, readers, tallies
        assert len(readers) % banks == 0
        for r, t in tallies.items():
            assert t.per == readers.count(r), (r, t.per, readers.count(r))

    def bank(self, e):
        return e % self.banks

    def free(self, it, e):
        back = e - self.banks
        r = self.readers[back]
        n = self.readers[:back % len(self.readers)].count(r) + 1 - (self.tallies[r].per if back < 0 else 0)
        return self.tallies[r].sem, self.tallies[r].at(it, n)


def split_product(pe, out, pairs):
    n = len(pairs)
    for i, ((ah, al), (bh, bl)) in enumerate(pairs):
        pe.matmul(out, ah, bh, start=(i == 0), stop=False)
        pe.matmul(out, ah, bl, start=False, stop=False)
        last = pe.matmul(out, al, bh, start=False, stop=(i == n - 1))
    return last


def transposes(pe, bank, src, kc, ident):
    for t in range(TILES):
        last = pe.transpose(bank[:, t * P:(t + 1) * P], src[:, t, kc * P:(kc + 1) * P], ident)
    return last


LN_STEPS = 3 * TILES


def make_constants(nc, ctx):
    ident = ctx.enter_context(nc.sbuf_tensor("ident", [P, P], F32))
    ones = ctx.enter_context(nc.sbuf_tensor("ones", [P, DH], F32))
    minus_half = ctx.enter_context(nc.sbuf_tensor("minus_half", [P, TILES], F32))
    made = ctx.enter_context(nc.semaphore("constants_made"))
    with nc.Block() as block:
        @block.gpsimd
        def _(pool):
            pool.memset(ones[:], 1.0).then_inc(made, 1)
            pool.memset(minus_half[:], -0.5).then_inc(made, 1)
            pool.memset(ident[:], 0.0).then_inc(made, 1)
            pool.wait_ge(made, 3)
            pool.affine_select(out=ident[:], in_=ident[:], compare_op=ALU.not_equal, fill=1.0, base=0,
                               pattern=[[-1, P]], channel_multiplier=1).then_inc(made, 1)
            pool.wait_ge(made, 4)
    sp_alone = Alone(ctx.enter_context(nc.semaphore("sync_waits")))
    dve_alone = Alone(ctx.enter_context(nc.semaphore("vector_waits")))
    return ident, ones, minus_half, sp_alone, dve_alone


class Weights:

    def __init__(self, nc, ctx, name, jobs, raws):
        self.jobs, self.raws = jobs, raws
        self.loaded = [ctx.enter_context(nc.semaphore(f"{name}_w_loaded{i}")) for i in range(len(raws))]
        self.hi_made = ctx.enter_context(nc.semaphore(f"{name}_w_hi"))
        self.lo_made = ctx.enter_context(nc.semaphore(f"{name}_w_lo"))

    def load(self, sp, which=None):
        for n in which or range(len(self.jobs)):
            src, raw, hi, lo = self.jobs[n]
            before = [m for m in range(n) if self.jobs[m][1] == raw]
            if before:
                sp.wait_ge(self.lo_made, before[-1] + 1)
            sp.dma_start(self.raws[raw], src).then_inc(self.loaded[raw], 16)

    def make_hi(self, act, n):
        src, raw, hi, lo = self.jobs[n]
        act.wait_ge(self.loaded[raw], 16 * sum(job[1] == raw for job in self.jobs[:n + 1]))
        act.activation(hi, self.raws[raw], ACT.Copy).then_inc(self.hi_made, 1)

    def make_lo(self, dve, n):
        src, raw, hi, lo = self.jobs[n]
        dve.wait_ge(self.hi_made, n + 1)
        dve.tensor_tensor(lo, self.raws[raw], hi.bitcast(F32), ALU.subtract).then_inc(self.lo_made, 1)

    def ready(self, eng, n=-1):
        eng.wait_ge(self.lo_made, range(len(self.jobs))[n] + 1)


def rows_of(a, t=TILES):
    return a.rearrange("(t p) n -> p t n", p=P)


def load_broadcast(eng, dst, src, sem):
    return eng.dma_start(dst, src.rearrange("(a n) -> a n", a=1).to_broadcast(list(dst.shape))).then_inc(sem, 16)


def project_qkv(nc, const, x, wq, wk, wv, gain_d, bias_d, scratch):
    ident, ones, minus_half, sp_alone, dve_alone = const
    xn_d, q_hi_d, q_lo_d, k_hi_d, k_lo_d, v_d = scratch
    with ExitStack() as ctx:
        def sb(name, shape, dt=F32):
            return ctx.enter_context(nc.sbuf_tensor("a_" + name, shape, dt))

        def tally(name, per, credit=False, ahead=0):
            return Tally(ctx.enter_context(nc.semaphore("a_" + name)), per, credit, ahead)

        w = {n: (sb(f"w{n}_hi", [P, KC, D], F32R), sb(f"w{n}_lo", [P, KC, D], F32R)) for n in "qkv"}
        gain, bias = sb("gain", [P, D]), sb("bias", [P, D])
        xin = [sb(f"xin{s}", [P, TILES, D]) for s in STREAMS]
        xn = [sb(f"xn{s}", [P, TILES, D]) for s in STREAMS]
        xT = [[sb(f"xT{p}{s}", [P, KC, CHUNK], F32R) for p in ("hi", "lo")] for s in STREAMS]
        stage = [{n: [sb(f"{n}T{p}{s}", [P, KC, CHUNK], F32R) for p in ("hi", "lo")] for n in "qk"} for s in STREAMS]
        vst = [sb(f"v{s}", [P, TILES, D]) for s in STREAMS]
        stats, mv = sb("stats", [P, TILES, 6]), sb("mv", [P, TILES, 2])
        veps, rstd = sb("veps", [P, TILES]), sb("rstd", [P, TILES])
        psum = ctx.enter_context(nc.psum_tensor("a_psum", [P, BANKS, 512], F32))

        weights = Weights(nc, ctx, "a", [(src.rearrange("(c p) n -> p c n", p=P), i, w[n][0][:], w[n][1][:])
                                         for i, (n, src) in enumerate(zip("qkv", (wq, wk, wv)))],
                          [a[:].bitcast(F32) for a in (stage[1]["q"][0], stage[1]["k"][0], stage[1]["k"][1])])

        PER_STREAM = 4 * 4
        params = ctx.enter_context(nc.semaphore("a_params"))
        loaded = [tally(f"x_loaded{s}", 16) for s in STREAMS]
        normed = [tally(f"normed{s}", 1, True) for s in STREAMS]
        filled = tally("bank_filled", 2 * PER_STREAM, ahead=KC)
        hi_made = tally("hi_made", 2 * 12, ahead=KC)
        emptied = tally("bank_emptied", 2 * PER_STREAM, True, ahead=KC)
        steps = tally("vector_steps", 2 * LN_STEPS, ahead=LN_STEPS)
        veps_made = tally("veps_made", 2, ahead=1)
        rstd_made = tally("rstd_made", 2, ahead=1)
        stored = [{n: tally(f"{n}_stored{s}", 16 * (2 if n in "qk" else 1), True) for n in ("xn", "q", "k", "v")}
                  for s in STREAMS]
        ring = Ring(BANKS, "D" * (2 * PER_STREAM), {"D": emptied})
        block = ctx.enter_context(nc.Block())

        def events(s, last):
            kinds = ("q", "k", "v") if last and s == 1 else ("q", "k", "turn", "v")
            return [(kind, 1 - s if kind == "turn" else s, c, s * PER_STREAM + 4 * n + c, s * 12 + 4 * n + c)
                    for n, kind in enumerate(kinds) for c in range(4)]

        first_turn = [("turn", 0, c, c - KC, c - KC) for c in range(KC)]

        def iterations(eng, body):
            with eng.Fori(0, CHUNKS - 1) as it:
                body(it, False)
            body(CHUNKS - 1, True)

        @block.scalar
        def _(act):
            def load_x(it, s):
                act.wait_ge(normed[s].sem, normed[s].at(it, 0))
                act.dma_start(xin[s][:], rows_of(x[bass.ds(it * CHUNK + s * SEQ, CHUNK), :])).then_inc(loaded[s].sem, 16)

            def step(it, kind, s, c, e, n):
                if kind == "v":
                    return
                hi = xT[s][0] if kind == "turn" else stage[s][kind][0]
                if kind in "qk" and c == 0:
                    act.wait_ge(stored[s][kind].sem, stored[s][kind].at(it, 0))
                act.wait_ge(filled.sem, filled.at(it, e + 1))
                act.activation(hi[:, c, :], psum[:, ring.bank(e), :], ACT.Copy).then_inc(hi_made.sem, 1)

            def body(it, last):
                for s in STREAMS:
                    if not last:
                        load_x(it + 1, s)
                    for event in events(s, last):
                        step(it, *event)

            for s in STREAMS:
                act.sem_inc(normed[s].sem, normed[s].per)
            load_x(0, 0)
            load_broadcast(act, gain[:], gain_d, params)
            load_broadcast(act, bias[:], bias_d, params)
            weights.make_hi(act, 0)
            load_x(0, 1)
            weights.make_hi(act, 1)
            for event in first_turn:
                step(0, *event)
            weights.make_hi(act, 2)
            weights.ready(act)
            iterations(act, body)

        @block.gpsimd
        def _(pool):
            def inverse_root(it, n):
                pool.wait_ge(veps_made.sem, veps_made.at(it, n))
                pool.tensor_tensor(rstd[:], veps[:], minus_half[:], ALU.pow).then_inc(rstd_made.sem, 1)

            def body(it, last):
                inverse_root(it, 1)
                if not last:
                    inverse_root(it, 2)

            inverse_root(0, 0)
            iterations(pool, body)

        @block.vector
        def _(dve):
            def norm(chain, it, s, n):
                dve.wait_ge(loaded[s].sem, loaded[s].at(it, 16))
                dve.wait_ge(stored[s]["xn"].sem, stored[s]["xn"].at(it, 0))
                x_, y_ = xin[s], xn[s]
                for t in range(TILES):
                    chain.link(dve.bn_stats(stats[:, t, :], x_[:, t, :]))
                chain.settle(dve_alone)
                for t in range(TILES):
                    chain.link(dve.bn_aggr(mv[:, t, :], stats[:, t, :]))
                chain.settle()
                dve.tensor_scalar(veps[:], mv[:, :, 1], EPS, None, ALU.add).then_inc(veps_made.sem, 1)
                for t in range(TILES):
                    chain.link(dve.scalar_tensor_tensor(y_[:, t, :], x_[:, t, :], mv[:, t, 0:1], gain[:],
                                                        ALU.subtract, ALU.mult))
                chain.settle()
                dve.wait_ge(rstd_made.sem, rstd_made.at(chain.it, n))
                for t in range(TILES):
                    last = dve.scalar_tensor_tensor(y_[:, t, :], y_[:, t, :], rstd[:, t:t + 1], bias[:],
                                                    ALU.mult, ALU.add)
                last.then_inc(normed[s].sem, 1)

            def step(it, kind, s, c, e, n):
                bank = psum[:, ring.bank(e), :]
                if kind == "v":
                    if c == 0:
                        dve.wait_ge(stored[s]["v"].sem, stored[s]["v"].at(it, 0))
                    dve.wait_ge(filled.sem, filled.at(it, e + 1))
                    dve.tensor_copy(vst[s][:, c, :], bank).then_inc(emptied.sem, 1)
                    return
                hi, lo = xT[s] if kind == "turn" else stage[s][kind]
                if kind in "qk" and c == 0:
                    dve.wait_ge(stored[s][kind].sem, stored[s][kind].at(it, 0))
                dve.wait_ge(hi_made.sem, hi_made.at(it, n + 1))
                dve.tensor_tensor(lo[:, c, :], bank, hi[:, c, :].bitcast(F32), ALU.subtract).then_inc(emptied.sem, 1)

            def body(it, last):
                chain = Chain(dve, steps, it)
                for s in STREAMS:
                    for event in events(s, last):
                        if event[0] == "k" and event[2] == 0 and not (last and s == 1):
                            norm(chain, it + s, 1 - s, s + 1)
                        step(it, *event)

            dve.sem_inc(emptied.sem, emptied.given)
            dve.wait_ge(params, 32)
            chain = Chain(dve, steps, 0)
            chain.n = -LN_STEPS
            norm(chain, 0, 0, 0)
            weights.make_lo(dve, 0)
            weights.make_lo(dve, 1)
            for event in first_turn:
                step(0, *event)
            weights.make_lo(dve, 2)
            iterations(dve, body)

        @block.tensor
        def _(pe):
            def step(it, kind, s, c, e, n):
                bank = psum[:, ring.bank(e), :]
                if e >= 0:
                    pe.wait_ge(*ring.free(it, e))
                if kind == "turn":
                    if c == 0:
                        ahead = 1 if s == 0 and e >= 0 else 0
                        pe.wait_ge(normed[s].sem, normed[s].at(it + ahead, 1))
                    last = transposes(pe, bank, xn[s], c, ident[:])
                elif kind == "v":
                    wh, wl = w["v"]
                    last = split_product(pe, bank, [
                        ((xT[s][0][:, k, c * P:(c + 1) * P], xT[s][1][:, k, c * P:(c + 1) * P]),
                         (wh[:, k, :], wl[:, k, :])) for k in range(KC)])
                else:
                    if kind == "q" and c == 0:
                        turned = PER_STREAM - 4 if s == 1 else -4
                        pe.wait_ge(emptied.sem, emptied.at(it, turned))
                    wh, wl = w[kind]
                    last = split_product(pe, bank, [
                        ((wh[:, k, c * P:(c + 1) * P], wl[:, k, c * P:(c + 1) * P]),
                         (xT[s][0][:, k, :], xT[s][1][:, k, :])) for k in range(KC)])
                last.then_inc(filled.sem, 1)

            def body(it, last):
                for s in STREAMS:
                    for event in events(s, last):
                        step(it, *event)

            for event in first_turn:
                step(0, *event)
            weights.ready(pe)
            pe.wait_ge(emptied.sem, emptied.per)
            iterations(pe, body)

        @block.sync
        def _(sp):
            sp.wait_ge(params, 32)
            weights.load(sp)
            for s in STREAMS:
                for n in ("xn", "q", "k", "v"):
                    sp.sem_inc(stored[s][n].sem, stored[s][n].per)

            def body(it, last):
                for s in STREAMS:
                    tokens = bass.ds(it * CHUNK + s * SEQ, CHUNK)
                    end = {kind: e + 1 for kind, _, c, e, _ in events(s, last) if c == 3}
                    sp_alone.wait(sp, normed[s].sem, normed[s].at(it, 1))
                    sp.dma_start(rows_of(xn_d[tokens, :]), xn[s][:]).then_inc(stored[s]["xn"].sem, 16)
                    for n, hi_d, lo_d in (("q", q_hi_d, q_lo_d), ("k", k_hi_d, k_lo_d)):
                        sp_alone.wait(sp, emptied.sem, emptied.at(it, end[n]))
                        for d, buf in zip((hi_d, lo_d), stage[s][n]):
                            sp.dma_start(d[:, tokens].rearrange("(c p) n -> p c n", p=P),
                                         buf[:].bitcast(F32)).then_inc(stored[s][n].sem, 16)
                    sp_alone.wait(sp, emptied.sem, emptied.at(it, end["v"]))
                    sp.dma_start(rows_of(v_d[tokens, :]), vst[s][:]).then_inc(stored[s]["v"].sem, 16)

            iterations(sp, body)
            for s in STREAMS:
                for n in ("xn", "q", "k", "v"):
                    sp_alone.wait(sp, stored[s][n].sem, stored[s][n].at(CHUNKS, 0))


def self_attention(nc, const, scratch, oT_d):
    ident, ones, minus_half, sp_alone, dve_alone = const
    xn_d, q_hi_d, q_lo_d, k_hi_d, k_lo_d, v_d = scratch
    STACK = 3 * DH
    ROWS = STACK + 2
    STEPS = BATCH * CHUNKS
    GROUPS = HEADS // GROUP
    QBUF, PBUF = 4, 4
    UNITS = TILES * GROUP * CHUNKS
    ALL_UNITS = UNITS + 1
    UB, SB = 3, 3
    UNIT_BANKS, SCORE_BANKS, O_BANK, L_BANK = 0, UB, UB + SB, UB + SB + 1
    DIRECT = (2, 5, 8, 11, 14)
    ADDED = [kt for kt in range(KT) if kt not in DIRECT]
    ADDS = len(ADDED) - 1
    NO_UNITS, TURN_AT = 2, 12
    SLOTS = [(0 if kt == NO_UNITS else 4) + (kt - 1 in DIRECT) for kt in range(KT)]
    EARLY = ALL_UNITS - sum(SLOTS[:TURN_AT + 1])
    assert sum(SLOTS) == ALL_UNITS
    SUMS_AT = sum(SLOTS[:NO_UNITS])
    with ExitStack() as ctx:
        def sb(name, shape, dt=F32):
            return ctx.enter_context(nc.sbuf_tensor("b_" + name, shape, dt))

        def tally(name, per, credit=False):
            return Tally(ctx.enter_context(nc.semaphore("b_" + name)), per, credit)

        kst = [sb(f"k_stack{b}", [ROWS, GROUP, SEQ], F32R) for b in STREAMS]
        qst = [sb(f"q_stack{i}", [ROWS, GROUP, CHUNK], F32R) for i in range(QBUF)]
        vt = [sb(f"v{b}", [P, KT, P]) for b in STREAMS]
        probs = [sb(f"probs{i}", [P, GROUP, CHUNK]) for i in range(PBUF)]
        part_max = [sb(f"part_max{i}", [P, TILES * GROUP, CHUNKS]) for i in range(2)]
        neg_max = [sb(f"neg_max{i}", [P, TILES * GROUP]) for i in range(2)]
        row_hi = [sb(f"row_hi{i}", [GROUP, CHUNK], F32R) for i in range(2)]
        row_lo = [sb(f"row_lo{i}", [GROUP, CHUNK], F32R) for i in range(2)]
        added = [sb(f"added{i}", [P, GROUP, CHUNK]) for i in range(2)]
        o_sb = [sb(f"o{i}", [P, CHUNK]) for i in range(2)]
        inv = [sb(f"inv{i}", [P, CHUNK]) for i in range(2)]
        psum = ctx.enter_context(nc.psum_tensor("b_psum", [P, BANKS, 512], F32))

        k_loaded = [tally(f"k_loaded{b}", 48) for b in STREAMS]
        v_loaded = [tally(f"v_loaded{b}", 16) for b in STREAMS]
        q_loaded = [tally(f"q_loaded{i}", 48 * STEPS // QBUF) for i in range(QBUF)]
        rows_loaded = [tally(f"rows_loaded{i}", 32 * STEPS // QBUF) for i in range(QBUF)]
        unit_filled = tally("unit_filled", STEPS * ALL_UNITS)
        unit_emptied = tally("unit_emptied", STEPS * ALL_UNITS, True)
        max_made = tally("max_made", STEPS)
        rows_made = tally("rows_made", STEPS)
        row_steps = tally("row_steps", STEPS)
        scored = tally("scored", STEPS * KT * GROUP)
        exped = tally("exped", STEPS * KT * GROUP, True)
        adds = tally("adds", STEPS * ADDS, True)
        l_done = tally("l_done", STEPS, True)
        pv_done = tally("pv_done", STEPS * KT, True)
        o_copied = tally("o_copied", STEPS, True)
        inv_made = tally("inv_made", STEPS, True)
        o_made = tally("o_made", STEPS)
        o_stored = [tally(f"o_stored{i}", 16 * STEPS // 2, True) for i in range(2)]
        ones_made = ctx.enter_context(nc.semaphore("b_ones_made"))
        block = ctx.enter_context(nc.Block())

        def tokens(q):
            return (q // CHUNKS) * SEQ + (q % CHUNKS) * CHUNK

        def at_step(it, q):
            return (it, q) if q >= 0 else (it - 1, q + STEPS)

        def before(it, q):
            return q >= 1 or not (isinstance(it, int) and it == 0)

        def units_of(q, last_group):
            todo = [(q + 1, u) for u in range(EARLY, ALL_UNITS)] + [(q + 2, u) for u in range(EARLY)]
            return [(a, u) for a, u in todo if a < STEPS or not last_group]

        def same_bank_before(n, banks, per):
            return n - banks if n >= banks else max(m for m in range(per - banks, per) if m % banks == n % banks) - per

        first_units = [(0, u) for u in range(ALL_UNITS)] + [(1, u) for u in range(EARLY)]

        @block.gpsimd
        def _(pool):
            for b in STREAMS:
                pool.memset(kst[b][STACK:ROWS].bitcast(F32), 1.0).then_inc(ones_made, 1)
            pool.sem_inc(adds.sem, adds.given)

            def body(it):
                for q in range(STEPS):
                    for i, kt in enumerate(ADDED):
                        if i == 0:
                            continue
                        n, total = q * KT + kt, added[q % 2][:]
                        pool.wait_ge(exped.sem, exped.at(it, GROUP * (n + 1)))
                        if i == 1:
                            pool.wait_ge(l_done.sem, l_done.at(it, q - 1))
                            first_term = probs[(q * KT + ADDED[0]) % PBUF][:]
                        else:
                            pool.wait_ge(adds.sem, adds.at(it, q * ADDS + i - 1))
                            first_term = total
                        pool.tensor_tensor(total, first_term, probs[n % PBUF][:], ALU.add).then_inc(adds.sem, 1)

            with pool.Fori(0, GROUPS) as it:
                body(it)

        @block.sync
        def _(sp):
            sp.sem_inc(pv_done.sem, pv_done.per)
            sp.sem_inc(l_done.sem, l_done.per)
            for i in range(2):
                sp.sem_inc(o_stored[i].sem, o_stored[i].per)

            def load_k(it, b):
                rows, cols = bass.ds(it * P, P), slice(b * SEQ, (b + 1) * SEQ)
                for n, d in enumerate((k_hi_d, k_lo_d, k_hi_d)):
                    sp.dma_start(kst[b][n * DH:(n + 1) * DH].bitcast(F32),
                                 d[rows, cols].rearrange("(h p) n -> p h n", p=DH)).then_inc(k_loaded[b].sem, 16)
                sp.dma_start(vt[b][:], v_d[cols, rows].rearrange("(t p) n -> p t n", p=P)).then_inc(v_loaded[b].sem, 16)

            def load_q(it, q):
                rows, cols = bass.ds(it * P, P), slice(tokens(q), tokens(q) + CHUNK)
                for n, d in enumerate((q_hi_d, q_hi_d, q_lo_d)):
                    sp.dma_start(qst[q % QBUF][n * DH:(n + 1) * DH].bitcast(F32),
                                 d[rows, cols].rearrange("(h p) n -> p h n", p=DH)).then_inc(q_loaded[q % QBUF].sem, 16)

            def send_rows(it, q):
                sp_alone.wait(sp, rows_made.sem, rows_made.at(it, q + 1))
                for n, row in enumerate((row_hi[q % 2], row_lo[q % 2])):
                    sp.dma_start(qst[q % QBUF][STACK + n:STACK + n + 1].bitcast(F32),
                                 row[:].bitcast(F32)).then_inc(rows_loaded[q % QBUF].sem, 16)

            def store_o(it, q):
                it, q = at_step(it, q)
                sp_alone.wait(sp, o_made.sem, o_made.at(it, q + 1))
                sp.dma_start(oT_d[bass.ds(it * P, P), tokens(q):tokens(q) + CHUNK], o_sb[q % 2][:]).then_inc(
                    o_stored[q % 2].sem, 16)

            def body(it, last):
                for q in range(STEPS):
                    if q == 0:
                        sp_alone.wait(sp, pv_done.sem, pv_done.at(it, 0))
                        load_k(it, 1)
                    if q == CHUNKS and not last:
                        sp_alone.wait(sp, pv_done.sem, pv_done.at(it, CHUNKS * KT))
                        load_k(it + 1, 0)
                    if q + 2 < STEPS or not last:
                        sp_alone.wait(sp, pv_done.sem, pv_done.at(it, (q - 1) * KT))
                        load_q(*((it, q + 2) if q + 2 < STEPS else (it + 1, q + 2 - STEPS)))
                    if before(it, q):
                        store_o(it, q - 1)
                    if q + 1 < STEPS:
                        send_rows(it, q + 1)
                    elif not last:
                        send_rows(it + 1, 0)

            load_q(0, 0)
            load_k(0, 0)
            load_q(0, 1)
            send_rows(0, 0)
            body(0, False)
            with sp.Fori(1, GROUPS - 1) as it:
                body(it, False)
            body(GROUPS - 1, True)
            store_o(GROUPS - 1, STEPS - 1)
            for i in range(2):
                sp_alone.wait(sp, o_stored[i].sem, o_stored[i].at(GROUPS, 0))

        @block.tensor
        def _(pe):
            pe.wait_ge(ones_made, len(STREAMS))

            def unit(it, q, u):
                it, q = (it, q) if q < STEPS else (it + 1, q - STEPS)
                b, n = q // CHUNKS, q * ALL_UNITS + u
                bank = UNIT_BANKS + n % UB
                if u == 0:
                    pe.wait_ge(q_loaded[q % QBUF].sem, q_loaded[q % QBUF].at(it, 48 * (q // QBUF + 1)))
                    pe.wait_ge(k_loaded[b].sem, k_loaded[b].at(it, 48))
                pe.wait_ge(unit_emptied.sem, unit_emptied.at(it, same_bank_before(n, UB, unit_emptied.per) + 1))
                if u < UNITS:
                    (t, h), c = divmod(u // CHUNKS, GROUP), u % CHUNKS
                    last = pe.matmul(psum[:, bank, :], qst[q % QBUF][0:STACK, h, t * P:(t + 1) * P],
                                     kst[b][0:STACK, h, c * 512:(c + 1) * 512], start=True, stop=True)
                else:
                    pe.wait_ge(max_made.sem, max_made.at(it, q + 1))
                    for t in range(TILES):
                        last = pe.transpose(psum[0:GROUP, bank, t * P:(t + 1) * P],
                                            neg_max[q % 2][:, t * GROUP:(t + 1) * GROUP], ident[:])
                last.then_inc(unit_filled.sem, 1)

            def body(it, last_group):
                pending = (-1, KT - 1) if before(it, 0) else None
                for q in range(STEPS):
                    todo = iter(units_of(q, last_group))

                    def units(n):
                        for _ in range(n):
                            step, u = next(todo, (0, None))
                            if u is not None:
                                unit(it, step, u)

                    pe.wait_ge(rows_loaded[q % QBUF].sem, rows_loaded[q % QBUF].at(it, 32 * (q // QBUF + 1)))
                    for kt in range(KT):
                        one = 0 if kt == NO_UNITS else 1
                        units(one)
                        scores(it, q, kt, 0)
                        scores(it, q, kt, 1)
                        units(one)
                        scores(it, q, kt, 2)
                        units(one)
                        if pending is not None:
                            pv(it, *pending, units)
                        scores(it, q, kt, 3)
                        if kt == NO_UNITS - 1 and before(it, q):
                            sum_added(it, q - 1)
                        units(one)
                        pending = (q, kt)

            def scores(it, q, kt, h):
                n = (q * KT + kt) * GROUP + h
                pe.wait_ge(exped.sem, exped.at(it, same_bank_before(n, SB, exped.per) + 1))
                pe.matmul(psum[:, SCORE_BANKS + n % SB, :], kst[q // CHUNKS][:, h, kt * P:(kt + 1) * P],
                          qst[q % QBUF][:, h, :], start=True, stop=True).then_inc(scored.sem, 1)

            def pv(it, q, kt, units):
                it, q = at_step(it, q)
                b, n = q // CHUNKS, q * KT + kt
                if kt == 0:
                    pe.wait_ge(o_copied.sem, o_copied.at(it, q))
                    pe.wait_ge(v_loaded[b].sem, v_loaded[b].at(it, 16))
                pe.wait_ge(exped.sem, exped.at(it, GROUP * (n + 1)))
                for h in range(GROUP):
                    last = pe.matmul(psum[h * DH:(h + 1) * DH, O_BANK, :], vt[b][:, kt, h * DH:(h + 1) * DH],
                                     probs[n % PBUF][:, h, :], start=(kt == 0), stop=(kt == KT - 1))
                if kt in DIRECT:
                    units(1)
                    if kt == DIRECT[0]:
                        pe.wait_ge(inv_made.sem, inv_made.at(it, q))
                    for h in range(GROUP):
                        last = pe.matmul(psum[h * DH:(h + 1) * DH, L_BANK, :], ones[:],
                                         probs[n % PBUF][:, h, :], start=(kt == DIRECT[0]), stop=False)
                last.then_inc(pv_done.sem, 1)

            def sum_added(it, q):
                it, q = at_step(it, q)
                pe.wait_ge(adds.sem, adds.at(it, (q + 1) * ADDS))
                for h in range(GROUP):
                    last = pe.matmul(psum[h * DH:(h + 1) * DH, L_BANK, :], ones[:], added[q % 2][:, h, :],
                                     start=False, stop=True)
                last.then_inc(l_done.sem, 1)

            for q, u in first_units:
                unit(0, q, u)
            body(0, False)
            with pe.Fori(1, GROUPS - 1) as it:
                body(it, False)
            body(GROUPS - 1, True)
            pv(GROUPS - 1, STEPS - 1, KT - 1, None)
            sum_added(GROUPS - 1, STEPS - 1)

        @block.scalar
        def _(act):
            for t in (exped, o_copied):
                act.sem_inc(t.sem, t.per)

            def copy_o(it, q):
                it, q = at_step(it, q)
                act.wait_ge(pv_done.sem, pv_done.at(it, (q + 1) * KT))
                act.wait_ge(o_stored[q % 2].sem, o_stored[q % 2].at(it, 16 * (q // 2)))
                act.activation(o_sb[q % 2][:], psum[:, O_BANK, :], ACT.Copy).then_inc(o_copied.sem, 1)

            def body(it):
                for q in range(STEPS):
                    for kt in range(KT):
                        n = q * KT + kt
                        act.wait_ge(pv_done.sem, pv_done.at(it, n - PBUF + 1))
                        if (kt - PBUF) % KT in ADDED:
                            step, which = (q if kt >= PBUF else q - 1), ADDED.index((kt - PBUF) % KT)
                            act.wait_ge(adds.sem, adds.at(it, step * ADDS + max(which, 1)))
                        for h in range(GROUP):
                            act.wait_ge(scored.sem, scored.at(it, GROUP * n + h + 1))
                            act.activation(probs[n % PBUF][:, h, :], psum[:, SCORE_BANKS + (GROUP * n + h) % SB, :],
                                           ACT.Exp, scale=SCALE).then_inc(exped.sem, 1)
                        if kt == 0 and before(it, q):
                            copy_o(it, q - 1)

            body(0)
            with act.Fori(1, GROUPS) as it:
                body(it)
            copy_o(GROUPS - 1, STEPS - 1)

        @block.vector
        def _(dve):
            for t in (unit_emptied, inv_made):
                dve.sem_inc(t.sem, t.per)

            def unit(it, q, u):
                it, q = (it, q) if q < STEPS else (it + 1, q - STEPS)
                n, i = q * ALL_UNITS + u, q % 2
                bank = UNIT_BANKS + n % UB
                if u == UNITS:
                    dve.wait_ge(unit_emptied.sem, unit_emptied.at(it, n))
                    dve.tensor_reduce(neg_max[i][:], part_max[i][:], AX.X, ALU.max,
                                      negate=True).then_inc(max_made.sem, 1)
                    dve.wait_ge(unit_filled.sem, unit_filled.at(it, n + 1))
                    dve.tensor_copy(row_hi[i][:], psum[0:GROUP, bank, :]).then_inc(row_steps.sem, 1)
                    dve.wait_ge(row_steps.sem, row_steps.at(it, q + 1))
                    dve.tensor_tensor(row_lo[i][:], psum[0:GROUP, bank, :], row_hi[i][:].bitcast(F32),
                                      ALU.subtract).then_inc(rows_made.sem, 1)
                    dve.wait_ge(rows_made.sem, rows_made.at(it, q + 1))
                    dve.sem_inc(unit_emptied.sem, 1)
                else:
                    dve.wait_ge(unit_filled.sem, unit_filled.at(it, n + 1))
                    dve.tensor_reduce(part_max[i][:, u // CHUNKS, u % CHUNKS:u % CHUNKS + 1], psum[:, bank, :],
                                      AX.X, ALU.max).then_inc(unit_emptied.sem, 1)

            def finish_o(it, q):
                it, q = at_step(it, q)
                i = q % 2
                dve.wait_ge(l_done.sem, l_done.at(it, q + 1))
                dve.reciprocal(inv[i][:], psum[:, L_BANK, :]).then_inc(inv_made.sem, 1)
                dve.wait_ge(inv_made.sem, inv_made.at(it, q + 1))
                dve.wait_ge(o_copied.sem, o_copied.at(it, q + 1))
                dve.tensor_tensor(o_sb[i][:], o_sb[i][:], inv[i][:], ALU.mult).then_inc(o_made.sem, 1)

            def body(it, last):
                for q in range(STEPS):
                    todo = units_of(q, last)
                    for step, u in todo[:SUMS_AT]:
                        unit(it, step, u)
                    if before(it, q):
                        finish_o(it, q - 1)
                    for step, u in todo[SUMS_AT:]:
                        unit(it, step, u)

            for q, u in first_units:
                unit(0, q, u)
            body(0, False)
            with dve.Fori(1, GROUPS - 1) as it:
                body(it, False)
            body(GROUPS - 1, True)
            finish_o(GROUPS - 1, STEPS - 1)


def context_keys(nc, const, name, ctx_d, wk_d, wv_d, norms, biases, kblk, values, jobs):
    ident, ones, minus_half, sp_alone, dve_alone = const
    with ExitStack() as ctx:
        def sb(n, shape, dt=F32):
            return ctx.enter_context(nc.sbuf_tensor(f"{name}_{n}", shape, dt))

        def sem(n):
            return ctx.enter_context(nc.semaphore(f"{name}_{n}"))

        rows = sb("ctx", [CTX, BATCH, D])
        w = [sb("wk", [P, KC, D]), sb("wv", [P, KC, D])]
        xT = [sb("kin_T", [P, KC, BATCH * CTX]), sb("vin_T", [P, KC, BATCH * CTX])]
        y = [sb("kin", [CTX, BATCH, D]), sb("vin", [CTX, BATCH, D])] if norms else [rows, rows]
        gb = [[sb(f"gb{i}{j}", [CTX, D]) for j in range(2)] for i in range(2)] if norms else None
        kbias = sb("kbias", [P, KC]) if biases else None
        vbias = sb("vbias", [CTX, D]) if biases else None
        stats, mv = sb("stats", [CTX, BATCH, 6]), sb("mv", [CTX, BATCH, 2])
        veps, rstd = sb("veps", [CTX, BATCH]), sb("rstd", [CTX, BATCH])
        psum = ctx.enter_context(nc.psum_tensor(f"{name}_psum", [P, BANKS, 512], F32))
        loaded, zeroed, veps_made, rstd_made = sem("loaded"), sem("zeroed"), sem("veps_made"), sem("rstd_made")
        steps, normed, filled, emptied = sem("vector_steps"), sem("normed"), sem("filled"), sem("emptied")
        LOADS = 1 + (4 if norms else 0) + (2 if biases else 0)
        w_loaded = [sem(f"{n}_loaded") for n in ("wk", "wv")]
        raws = [sb(f"raw{i}", [P, KC, D]) for i in range(len(jobs))]
        weights = Weights(nc, ctx, name, jobs, [a[:] for a in raws])
        block = ctx.enter_context(nc.Block())

        @block.sync
        def _(sp):
            sp.dma_start(rows[:], ctx_d.rearrange("(b n) d -> n b d", b=BATCH)).then_inc(loaded, 16)
            if norms:
                for i in range(2):
                    for j in range(2):
                        load_broadcast(sp, gb[i][j][:], norms[i][j], loaded)
            if biases:
                sp.dma_start(kbias[:], biases[0]).then_inc(loaded, 16)
                load_broadcast(sp, vbias[:], biases[1], loaded)
            for i, d in enumerate((wk_d, wv_d)):
                sp.dma_start(w[i][:], d.rearrange("(c p) n -> p c n", p=P)).then_inc(w_loaded[i], 16)
            weights.load(sp)

        @block.scalar
        def _(act):
            for n in range(len(jobs)):
                weights.make_hi(act, n)

        @block.gpsimd
        def _(pool):
            pool.memset(kblk[:], 0.0).then_inc(zeroed, 1)
            if norms:
                pool.wait_ge(veps_made, 1)
                pool.tensor_tensor(rstd[:], veps[:], minus_half[0:CTX, 0:BATCH], ALU.pow).then_inc(rstd_made, 1)

        @block.vector
        def _(dve):
            chain = Chain(dve, Tally(steps, 0), 0)
            dve.wait_ge(loaded, 16 * LOADS)
            if norms:
                for b in range(BATCH):
                    chain.link(dve.bn_stats(stats[:, b, :], rows[:, b, :]))
                chain.settle(dve_alone)
                for b in range(BATCH):
                    chain.link(dve.bn_aggr(mv[:, b, :], stats[:, b, :]))
                chain.settle()
                dve.tensor_scalar(veps[:], mv[:, :, 1], EPS, None, ALU.add).then_inc(veps_made, 1)
                for i in range(2):
                    for b in range(BATCH):
                        chain.link(dve.scalar_tensor_tensor(y[i][:, b, :], rows[:, b, :], mv[:, b, 0:1], gb[i][0][:],
                                                            ALU.subtract, ALU.mult))
                chain.settle()
                dve.wait_ge(rstd_made, 1)
                for i in range(2):
                    for b in range(BATCH):
                        dve.scalar_tensor_tensor(y[i][:, b, :], y[i][:, b, :], rstd[:, b:b + 1], gb[i][1][:],
                                                 ALU.mult, ALU.add).then_inc(normed, 1)
            for i in range(2):
                for c in range(KC):
                    dve.wait_ge(filled, i * KC + c + 1)
                    dve.tensor_copy(xT[i][:, c, :], psum[:, i * KC + c, 0:BATCH * CTX]).then_inc(emptied, 1)
            weights.make_lo(dve, 0)
            dve.wait_ge(zeroed, 1)
            for c in range(KC):
                dve.wait_ge(filled, 2 * KC + c + 1)
                for h in range(GROUP):
                    r = slice(h * DH, (h + 1) * DH)
                    out = kblk[r, :, c, h * CTX:(h + 1) * CTX]
                    src = psum[r, c, 0:BATCH * CTX].rearrange("p (b n) -> p b n", b=BATCH)
                    if biases:
                        dve.tensor_scalar(out, src, kbias[r, c:c + 1], None, ALU.add).then_inc(emptied, 1)
                    else:
                        dve.tensor_copy(out, src).then_inc(emptied, 1)
            for b in range(BATCH):
                dve.wait_ge(filled, 3 * KC + b + 1)
                src = psum[0:CTX, KC + b, :]
                if biases:
                    dve.tensor_tensor(values[:, b, :], src, vbias[:], ALU.add).then_inc(emptied, 1)
                else:
                    dve.tensor_copy(values[:, b, :], src).then_inc(emptied, 1)
            for n in range(1, len(jobs)):
                weights.make_lo(dve, n)
            weights.ready(dve)
            dve.wait_ge(emptied, 2 * KC + KC * GROUP + BATCH)

        @block.tensor
        def _(pe):
            pe.wait_ge(loaded, 16 * LOADS)
            if norms:
                pe.wait_ge(normed, 2 * BATCH)
            for i in range(2):
                for c in range(KC):
                    for b in range(BATCH):
                        last = pe.transpose(psum[:, i * KC + c, b * CTX:(b + 1) * CTX],
                                            y[i][:, b, c * P:(c + 1) * P], ident[0:CTX, 0:CTX])
                    last.then_inc(filled, 1)
            pe.wait_ge(emptied, 2 * KC)
            pe.wait_ge(w_loaded[0], 16)
            for c in range(KC):
                for k in range(KC):
                    last = pe.matmul(psum[:, c, 0:BATCH * CTX], w[0][:, k, c * P:(c + 1) * P], xT[0][:, k, :],
                                     start=(k == 0), stop=(k == KC - 1))
                last.then_inc(filled, 1)
            pe.wait_ge(w_loaded[1], 16)
            for b in range(BATCH):
                for k in range(KC):
                    last = pe.matmul(psum[0:CTX, KC + b, :], xT[1][:, k, b * CTX:(b + 1) * CTX], w[1][:, k, :],
                                     start=(k == 0), stop=(k == KC - 1))
                last.then_inc(filled, 1)


def attention_order(first):
    tiles = BATCH * TILES
    places = {}

    def put(slot, place, steps):
        places.setdefault((slot, place), []).extend(steps)

    def steps(kind, ahead, s, which):
        return [(kind, ahead, s, j) for j in which]

    def projected(ahead, s, t):
        return [("out0", ahead, s, t)] + ([("n2", ahead, s, t - 1)] if t else []) + [("n1", ahead, s, t)]

    if first:
        put(5, 0, projected(1, 0, 0))
        put(5, 1, projected(1, 0, 1))
        put(6, 0, projected(1, 0, 2))
        put(6, 1, projected(1, 0, 3) + [("n2", 1, 0, 3)])
        put(7, 0, steps("turn", 1, 0, (0, 1)))
        put(7, 1, steps("turn", 1, 0, (2, 3)))
        put(8, 0, [("split", 1, 1, 0)] + steps("q", 1, 0, (0, 1)))
        put(8, 1, steps("q", 1, 0, (2, 3)))
        put(9, 0, projected(1, 1, 0))
        put(9, 1, projected(1, 1, 1))
        put(10, "first", projected(1, 1, 2))
        put(0, 0, projected(0, 1, 3) + [("n2", 0, 1, 3)])
        put(1, 0, steps("turn", 0, 1, range(KC)))
        put(2, 0, steps("q", 0, 1, (0,)))
        put(3, 0, steps("q", 0, 1, (1,)))
        put(3, 1, [("split", 1, 0, 0)] + steps("q", 0, 1, (2, 3)))
    else:
        for ahead, s, turn, q in ((0, 1, 10, (0, 0, 1, 2)), (1, 0, 4, (5, 6, 8, 9))):
            put(turn, 0, steps("turn", 1, s, (0, 1)))
            put(turn, 1, steps("turn", 1, s, (2, 3)))
            for c in range(KC):
                put(q[c], 1, steps("q", ahead, s, (c,)))
    order = []
    for i in range(tiles + 4):
        def at(kind, tile, groups=(0,)):
            return [(kind, tile, g) for g in groups] if 0 <= tile < tiles else []

        if not first and i in (2, 2 + TILES):
            order.append(("residual", (i - 2) // TILES, 0))
        order += places.get((i, "first"), []) + at("soft", i - 1) + at("scores", i) + ([] if first else at("n2", i - 4))
        order += at("pT", i - 2, (0, 1)) + at("out", i - 3) + at("pT", i - 2, (2,)) + places.get((i, 0), [])
        order += at("pT", i - 2, (3,)) + at("exp", i) + places.get((i, 1), []) + at("pv", i - 2)
    return order


def cross_weights(nc, held, name, sources):
    w = {n: [held.enter_context(nc.sbuf_tensor(f"{name}_{n}_{part}", [P, KC, D], F32R)) for part in ("hi", "lo")]
         for n in sources}
    return w, [(d.rearrange("(c p) n -> p c n", p=P), i, w[n][0][:], w[n][1][:])
               for i, (n, d) in enumerate(sources.items())]


def cross_attention(nc, const, name, first, x_d, out_d, oT_d, w, vectors, q_bias_d, kblk, values):
    ident, ones, minus_half, sp_alone, dve_alone = const
    GW = GROUP * CTX
    N = BATCH * TILES
    with ExitStack() as ctx:
        def sb(n, shape, dt=F32):
            return ctx.enter_context(nc.sbuf_tensor(f"{name}_{n}", shape, dt))

        def tally(n, per, credit=False):
            return Tally(ctx.enter_context(nc.semaphore(f"{name}_{n}")), per, credit)

        vec = [sb(f"vec{i}", [P, D]) for i in range(len(vectors))]
        q_bias = None if first else sb("q_bias", [P, KC])
        oT = sb("oT", [P, KC, CHUNK]) if first else None
        xin = sb("xin", [P, TILES, D]) if first else None
        x = [sb(f"x{s}", [P, TILES, D]) for s in STREAMS]
        xT = [[sb(f"xT{p}{s}", [P, KC, CHUNK], F32R) for p in ("hi", "lo")] for s in STREAMS]
        qT = [sb(f"qT{s}", [P, KC, CHUNK]) for s in STREAMS]
        probs = [sb(f"probs{i}", [P, HEADS, CTX]) for i in range(3)]
        pT = sb("pT", [CTX, HEADS, P])
        o2T = [[sb(f"o2T{p}{i}", [P, KC, P], F32R) for p in ("hi", "lo")] for i in range(2)]
        y = [sb(f"y{s}", [P, TILES, D]) for s in STREAMS]
        row_max = sb("row_max", [P, HEADS])
        row_sum, row_inv = ([sb(f"{n}{i}", [P, HEADS]) for i in range(2)] for n in ("row_sum", "row_inv"))
        stats, mv = sb("stats", [P, TILES, 6]), sb("mv", [P, TILES, 2])
        veps, rstd = sb("veps", [P, TILES]), sb("rstd", [P, TILES])
        psum = ctx.enter_context(nc.psum_tensor(f"{name}_psum", [P, BANKS, 512], F32))
        RING = 2
        PREP_BANKS, ATT_BANKS, S_BANK = 0, RING, 2 * RING

        order = attention_order(first)
        prep = [(kind, s, j) for s in STREAMS for kind in (("out0",) if first else ()) + ("turn", "q")
                for j in range(4)]
        att = [e for e in order if e[0] in ("pT", "out", "pv")]
        prep_readers = "".join({"out0": "D", "turn": "D", "q": "A"}[e[0]] for e in prep)
        att_readers = "".join({"out": "D", "pv": "D", "pT": "A"}[e[0]] for e in att)
        prep_filled, att_filled = tally("prep_filled", len(prep)), tally("att_filled", len(att))
        prep_read = {r: tally(f"prep_read_{r}", prep_readers.count(r), True) for r in "DA"}
        att_read = {r: tally(f"att_read_{r}", att_readers.count(r), True) for r in "DA"}
        prep_ring, att_ring = Ring(RING, prep_readers, prep_read), Ring(RING, att_readers, att_read)
        turn_hi, pv_hi = tally("turn_hi", BATCH * KC), tally("pv_hi", N)

        def was_read(it, e):
            events, readers, read = (prep, prep_readers, prep_read) if e in prep else (att, att_readers, att_read)
            n = events.index(e)
            return read[readers[n]].sem, read[readers[n]].at(it, readers[:n + 1].count(readers[n]))

        if first:
            oT_loaded, xin_loaded = tally("oT_loaded", 16 * BATCH), tally("xin_loaded", 16 * BATCH)
            oT_hi, oT_lo = tally("oT_hi", BATCH), tally("oT_lo", BATCH)
            prep_steps = tally("prep_steps", 3 * N)
        else:
            x_loaded = [tally(f"x_loaded{s}", 16) for s in STREAMS]
            y_loaded = [tally(f"y_loaded{s}", 16) for s in STREAMS]
            residual = tally("residual", BATCH)
        veps_made, rstd_made, normed = tally("veps_made", N), tally("rstd_made", N), tally("normed", N)
        scores_filled = tally("scores_filled", N)
        scores_emptied = tally("scores_emptied", N, True)
        exped, inverted, probs_made = tally("exped", N), tally("inverted", N), tally("probs_made", N)
        att_steps = tally("att_steps", (2 if first else 5) * N)
        stored = [tally(f"stored{s}", 16, True) for s in STREAMS]
        params = ctx.enter_context(nc.semaphore(f"{name}_params"))
        N_PARAMS = len(vectors) + (0 if first else 1)
        block = ctx.enter_context(nc.Block())

        PREPARING = ("split", "out0", "turn", "q")
        start = [("split", 0, s, 0) for s in STREAMS] if first else []
        for s in STREAMS:
            if first:
                for t in range(TILES - s):
                    start += [("out0", 0, s, t)] + ([("n2", 0, s, t - 1)] if t else []) + [("n1", 0, s, t)]
                if s == 0:
                    start.append(("n2", 0, s, TILES - 1))
            if s == 0 or not first:
                start += [("turn", 0, s, c) for c in range(KC)]
            if s == 0:
                start += [("q", 0, s, c) for c in range(KC)]

        def is_prep(e):
            return e[0] in PREPARING or (first and e[0] in ("n1", "n2"))

        def run(eng, prepare, attend):
            for kind, _, s, j in start:
                prepare(0, kind, s, j)

            def body(it, last):
                for e in order:
                    if is_prep(e):
                        kind, ahead, s, j = e
                        if not (last and ahead):
                            prepare(it + 1 if ahead else it, kind, s, j)
                    else:
                        attend(it, *e)

            with eng.Fori(0, CHUNKS - 1) as it:
                body(it, False)
            body(CHUNKS - 1, True)

        @block.sync
        def _(sp):
            for s in STREAMS:
                sp.sem_inc(stored[s].sem, stored[s].per)
            def tokens(it, s):
                return bass.ds(it * CHUNK + s * SEQ, CHUNK)

            def load_oT(it, s, wait=True):
                if wait:
                    sp_alone.wait(sp, oT_lo.sem, oT_lo.at(it, s))
                sp.dma_start(oT[:], oT_d[:, tokens(it, s)].rearrange("(c p) n -> p c n", p=P)).then_inc(oT_loaded.sem, 16)

            def load_xin(it, s, wait=True):
                if wait:
                    sp_alone.wait(sp, *was_read(it - 1 + s, ("out0", 1 - s, TILES - 1)))
                sp.dma_start(xin[:], rows_of(x_d[tokens(it, s), :])).then_inc(xin_loaded.sem, 16)

            def load_x(it, s, wait=True):
                if wait:
                    sp_alone.wait(sp, *was_read(it - 1, ("turn", s, KC - 1)))
                sp.dma_start(x[s][:], rows_of(x_d[tokens(it, s), :])).then_inc(x_loaded[s].sem, 16)

            def load_y(it, s):
                sp_alone.wait(sp, stored[s].sem, stored[s].at(it, 0))
                sp.dma_start(y[s][:], rows_of(x_d[tokens(it, s), :])).then_inc(y_loaded[s].sem, 16)

            def store(it, s):
                if first:
                    sp_alone.wait(sp, *was_read(it, ("out", s * TILES + TILES - 1, 0)))
                else:
                    sp_alone.wait(sp, normed.sem, normed.at(it, (s + 1) * TILES))
                sp.dma_start(rows_of(out_d[tokens(it, s), :]), y[s][:]).then_inc(stored[s].sem, 16)

            def body(it, last):
                if first and not last:
                    load_oT(it + 1, 0)
                    load_xin(it + 1, 0)
                    load_oT(it + 1, 1)
                if not first and not last:
                    load_x(it + 1, 0)
                    load_x(it + 1, 1)
                store(it, 0)
                if not last:
                    load_xin(it + 1, 1) if first else load_y(it + 1, 0)
                store(it, 1)
                if not first and not last:
                    load_y(it + 1, 1)

            if first:
                load_oT(0, 0, False)
                load_xin(0, 0, False)
            else:
                load_x(0, 0, False)
            for v, d in zip(vec, vectors):
                load_broadcast(sp, v[:], d, params)
            if first:
                load_oT(0, 1)
                load_xin(0, 1)
            else:
                sp.dma_start(q_bias[:], q_bias_d).then_inc(params, 16)
                load_x(0, 1, False)
                for s in STREAMS:
                    load_y(0, s)
            with sp.Fori(0, CHUNKS - 1) as it:
                body(it, False)
            body(CHUNKS - 1, True)
            for s in STREAMS:
                sp_alone.wait(sp, stored[s].sem, stored[s].at(CHUNKS, 0))

        @block.gpsimd
        def _(pool):
            def inverse_root(it, n, t):
                pool.wait_ge(veps_made.sem, veps_made.at(it, n + 1))
                pool.tensor_tensor(rstd[:, t:t + 1], veps[:, t:t + 1], minus_half[:, 0:1], ALU.pow).then_inc(
                    rstd_made.sem, 1)

            def prepare(it, kind, s, j):
                if kind == "n1":
                    inverse_root(it, s * TILES + j, j)

            def attend(it, kind, i, g):
                if kind == "soft":
                    pool.wait_ge(inverted.sem, inverted.at(it, i + 1))
                    pool.tensor_tensor(probs[i % 3][:], probs[i % 3][:],
                                       row_inv[i % 2][:].unsqueeze(2).to_broadcast([P, HEADS, CTX]),
                                       ALU.mult).then_inc(probs_made.sem, 1)
                elif kind == "residual":
                    pool.wait_ge(y_loaded[i].sem, y_loaded[i].at(it, 16))
                    pool.tensor_tensor(y[i][:], y[i][:], vec[2][:].unsqueeze(1).to_broadcast([P, TILES, D]),
                                       ALU.add).then_inc(residual.sem, 1)
                elif kind == "out" and not first:
                    inverse_root(it, i, i % TILES)

            if not first:
                pool.wait_ge(params, 16 * N_PARAMS)
            run(pool, prepare, attend)

        @block.tensor
        def _(pe):
            def prepare(it, kind, s, j):
                if kind not in ("out0", "turn", "q"):
                    return
                n = prep.index((kind, s, j))
                bank = psum[:, PREP_BANKS + prep_ring.bank(n), :]
                if j == 0:
                    if kind == "out0":
                        pe.wait_ge(oT_lo.sem, oT_lo.at(it, s + 1))
                    elif kind == "q":
                        pe.wait_ge(*was_read(it, ("turn", s, KC - 1)))
                    elif first:
                        pe.wait_ge(normed.sem, normed.at(it, (s + 1) * TILES))
                    else:
                        pe.wait_ge(x_loaded[s].sem, x_loaded[s].at(it, 16))
                pe.wait_ge(*prep_ring.free(it, n))
                if kind == "out0":
                    last = split_product(pe, bank, [
                        ((xT[s][0][:, k, j * P:(j + 1) * P], xT[s][1][:, k, j * P:(j + 1) * P]),
                         (w["wo0"][0][:, k, :], w["wo0"][1][:, k, :])) for k in range(KC)])
                elif kind == "turn":
                    last = transposes(pe, bank, x[s], j, ident[:])
                else:
                    last = split_product(pe, bank, [
                        ((w["wq"][0][:, k, j * P:(j + 1) * P], w["wq"][1][:, k, j * P:(j + 1) * P]),
                         (xT[s][0][:, k, :], xT[s][1][:, k, :])) for k in range(KC)])
                last.then_inc(prep_filled.sem, 1)

            def attend(it, kind, i, g):
                s, t = divmod(i, TILES)
                if kind == "scores":
                    if t == 0:
                        pe.wait_ge(*was_read(it, ("q", s, KC - 1)))
                    pe.wait_ge(scores_emptied.sem, scores_emptied.at(it, i))
                    for c in range(KC):
                        last = pe.matmul(psum[:, S_BANK + c, 0:GW], qT[s][:, c, t * P:(t + 1) * P],
                                         kblk[:, s, c, :], start=True, stop=True)
                    last.then_inc(scores_filled.sem, 1)
                if kind not in ("pT", "out", "pv"):
                    return
                n = att.index((kind, i, g))
                bank = psum[:, ATT_BANKS + att_ring.bank(n), :]
                pe.wait_ge(*att_ring.free(it, n))
                if kind == "pT":
                    if g == 0:
                        pe.wait_ge(probs_made.sem, probs_made.at(it, i + 1))
                    for h in range(GROUP):
                        last = pe.transpose(bank[0:CTX, h * P:(h + 1) * P], probs[i % 3][:, g * GROUP + h, :], ident[:])
                elif kind == "pv":
                    pe.wait_ge(*was_read(it, ("pT", i, KC - 1)))
                    for c in range(KC):
                        for h in range(GROUP):
                            last = pe.matmul(bank[h * DH:(h + 1) * DH, c * P:(c + 1) * P],
                                             values[:, s, (c * GROUP + h) * DH:(c * GROUP + h + 1) * DH],
                                             pT[:, c * GROUP + h, :], start=True, stop=True)
                else:
                    pe.wait_ge(*was_read(it, ("pv", i, 0)))
                    hi, lo = o2T[i % 2]
                    last = split_product(pe, bank, [
                        ((hi[:, k, :], lo[:, k, :]), (w["wo"][0][:, k, :], w["wo"][1][:, k, :])) for k in range(KC)])
                last.then_inc(att_filled.sem, 1)

            run(pe, prepare, attend)

        @block.scalar
        def _(act):
            def prepare(it, kind, s, j):
                if kind == "split":
                    act.wait_ge(oT_loaded.sem, oT_loaded.at(it, 16 * (s + 1)))
                    act.activation(xT[s][0][:], oT[:], ACT.Copy).then_inc(oT_hi.sem, 1)
                if kind not in ("turn", "q"):
                    return
                n = prep.index((kind, s, j))
                bank = psum[:, PREP_BANKS + prep_ring.bank(n), :]
                act.wait_ge(prep_filled.sem, prep_filled.at(it, n + 1))
                if kind == "turn":
                    act.activation(xT[s][0][:, j, :], bank, ACT.Copy).then_inc(turn_hi.sem, 1)
                elif first:
                    act.activation(qT[s][:, j, :], bank, ACT.Copy).then_inc(prep_read["A"].sem, 1)
                else:
                    act.activation(qT[s][:, j, :], bank, ACT.Identity, bias=q_bias[:, j:j + 1]).then_inc(
                        prep_read["A"].sem, 1)

            def attend(it, kind, i, g):
                if kind == "exp":
                    act.wait_ge(scores_emptied.sem, scores_emptied.at(it, i + 1))
                    act.activation(probs[i % 3][:], probs[i % 3][:], ACT.Exp, scale=SCALE).then_inc(exped.sem, 1)
                if kind not in ("pT", "pv"):
                    return
                n = att.index((kind, i, g))
                bank = psum[:, ATT_BANKS + att_ring.bank(n), :]
                act.wait_ge(att_filled.sem, att_filled.at(it, n + 1))
                if kind == "pT":
                    act.activation(pT[:, g * GROUP:(g + 1) * GROUP, :].rearrange("p h n -> p (h n)"),
                                   bank[0:CTX, :], ACT.Copy).then_inc(att_read["A"].sem, 1)
                else:
                    act.activation(o2T[i % 2][0][:].rearrange("p c n -> p (c n)"), bank,
                                   ACT.Copy).then_inc(pv_hi.sem, 1)

            for t in (prep_read["A"], att_read["A"]):
                act.sem_inc(t.sem, t.per)
            act.wait_ge(params, 16 * N_PARAMS)
            run(act, prepare, attend)

        @block.vector
        def _(dve):
            for t in (prep_read["D"], att_read["D"], scores_emptied):
                dve.sem_inc(t.sem, t.per)
            dve.wait_ge(params, 16 * N_PARAMS)

            def norm_begin(chain, a, t):
                chain.link(dve.bn_stats(stats[:, t, :], a))
                chain.settle(dve_alone)
                chain.link(dve.bn_aggr(mv[:, t, :], stats[:, t, :]))
                chain.settle()
                dve.tensor_scalar(veps[:, t:t + 1], mv[:, t, 1:2], EPS, None, ALU.add).then_inc(veps_made.sem, 1)
                chain.link(dve.scalar_tensor_tensor(a, a, mv[:, t, 0:1], vec[0][:], ALU.subtract, ALU.mult))

            def norm_end(chain, it, n, a, t):
                chain.settle()
                dve.wait_ge(rstd_made.sem, rstd_made.at(it, n + 1))
                dve.scalar_tensor_tensor(a, a, rstd[:, t:t + 1], vec[1][:], ALU.mult, ALU.add).then_inc(normed.sem, 1)

            def prepare(it, kind, s, j):
                tile = x[s][:, j, :]
                if kind == "split":
                    dve.wait_ge(oT_hi.sem, oT_hi.at(it, s + 1))
                    dve.tensor_tensor(xT[s][1][:], oT[:], xT[s][0][:].bitcast(F32), ALU.subtract).then_inc(oT_lo.sem, 1)
                elif kind in ("n1", "n2"):
                    chain = Chain(dve, prep_steps, it)
                    chain.n = 3 * (s * TILES + j) + (3 if kind == "n2" else 0)
                    if kind == "n1":
                        dve.wait_ge(*was_read(it, ("out0", s, j)))
                        norm_begin(chain, tile, j)
                    else:
                        norm_end(chain, it, s * TILES + j, tile, j)
                if kind not in ("out0", "turn"):
                    return
                n = prep.index((kind, s, j))
                bank = psum[:, PREP_BANKS + prep_ring.bank(n), :]
                if kind == "out0":
                    if j == 0:
                        dve.wait_ge(xin_loaded.sem, xin_loaded.at(it, 16 * (s + 1)))
                    dve.wait_ge(*was_read(it - 1, ("out", s * TILES + j, 0)))
                    dve.wait_ge(prep_filled.sem, prep_filled.at(it, n + 1))
                    dve.tensor_tensor(tile, bank, xin[:, j, :], ALU.add).then_inc(prep_read["D"].sem, 1)
                else:
                    dve.wait_ge(turn_hi.sem, turn_hi.at(it, s * KC + j + 1))
                    dve.tensor_tensor(xT[s][1][:, j, :], bank, xT[s][0][:, j, :].bitcast(F32),
                                      ALU.subtract).then_inc(prep_read["D"].sem, 1)

            chains = {}

            def attend(it, kind, i, g):
                s, t = divmod(i, TILES)
                if kind == "scores" and i == 0:
                    chains["att"] = Chain(dve, att_steps, it)
                chain = chains.get("att")
                if kind == "scores":
                    dve.wait_ge(scores_filled.sem, scores_filled.at(it, i + 1))
                    scores = psum[:, S_BANK:S_BANK + KC, 0:GW].rearrange("p g (h n) -> p g h n", h=GROUP)
                    by_head = row_max[:].rearrange("p (g h) -> p g h", g=KC)
                    chain.link(dve.tensor_reduce(by_head, scores, AX.X, ALU.max))
                    chain.settle()
                    dve.tensor_tensor(probs[i % 3][:].rearrange("p (g h) n -> p g h n", g=KC), scores,
                                      by_head.unsqueeze(3).to_broadcast([P, KC, GROUP, CTX]),
                                      ALU.subtract).then_inc(scores_emptied.sem, 1)
                elif kind == "soft":
                    dve.wait_ge(exped.sem, exped.at(it, i + 1))
                    chain.link(dve.tensor_reduce(row_sum[i % 2][:], probs[i % 3][:], AX.X, ALU.add))
                    chain.settle()
                    dve.reciprocal(row_inv[i % 2][:], row_sum[i % 2][:]).then_inc(inverted.sem, 1)
                elif kind == "pv":
                    n = att.index((kind, i, g))
                    dve.wait_ge(pv_hi.sem, pv_hi.at(it, i + 1))
                    hi, lo = (a[:].rearrange("p c n -> p (c n)") for a in o2T[i % 2])
                    dve.tensor_tensor(lo, psum[:, ATT_BANKS + att_ring.bank(n), :], hi.bitcast(F32),
                                      ALU.subtract).then_inc(att_read["D"].sem, 1)
                elif kind == "out":
                    n, tile = att.index((kind, i, g)), y[s][:, t, :]
                    if t == 0:
                        if first:
                            dve.wait_ge(stored[s].sem, stored[s].at(it, 0))
                        else:
                            dve.wait_ge(residual.sem, residual.at(it, s + 1))
                    dve.wait_ge(att_filled.sem, att_filled.at(it, n + 1))
                    dve.tensor_tensor(tile, psum[:, ATT_BANKS + att_ring.bank(n), :], x[s][:, t, :] if first else tile,
                                      ALU.add).then_inc(att_read["D"].sem, 1)
                    if not first:
                        dve.wait_ge(*was_read(it, (kind, i, g)))
                        norm_begin(chain, tile, t)
                    if i == N - 1:
                        chain.end()
                elif kind == "n2":
                    norm_end(chain, it, i, y[s][:, t, :], t)

            run(dve, prepare, attend)


def mlp(nc, const, x_d, out_d, w1_d, w2_d, b1_d, b2_d, gain_d, bias_d):
    ident, ones, minus_half, sp_alone, dve_alone = const
    PART = 2
    PARTS = DFF // P // PART
    RING, ACC = 4, 4
    SLOTS = range(2)
    N = BATCH * CHUNKS // 2
    with ExitStack() as ctx:
        def sb(n, shape, dt=F32):
            return ctx.enter_context(nc.sbuf_tensor(f"m_{n}", shape, dt))

        def tally(n, per, credit=False, ahead=0):
            return Tally(ctx.enter_context(nc.semaphore(f"m_{n}")), per, credit, ahead)

        w1 = [sb(f"w1_{p}", [P, KC, DFF], F32R) for p in ("hi", "lo")]
        w2 = [sb(f"w2_{p}", [P, DFF // P, D], F32R) for p in ("hi", "lo")]
        gain, bias, b2 = sb("gain", [P, D]), sb("bias", [P, D]), sb("b2", [P, D])
        b1 = sb("b1", [P, DFF // P])
        x = [sb(f"x{s}", [P, TILES, D]) for s in SLOTS]
        h = sb("h", [P, TILES, D])
        raw = sb("raw", [P, KC, D])
        hT = [sb(f"hT_{p}", [P, KC, CHUNK], F32R) for p in ("hi", "lo")]
        relu = [sb(f"relu{i}", [P, CHUNK]) for i in range(2)]
        hidden = [[sb(f"hidden_{p}{i}", [P, PART, CHUNK], F32R) for p in ("hi", "lo")] for i in range(2)]
        stats, mv = sb("stats", [P, TILES, 6]), sb("mv", [P, TILES, 2])
        veps, rstd = sb("veps", [P, TILES]), sb("rstd", [P, TILES])
        psum = ctx.enter_context(nc.psum_tensor("m_psum", [P, BANKS, 512], F32))

        def quarter(which, k, i):
            if which == 1:
                part = slice(k * D, (k + 1) * D)
                return (w1_d[:, part].rearrange("(c p) n -> p c n", p=P), i, w1[0][:, :, part], w1[1][:, :, part])
            part = slice(k * KC, (k + 1) * KC)
            return (w2_d[k * D:(k + 1) * D, :].rearrange("(c p) n -> p c n", p=P), i,
                    w2[0][:, part, :], w2[1][:, part, :])

        quarters = [(1, 0), (1, 1), (2, 0), (1, 2), (2, 1), (1, 3), (2, 2), (2, 3)]
        weights = Weights(nc, ctx, "m", [quarter(*q, i) for q, i in zip(quarters, (0, 1, 0, 1, 0, 0, 0, 0))],
                          [raw[:], x[1][:]])
        BEFORE_X = 4
        SPLIT_AT = {1: 1, 2: 2, 4: 3, 5: 4, 8: 5, 10: 6, 13: 7}

        MADE = PARTS * PART
        EVENTS = MADE + KC
        d_emptied = tally("vector_emptied", 2 * KC, True, KC)
        a_emptied = tally("scalar_emptied", 2 * MADE, True)
        ring = Ring(RING, ("A" * MADE + "D" * KC) * 2, {"D": d_emptied, "A": a_emptied})
        filled = tally("filled", 2 * EVENTS, ahead=KC)
        hi_made = tally("hT_hi_made", 2 * KC, ahead=KC)
        hidden_made = tally("hidden_made", 2 * MADE, True)
        split = tally("hidden_hi_made", 2 * MADE)
        part_used = tally("part_used", 2 * PARTS, True)
        out_emptied = tally("out_emptied", 2 * TILES, True)
        loaded = [tally(f"loaded{s}", 16) for s in SLOTS]
        stored = [tally(f"stored{s}", 16, True) for s in SLOTS]
        steps = tally("vector_steps", 2 * LN_STEPS, ahead=LN_STEPS)
        veps_made, rstd_made = tally("veps_made", 2, ahead=1), tally("rstd_made", 2, ahead=1)
        h_made = tally("h_made", 2, ahead=1)
        x_read = tally("x_read", 2, ahead=1)
        b2_added = tally("b2_added", 2, ahead=1)
        params = ctx.enter_context(nc.semaphore("m_params"))
        block = ctx.enter_context(nc.Block())

        def event(s, j):
            return s * EVENTS + j

        def first(it, s):
            return isinstance(it, int) and (it, s) == (0, 0)

        @block.sync
        def _(sp):
            for s in SLOTS:
                sp.sem_inc(stored[s].sem, stored[s].given)
            def load(it, s):
                sp_alone.wait(sp, stored[s].sem, stored[s].at(it, 0))
                sp.dma_start(x[s][:], rows_of(x_d[bass.ds(it * (2 * CHUNK) + s * CHUNK, CHUNK), :])).then_inc(
                    loaded[s].sem, 16)

            def body(it, last):
                for s in SLOTS:
                    if s == 0:
                        load(it, 1)
                        if first(it, s):
                            weights.load(sp, range(BEFORE_X, len(quarters)))
                    elif not last:
                        load(it + 1, 0)
                    sp_alone.wait(sp, out_emptied.sem, out_emptied.at(it, (s + 1) * TILES))
                    sp.dma_start(rows_of(out_d[bass.ds(it * (2 * CHUNK) + s * CHUNK, CHUNK), :]), x[s][:]).then_inc(
                        stored[s].sem, 16)

            load(0, 0)
            for v, d in ((gain, gain_d), (bias, bias_d), (b2, b2_d)):
                load_broadcast(sp, v[:], d, params)
            sp.dma_start(b1[:], b1_d).then_inc(params, 16)
            weights.load(sp, range(BEFORE_X))
            weights.ready(sp, BEFORE_X - 1)
            body(0, False)
            with sp.Fori(1, N - 1) as it:
                body(it, False)
            body(N - 1, True)
            for s in SLOTS:
                sp_alone.wait(sp, stored[s].sem, stored[s].at(N, 0))

        @block.gpsimd
        def _(pool):
            pool.wait_ge(params, 64)

            def norm(it, s, k):
                pool.wait_ge(veps_made.sem, veps_made.at(it, k))
                pool.tensor_tensor(rstd[:], veps[:], minus_half[:], ALU.pow).then_inc(rstd_made.sem, 1)
                pool.wait_ge(x_read.sem, x_read.at(it, k))
                pool.tensor_tensor(x[s][:], x[s][:], b2[:].unsqueeze(1).to_broadcast([P, TILES, D]),
                                   ALU.add).then_inc(b2_added.sem, 1)

            norm(0, 0, 0)
            with pool.Fori(0, N - 1) as it:
                for s in SLOTS:
                    norm(it, 1 - s, s + 1)
            norm(N - 1, 1, 1)

        @block.tensor
        def _(pe):
            def turn(it, s, j0):
                pe.wait_ge(h_made.sem, h_made.at(it, s + 1))
                for c in range(KC):
                    if j0 is not None:
                        pe.wait_ge(*ring.free(it, j0 + c))
                    transposes(pe, psum[:, ring.bank((j0 or 0) + c), :], h, c, ident[:]).then_inc(filled.sem, 1)

            def up(it, s, part):
                if first(it, s) and part % 2 == 0:
                    weights.ready(pe, quarters.index((1, part // 2)))
                for m in range(PART):
                    j = part * PART + m
                    e = event(s, j)
                    pe.wait_ge(*ring.free(it, e))
                    split_product(pe, psum[:, ring.bank(e), :], [
                        ((w1[0][:, k, j * P:(j + 1) * P], w1[1][:, k, j * P:(j + 1) * P]),
                         (hT[0][:, k, :], hT[1][:, k, :])) for k in range(KC)]).then_inc(filled.sem, 1)

            def down(it, s, part):
                hi, lo = hidden[part % 2]
                if first(it, s) and part % 2 == 0:
                    weights.ready(pe, quarters.index((2, part // 2)))
                if part == 0:
                    pe.wait_ge(out_emptied.sem, out_emptied.at(it, s * TILES))
                pe.wait_ge(hidden_made.sem, hidden_made.at(it, s * MADE + (part + 1) * PART))
                for t in range(TILES):
                    out = psum[:, ACC + t, :]
                    for m in range(PART):
                        k = part * PART + m
                        ah, al = hi[:, m, t * P:(t + 1) * P], lo[:, m, t * P:(t + 1) * P]
                        pe.matmul(out, ah, w2[0][:, k, :], start=(k == 0), stop=False)
                        pe.matmul(out, ah, w2[1][:, k, :], start=False, stop=False)
                        last = pe.matmul(out, al, w2[0][:, k, :], start=False, stop=(k == DFF // P - 1))
                last.then_inc(part_used.sem, 1)

            def body(it, last):
                for s in SLOTS:
                    pe.wait_ge(d_emptied.sem, d_emptied.at(it, s * KC))
                    up(it, s, 0)
                    for part in range(1, PARTS):
                        up(it, s, part)
                        down(it, s, part - 1)
                    if s == 0 or not last:
                        turn(it, s, event(s, MADE))
                    down(it, s, PARTS - 1)

            turn(0, -1, None)
            body(0, False)
            with pe.Fori(1, N - 1) as it:
                body(it, False)
            body(N - 1, True)

        @block.scalar
        def _(act):
            act.sem_inc(a_emptied.sem, a_emptied.given)
            act.wait_ge(params, 64)

            def turn(it, s, j0):
                for c in range(KC):
                    act.wait_ge(filled.sem, filled.at(it, j0 + c + 1))
                    act.activation(hT[0][:, c, :], psum[:, ring.bank(j0 + c), :], ACT.Copy).then_inc(hi_made.sem, 1)

            def body(it, last):
                for s in SLOTS:
                    for j in range(MADE):
                        e, n = event(s, j), s * MADE + j
                        if first(it, s) and j in SPLIT_AT:
                            weights.make_hi(act, SPLIT_AT[j])
                        act.wait_ge(filled.sem, filled.at(it, e + 1))
                        act.wait_ge(hidden_made.sem, hidden_made.at(it, n - 1))
                        act.activation(relu[j % 2][:], psum[:, ring.bank(e), :], ACT.Relu,
                                       bias=b1[:, j:j + 1]).then_inc(a_emptied.sem, 1)
                    if s == 0 or not last:
                        turn(it, s, event(s, MADE))

            weights.make_hi(act, 0)
            turn(0, -1, -KC)
            body(0, False)
            with act.Fori(1, N - 1) as it:
                body(it, False)
            body(N - 1, True)

        @block.vector
        def _(dve):
            for t in (d_emptied, hidden_made, part_used, out_emptied):
                dve.sem_inc(t.sem, t.given)
            dve.wait_ge(params, 64)

            def norm(it, s, k, chain):
                x_ = x[s]
                dve.wait_ge(loaded[s].sem, loaded[s].at(it + 1 if k == 2 else it, 16))
                for t in range(TILES):
                    chain.link(dve.bn_stats(stats[:, t, :], x_[:, t, :]))
                chain.settle(dve_alone)
                for t in range(TILES):
                    chain.link(dve.bn_aggr(mv[:, t, :], stats[:, t, :]))
                chain.settle()
                dve.tensor_scalar(veps[:], mv[:, :, 1], EPS, None, ALU.add).then_inc(veps_made.sem, 1)
                for t in range(TILES):
                    last = chain.link(dve.scalar_tensor_tensor(h[:, t, :], x_[:, t, :], mv[:, t, 0:1], gain[:],
                                                               ALU.subtract, ALU.mult))
                chain.settle()
                dve.sem_inc(x_read.sem, 1)
                dve.wait_ge(rstd_made.sem, rstd_made.at(it, k))
                for t in range(TILES):
                    last = dve.scalar_tensor_tensor(h[:, t, :], h[:, t, :], rstd[:, t:t + 1], bias[:],
                                                    ALU.mult, ALU.add)
                last.then_inc(h_made.sem, 1)

            def turn(it, s, j0):
                for c in range(KC):
                    dve.wait_ge(hi_made.sem, hi_made.at(it, s * KC + c + 1))
                    dve.tensor_tensor(hT[1][:, c, :], psum[:, ring.bank(j0 + c), :], hT[0][:, c, :].bitcast(F32),
                                      ALU.subtract).then_inc(d_emptied.sem, 1)

            def body(it, last):
                chain = Chain(dve, steps, it)
                for s in SLOTS:
                    for j in range(MADE):
                        n, (part, m) = s * MADE + j, divmod(j, PART)
                        if first(it, s) and j in SPLIT_AT:
                            weights.make_lo(dve, SPLIT_AT[j])
                        if j == MADE // 2 and (s == 0 or not last):
                            norm(it, 1 - s, s + 1, chain)
                        dve.wait_ge(a_emptied.sem, a_emptied.at(it, n + 1))
                        dve.wait_ge(part_used.sem, part_used.at(it, s * PARTS + part - 1))
                        hi, lo = (a[:, m, :] for a in hidden[part % 2])
                        dve.tensor_copy(hi, relu[j % 2][:]).then_inc(split.sem, 1)
                        dve.wait_ge(split.sem, split.at(it, n + 1))
                        dve.tensor_tensor(lo, relu[j % 2][:], hi.bitcast(F32), ALU.subtract).then_inc(hidden_made.sem, 1)
                    if s == 0 or not last:
                        turn(it, s, event(s, MADE))
                    dve.wait_ge(part_used.sem, part_used.at(it, (s + 1) * PARTS))
                    dve.wait_ge(b2_added.sem, b2_added.at(it, s))
                    for t in range(TILES):
                        dve.tensor_tensor(x[s][:, t, :], psum[:, ACC + t, :], x[s][:, t, :], ALU.add).then_inc(
                            out_emptied.sem, 1)

            norm(0, 0, 0, Chain(dve, Tally(steps.sem, 0), 0))
            weights.make_lo(dve, 0)
            turn(0, -1, -KC)
            body(0, False)
            with dve.Fori(1, N - 1) as it:
                body(it, False)
            body(N - 1, True)


def two_layers(nc, t, out):
    x, context = t["x"], t["ctx_1024"]
    with ExitStack() as ctx:
        def dram(name, shape):
            return nc.dram_tensor(name, shape, F32, kind="Internal").ap()

        tokens = BATCH * SEQ
        xn, v = dram("xn_scratch", [tokens, D]), dram("v_scratch", [tokens, D])
        q_hi, q_lo, k_hi, k_lo, oT = (dram(n + "_scratch", [D, tokens]) for n in ("q_hi", "q_lo", "k_hi", "k_lo", "oT"))
        after_cross, after_mlp = dram("cross_scratch", [tokens, D]), dram("mlp_scratch", [tokens, D])
        const = make_constants(nc, ctx)
        scratch = (xn, q_hi, q_lo, k_hi, k_lo, v)
        project_qkv(nc, const, x, t["sa_wqT"], t["sa_wkT"], t["sa_wvT"], t["g_sa"], t["b_sa"], scratch)
        self_attention(nc, const, scratch, oT)
        with ExitStack() as held:
            kblk = held.enter_context(nc.sbuf_tensor("kblk0", [P, BATCH, KC, GROUP * CTX], F32))
            values = held.enter_context(nc.sbuf_tensor("values0", [CTX, BATCH, D], F32))
            w, jobs = cross_weights(nc, held, "d", {"wo0": t["sa_woT"], "wq": t["ca_wqT"], "wo": t["ca_woT"]})
            context_keys(nc, const, "c", context, t["ca_wkT"], t["ca_wvT"],
                         ((t["g_kca"], t["b_kca"]), (t["g_vca"], t["b_vca"])), None, kblk, values, jobs)
            cross_attention(nc, const, "d", True, xn, after_cross, oT, w, (t["g_qca"], t["b_qca"]), None, kblk, values)
        mlp(nc, const, after_cross, after_mlp, t["w1T"], t["w2T"], t["b1"], t["b2"], t["g_out"], t["b_out"])
        with ExitStack() as held:
            kblk = held.enter_context(nc.sbuf_tensor("kblk1", [P, BATCH, KC, GROUP * CTX], F32))
            values = held.enter_context(nc.sbuf_tensor("values1", [CTX, BATCH, D], F32))
            w, jobs = cross_weights(nc, held, "g", {"wq": t["l1_wqT"], "wo": t["l1_woT"]})
            context_keys(nc, const, "f", context, t["l1_wkT"], t["l1_wvT"], None, (t["l1_bk"], t["l1_bv"]),
                         kblk, values, jobs)
            cross_attention(nc, const, "g", False, after_mlp, out, None, w,
                            (t["l1_gain"], t["l1_bias"], t["l1_bo"]), t["l1_bq"], kblk, values)


def kernel(**inputs):
    import numpy as np
    import concourse.bacc as bacc
    from concourse.bass_utils import run_bass_kernel_spmd

    def turned(a):
        return np.ascontiguousarray(np.asarray(a).T)

    def by_partition(a):
        return np.ascontiguousarray(np.asarray(a).reshape(-1, P).T)

    a0 = {k[len("L0_xattn_"):]: np.asarray(v) for k, v in inputs.items() if k.startswith("L0_xattn_")}
    a1 = {k[len("L1_xattn_"):]: np.asarray(v) for k, v in inputs.items() if k.startswith("L1_xattn_")}
    arrays = {
        "x": np.ascontiguousarray(np.asarray(inputs["x"]).reshape(BATCH * SEQ, D)),
        "ctx_1024": np.ascontiguousarray(np.asarray(inputs["ctx_1024"]).reshape(BATCH * CTX, D)),
    }
    for n in ("sa_wq", "sa_wk", "sa_wv", "sa_wo", "ca_wq", "ca_wk", "ca_wv", "ca_wo"):
        arrays[n + "T"] = turned(a0[n])
    for n in ("g_sa", "b_sa", "g_qca", "b_qca", "g_kca", "b_kca", "g_vca", "b_vca", "g_out", "b_out"):
        arrays[n] = np.ascontiguousarray(a0[n])
    arrays["w1T"], arrays["w2T"] = turned(a0["ffn_w1"]), turned(a0["ffn_w2"])
    arrays["b1"], arrays["b2"] = by_partition(a0["ffn_b1"]), np.ascontiguousarray(a0["ffn_b2"])
    for i, n in enumerate(("wq", "wk", "wv")):
        arrays[f"l1_{n}T"] = turned(a1["W_qkv"][i * D:(i + 1) * D])
    arrays["l1_woT"] = turned(a1["W_o"])
    arrays["l1_bq"] = by_partition(a1["b_qkv"][0:D])
    arrays["l1_bk"] = by_partition(a1["b_qkv"][D:2 * D])
    arrays["l1_bv"] = np.ascontiguousarray(a1["b_qkv"][2 * D:3 * D])
    arrays["l1_bo"] = np.ascontiguousarray(a1["b_o"])
    arrays["l1_gain"], arrays["l1_bias"] = np.ascontiguousarray(a1["ln_gamma"]), np.ascontiguousarray(a1["ln_beta"])

    nc = bacc.Bacc("TRN2", target_bir_lowering=False, num_devices=1)
    handles = {n: nc.dram_tensor(n, a.shape, mybir.dt.from_np(a.dtype), kind="ExternalInput").ap()
               for n, a in arrays.items()}
    out = nc.dram_tensor("out", [BATCH * SEQ, D], F32, kind="ExternalOutput").ap()
    two_layers(nc, handles, out)
    result = run_bass_kernel_spmd(nc, [arrays], core_ids=[0]).results[0]["out"]
    return np.asarray(result).reshape(BATCH, SEQ, D)
```
